# Optimizing a Trainium2 kernel written in Bass

```python
import numpy as np
import jax
import jax.numpy as jnp

def _softmax(x, axis=-1):
    return jax.nn.softmax(x, axis=axis)

def _gelu(x):
    return jax.nn.gelu(x, approximate=True)

def _silu(x):
    return jax.nn.silu(x)

def _sigmoid(x):
    return jax.nn.sigmoid(x)

def _layernorm(x, axis=-1, eps=1e-05):
    m = jnp.mean(x, axis=axis, keepdims=True)
    v = jnp.var(x, axis=axis, keepdims=True)
    return (x - m) / jnp.sqrt(v + eps)

def _scatter_add(tgt, idx, src, axis=0):
    return tgt.at[idx].add(src)

def _segment_sum(src, seg, n):
    return jax.ops.segment_sum(src, seg, n)
kernel_name = 'mk_adaln_attn_ffn_d1_seqx_r4_13d50c'

def setup_inputs(seed: int=0):
    np.random.seed(seed)
    _w = jnp.asarray

    def _rec_inputs():
        import jax
        import jax.numpy as jnp
        _rk = jax.random.key(seed)
        x = -0.000125 + 0.9999 * jax.random.normal(jax.random.fold_in(_rk, 1), (2, 1024, 256), jnp.float32)
        _lenS = 1024 - jax.random.randint(jax.random.fold_in(_rk, 7), (2,), 0, max(1, 1024 // 4) + 1, jnp.int32)
        _lenS2 = 1024 - jax.random.randint(jax.random.fold_in(_rk, 8), (2,), 0, max(1, 1024 // 4) + 1, jnp.int32)
        cond_1024 = 0.00782532 + 1.00527 * jax.random.normal(jax.random.fold_in(_rk, 11), (2, 256), jnp.float32)
        _validS = jnp.arange(1024)[None, :] < _lenS[:, None]
        _validS2 = jnp.arange(1024)[None, :] < _lenS2[:, None]
        _causal = jnp.tril(jnp.ones((1024, 1024), dtype=bool))
        mask_SxS_bk0 = jnp.logical_not(jnp.broadcast_to(_validS[0:1, :], (1024, 1024)))
        return (x, cond_1024, mask_SxS_bk0)
    x, cond_1024, mask_SxS_bk0 = _rec_inputs()

    def _L0_cond_setup():
        import jax, jax.numpy as jnp
        import numpy as np
        key = jax.random.key(seed)
        k1, k2, k3 = jax.random.split(key, 3)
        B, R, C = (8, 1024, 256)
        input_dim = 256
        weight_params = jax.random.normal(k1, (B, R, C), dtype=jnp.float32)
        logits = jax.random.normal(k2, (B, input_dim), dtype=jnp.float32)
        score_w = jax.random.normal(k3, (input_dim, 1), dtype=jnp.float32) * (1.0 / np.sqrt(input_dim))
        score_b = jnp.zeros((1,), dtype=jnp.float32)
        return {'weight_params': weight_params, 'logits': logits, 'score_w': score_w, 'score_b': score_b}
    _L0_cond_all = _L0_cond_setup()
    _L0_cond_in = {k: v for k, v in _L0_cond_all.items() if k in ('score_w', 'score_b')}
    del _L0_cond_all

    def _L0_attn_setup():
        import jax, jax.numpy as jnp
        import numpy as np
        EPS = 1e-05

        def rmsnorm(x, w):
            var = jnp.mean(x * x, axis=-1, keepdims=True)
            return x * jax.lax.rsqrt(var + EPS) * w

        def _mamba_block(x, rms_w, in_proj, conv_w, conv_b, x_proj, dt_w, dt_b, A_log, D, out_proj):
            B, L, dim = x.shape
            d_inner, K = conv_w.shape
            d_state = A_log.shape[1]
            dt_rank = dt_w.shape[0]
            xn = rmsnorm(x, rms_w)
            xz = xn @ in_proj
            xi, z = jnp.split(xz, 2, axis=-1)
            xc = jax.lax.conv_general_dilated(xi.transpose(0, 2, 1), conv_w[:, None, :], window_strides=(1,), padding=[(K - 1, 0)], feature_group_count=d_inner).transpose(0, 2, 1) + conv_b
            xi = jax.nn.silu(xc)
            dbc = xi @ x_proj
            dt, Bm, Cm = jnp.split(dbc, [dt_rank, dt_rank + d_state], axis=-1)
            delta = jax.nn.softplus(dt @ dt_w + dt_b)
            A = -jnp.exp(A_log)

            def step(h, inputs):
                d_t, x_t, B_t, C_t = inputs
                dA = jnp.exp(d_t[..., None] * A)
                h = dA * h + (d_t * x_t)[..., None] * B_t[:, None, :]
                y = jnp.einsum('bds,bs->bd', h, C_t)
                return (h, y)
            h0 = jnp.zeros((B, d_inner, d_state), x.dtype)
            xs = (delta.transpose(1, 0, 2), xi.transpose(1, 0, 2), Bm.transpose(1, 0, 2), Cm.transpose(1, 0, 2))
            _, ys = jax.lax.scan(step, h0, xs)
            y = ys.transpose(1, 0, 2) + xi * D
            y = y * jax.nn.silu(z)
            return x + y @ out_proj
        key = jax.random.key(seed)
        B, L, dim = (4, 512, 256)
        d_inner, d_state, d_conv, dt_rank = (2 * dim, 16, 4, dim // 16)
        ks = jax.random.split(key, 8)
        g = lambda k, shape, scale: jax.random.normal(k, shape, jnp.float32) * scale
        return {'x': g(ks[0], (B, L, dim), 1.0), 'rms_w': jnp.ones((dim,), jnp.float32), 'in_proj': g(ks[1], (dim, 2 * d_inner), dim ** (-0.5)), 'conv_w': g(ks[2], (d_inner, d_conv), 0.25), 'conv_b': jnp.zeros((d_inner,), jnp.float32), 'x_proj': g(ks[3], (d_inner, dt_rank + 2 * d_state), d_inner ** (-0.5)), 'dt_w': g(ks[4], (dt_rank, d_inner), dt_rank ** (-0.5)), 'dt_b': jnp.full((d_inner,), float(np.log(np.expm1(0.01))), jnp.float32), 'A_log': jnp.log(jnp.broadcast_to(jnp.arange(1, d_state + 1, dtype=jnp.float32), (d_inner, d_state))).copy(), 'D': jnp.ones((d_inner,), jnp.float32), 'out_proj': g(ks[5], (d_inner, dim), d_inner ** (-0.5))}
    _L0_attn_all = _L0_attn_setup()
    _L0_attn_in = {k: v for k, v in _L0_attn_all.items() if k in ('rms_w', 'in_proj', 'conv_w', 'conv_b', 'x_proj', 'dt_w', 'dt_b', 'A_log', 'D', 'out_proj')}
    del _L0_attn_all

    def _L0_cond2_setup():
        import jax, jax.numpy as jnp
        import numpy as np
        B, T, D, H = (2, 512, 256, 16)
        E = D // H
        key = jax.random.key(seed)
        ks = jax.random.split(key, 7)
        s = 1.0 / np.sqrt(D)
        return {'x': jax.random.normal(ks[0], (B, T, D), dtype=jnp.float32), 't': jax.random.normal(ks[1], (B, D), dtype=jnp.float32), 'mask': jnp.tril(jnp.ones((T, T), dtype=bool)), 'Wq': jax.random.normal(ks[2], (D, D), dtype=jnp.float32) * s, 'Wk': jax.random.normal(ks[3], (D, D), dtype=jnp.float32) * s, 'Wv': jax.random.normal(ks[4], (D, D), dtype=jnp.float32) * s, 'Wt': jax.random.normal(ks[5], (D, D), dtype=jnp.float32) * s, 'Wo': jax.random.normal(ks[6], (D, D), dtype=jnp.float32) * s}
    _L0_cond2_all = _L0_cond2_setup()
    _L0_cond2_in = {k: v for k, v in _L0_cond2_all.items() if k in ('Wq', 'Wk', 'Wv', 'Wt', 'Wo')}
    del _L0_cond2_all

    def _L0_ffn_setup():
        import jax, jax.numpy as jnp
        import numpy as np
        D_IN, D_HID = (256, 1024)

        def _ternary(key, shape):
            return jax.random.randint(key, shape, -1, 2).astype(jnp.float32)

        def _tlin(x, w, s):
            return jnp.einsum('bsi,oi->bso', x, w) * s
        key = jax.random.key(seed)
        ks = jax.random.split(key, 12)
        inv = lambda fan: 1.0 / np.sqrt(fan).astype(np.float32)
        return {'x': jax.random.normal(ks[0], (4, 512, D_IN), dtype=jnp.float32), 'w1_w': _ternary(ks[1], (D_HID, D_IN)), 'w1_s': jax.random.uniform(ks[2], (D_HID,), dtype=jnp.float32) * inv(D_IN), 'w2_w': _ternary(ks[3], (D_HID, D_IN)), 'w2_s': jax.random.uniform(ks[4], (D_HID,), dtype=jnp.float32) * inv(D_IN), 'h1_w': _ternary(ks[5], (D_HID, D_HID)), 'h1_s': jax.random.uniform(ks[6], (D_HID,), dtype=jnp.float32) * inv(D_HID), 'h2_w': _ternary(ks[7], (D_HID, D_HID)), 'h2_s': jax.random.uniform(ks[8], (D_HID,), dtype=jnp.float32) * inv(D_HID), 'w3_w': _ternary(ks[9], (D_IN, D_HID)), 'w3_s': jax.random.uniform(ks[10], (D_IN,), dtype=jnp.float32) * inv(D_HID)}
    _L0_ffn_all = _L0_ffn_setup()
    _L0_ffn_in = {k: v for k, v in _L0_ffn_all.items() if k in ('w1_w', 'w1_s', 'w2_w', 'w2_s', 'h1_w', 'h1_s', 'h2_w', 'h2_s', 'w3_w', 'w3_s')}
    del _L0_ffn_all
    return {'x': x, 'cond_1024': cond_1024, 'mask_SxS_bk0': mask_SxS_bk0, 'L0_cond_score_w': _L0_cond_in['score_w'], 'L0_cond_score_b': _L0_cond_in['score_b'], 'L0_attn_rms_w': _L0_attn_in['rms_w'], 'L0_attn_in_proj': _L0_attn_in['in_proj'], 'L0_attn_conv_w': _L0_attn_in['conv_w'], 'L0_attn_conv_b': _L0_attn_in['conv_b'], 'L0_attn_x_proj': _L0_attn_in['x_proj'], 'L0_attn_dt_w': _L0_attn_in['dt_w'], 'L0_attn_dt_b': _L0_attn_in['dt_b'], 'L0_attn_A_log': _L0_attn_in['A_log'], 'L0_attn_D': _L0_attn_in['D'], 'L0_attn_out_proj': _L0_attn_in['out_proj'], 'L0_cond2_Wq': _L0_cond2_in['Wq'], 'L0_cond2_Wk': _L0_cond2_in['Wk'], 'L0_cond2_Wv': _L0_cond2_in['Wv'], 'L0_cond2_Wt': _L0_cond2_in['Wt'], 'L0_cond2_Wo': _L0_cond2_in['Wo'], 'L0_ffn_w1_w': _L0_ffn_in['w1_w'], 'L0_ffn_w1_s': _L0_ffn_in['w1_s'], 'L0_ffn_w2_w': _L0_ffn_in['w2_w'], 'L0_ffn_w2_s': _L0_ffn_in['w2_s'], 'L0_ffn_h1_w': _L0_ffn_in['h1_w'], 'L0_ffn_h1_s': _L0_ffn_in['h1_s'], 'L0_ffn_h2_w': _L0_ffn_in['h2_w'], 'L0_ffn_h2_s': _L0_ffn_in['h2_s'], 'L0_ffn_w3_w': _L0_ffn_in['w3_w'], 'L0_ffn_w3_s': _L0_ffn_in['w3_s']}

def reference(x, cond_1024, mask_SxS_bk0, L0_cond_score_w, L0_cond_score_b, L0_attn_rms_w, L0_attn_in_proj, L0_attn_conv_w, L0_attn_conv_b, L0_attn_x_proj, L0_attn_dt_w, L0_attn_dt_b, L0_attn_A_log, L0_attn_D, L0_attn_out_proj, L0_cond2_Wq, L0_cond2_Wk, L0_cond2_Wv, L0_cond2_Wt, L0_cond2_Wo, L0_ffn_w1_w, L0_ffn_w1_s, L0_ffn_w2_w, L0_ffn_w2_s, L0_ffn_h1_w, L0_ffn_h1_s, L0_ffn_h2_w, L0_ffn_h2_s, L0_ffn_w3_w, L0_ffn_w3_s):
    import jax
    import jax.numpy as jnp

    def _L0_cond_ref(weight_params, logits, score_w, score_b):
        import jax, jax.numpy as jnp
        import numpy as np
        keep_fraction = jax.nn.sigmoid(logits @ score_w + score_b)
        total_row_count = weight_params.shape[-2]
        rows_to_keep = jnp.clip((keep_fraction * total_row_count).astype(jnp.int32), 1, None).squeeze(-1)
        row_magnitudes = jnp.linalg.norm(weight_params, axis=-1)
        sorted_magnitudes = jnp.sort(row_magnitudes, axis=-1)[..., ::-1]
        thresholds = jnp.take_along_axis(sorted_magnitudes, (rows_to_keep - 1)[:, None], axis=-1)
        top_k_row_mask = (row_magnitudes >= thresholds).astype(weight_params.dtype)
        return weight_params * top_k_row_mask[..., None]

    def _L0_attn_ref(x, rms_w, in_proj, conv_w, conv_b, x_proj, dt_w, dt_b, A_log, D, out_proj):
        import jax, jax.numpy as jnp
        import numpy as np
        EPS = 1e-05

        def rmsnorm(x, w):
            var = jnp.mean(x * x, axis=-1, keepdims=True)
            return x * jax.lax.rsqrt(var + EPS) * w

        def _mamba_block(x, rms_w, in_proj, conv_w, conv_b, x_proj, dt_w, dt_b, A_log, D, out_proj):
            B, L, dim = x.shape
            d_inner, K = conv_w.shape
            d_state = A_log.shape[1]
            dt_rank = dt_w.shape[0]
            xn = rmsnorm(x, rms_w)
            xz = xn @ in_proj
            xi, z = jnp.split(xz, 2, axis=-1)
            xc = jax.lax.conv_general_dilated(xi.transpose(0, 2, 1), conv_w[:, None, :], window_strides=(1,), padding=[(K - 1, 0)], feature_group_count=d_inner).transpose(0, 2, 1) + conv_b
            xi = jax.nn.silu(xc)
            dbc = xi @ x_proj
            dt, Bm, Cm = jnp.split(dbc, [dt_rank, dt_rank + d_state], axis=-1)
            delta = jax.nn.softplus(dt @ dt_w + dt_b)
            A = -jnp.exp(A_log)

            def step(h, inputs):
                d_t, x_t, B_t, C_t = inputs
                dA = jnp.exp(d_t[..., None] * A)
                h = dA * h + (d_t * x_t)[..., None] * B_t[:, None, :]
                y = jnp.einsum('bds,bs->bd', h, C_t)
                return (h, y)
            h0 = jnp.zeros((B, d_inner, d_state), x.dtype)
            xs = (delta.transpose(1, 0, 2), xi.transpose(1, 0, 2), Bm.transpose(1, 0, 2), Cm.transpose(1, 0, 2))
            _, ys = jax.lax.scan(step, h0, xs)
            y = ys.transpose(1, 0, 2) + xi * D
            y = y * jax.nn.silu(z)
            return x + y @ out_proj
        return _mamba_block(x, rms_w, in_proj, conv_w, conv_b, x_proj, dt_w, dt_b, A_log, D, out_proj)

    def _L0_cond2_ref(x, t, mask, Wq, Wk, Wv, Wt, Wo):
        import jax, jax.numpy as jnp
        import numpy as np
        B, T, D, H = (2, 512, 256, 16)
        E = D // H
        b, seq, d = x.shape
        h, e = (H, d // H)
        q = (x @ Wq.T).reshape(b, seq, h, e).transpose(0, 2, 1, 3)
        k = (x @ Wk.T).reshape(b, seq, h, e).transpose(0, 2, 1, 3)
        v = (x @ Wv.T).reshape(b, seq, h, e).transpose(0, 2, 1, 3)
        tp = (t @ Wt.T).reshape(b, h, e)
        a = jnp.einsum('bhe,bhse->bhs', tp, q)
        qmod = jnp.einsum('bhs,bhse->bhe', a, q)
        qmod = jnp.broadcast_to(qmod[:, :, None, :], (b, h, seq, e))
        scores = jnp.einsum('bhte,bhse->bhts', qmod, k) / jnp.sqrt(jnp.asarray(e, x.dtype))
        neg = jnp.asarray(jnp.finfo(scores.dtype).min, scores.dtype)
        scores = jnp.where(mask, scores, neg)
        attn = jax.nn.softmax(scores, axis=-1)
        o = jnp.einsum('bhts,bhse->bhte', attn, v)
        o = o.transpose(0, 2, 1, 3).reshape(b, seq, d)
        return o @ Wo.T

    def _L0_ffn_ref(x, w1_w, w1_s, w2_w, w2_s, h1_w, h1_s, h2_w, h2_s, w3_w, w3_s):
        import jax, jax.numpy as jnp
        import numpy as np
        D_IN, D_HID = (256, 1024)

        def _ternary(key, shape):
            return jax.random.randint(key, shape, -1, 2).astype(jnp.float32)

        def _tlin(x, w, s):
            return jnp.einsum('bsi,oi->bso', x, w) * s
        h = jax.nn.silu(_tlin(x, w1_w, w1_s)) * _tlin(x, w2_w, w2_s)
        h = jax.nn.gelu(_tlin(h, h1_w, h1_s), approximate=False)
        h = jax.nn.gelu(_tlin(h, h2_w, h2_s), approximate=False)
        return _tlin(h, w3_w, w3_s)
    x = x + _L0_attn_ref(_L0_cond_ref(x, cond_1024, L0_cond_score_w, L0_cond_score_b), L0_attn_rms_w, L0_attn_in_proj, L0_attn_conv_w, L0_attn_conv_b, L0_attn_x_proj, L0_attn_dt_w, L0_attn_dt_b, L0_attn_A_log, L0_attn_D, L0_attn_out_proj)
    x = x + _L0_ffn_ref(_L0_cond2_ref(x, cond_1024, mask_SxS_bk0, L0_cond2_Wq, L0_cond2_Wk, L0_cond2_Wv, L0_cond2_Wt, L0_cond2_Wo), L0_ffn_w1_w, L0_ffn_w1_s, L0_ffn_w2_w, L0_ffn_w2_s, L0_ffn_h1_w, L0_ffn_h1_s, L0_ffn_h2_w, L0_ffn_h2_s, L0_ffn_w3_w, L0_ffn_w3_s)
    return x

_drawn_inputs = setup_inputs


def setup_inputs(seed=0):
    import zlib

    import numpy as np

    out = dict(_drawn_inputs(seed))
    spreads = {'L0_attn_rms_w': (1.0, 0.2),
     'L0_attn_conv_b': (0.0, 0.1),
     'L0_attn_dt_b': (-4.600165843963623, 0.2),
     'L0_attn_D': (1.0, 0.2)}
    factors = {}
    for name, (base, spread) in spreads.items():
        noise = np.random.default_rng([zlib.crc32(name.encode()), seed]).standard_normal(out[name].shape)
        drawn = base * np.exp(spread * noise) if base else spread * noise
        out[name] = jnp.asarray(drawn.astype(out[name].dtype))
    for name, factor in factors.items():
        out[name] = (out[name] * factor).astype(out[name].dtype)
    return out
```

```python
import numpy as np
import concourse.bass as bass
from concourse import mybir
from concourse.alu_op_type import AluOpType as ALU
from contextlib import ExitStack

F32 = mybir.dt.float32
BF16 = mybir.dt.bfloat16
U8 = mybir.dt.uint8
I32 = mybir.dt.int32
ACT = mybir.ActivationFunctionType
AX = mybir.AxisListType

P = 128
B, S, DM = 2, 1024, 256
DI, NS, DR, KC = 512, 16, 16, 4
NH, HE = 16, 16
HID = 1024
KD = DM // P
CT = DI // P
T = 512
NT = T // P
HALVES = S // T
NCH = B * HALVES
NG = B * S // P
GB = S // P
KH = HID // P
FLT_MAX = float(np.finfo(np.float32).max)
EPS = 1e-5

VEC = {}
_at = 0
for _name, _n in (("rms_w", KD), ("conv_w", CT * KC), ("conv_b", CT), ("dt_b", CT), ("A_log", CT * NS), ("D", CT),
                  ("score_w", KD), ("cond", KD * B), ("score_b", 1), ("w1_s", KH), ("w2_s", KH), ("h1_s", KH),
                  ("h2_s", KH), ("w3_s", KD)):
    VEC[_name] = (_at, _at + _n)
    _at += _n
NVEC = _at

BROWS = 2
BSLOTS = 5
PIECES = NS // BROWS


def prologue_slots(n):
    return {1: [("T", n, 0), ("T", n, 1)], 2: [("I", n, 0), ("I", n, 1)], 3: [("I", n, 2), ("I", n, 3)],
            4: [("V", n, 0), ("V", n, 1)], 5: [("V", n, 2), ("V", n, 3)], 7: [("X", n, 0), ("Z", n, 0)],
            8: [("XT", n, 0), ("Z", n, 1)], 9: [("Z", n, 2), ("Z", n, 3)], 10: [("D", n, 0), ("D", n, 1)],
            11: [("D", n, 2), ("D", n, 3)]}


def epilogue_slots(e):
    last = 14 if e == 2 else 12
    return {0: [("Y", e, 1), ("Y", e, 3)], 6: [("O", e, 0), ("O", e, 1)],
            last: [("R", e, 0), ("R", e, 1)]}


def attention_jobs(b):
    return [(name, b, 0) for name in ("A", "G", "M", "RR", "S0", "S1", "PT", "YV", "VV", "WO")]


def all_slots():
    head = [("F", 0, 0), ("TP", 0, 0), ("U", 0, 0)]
    head += [("T", 0, k) for k in range(KD)] + [("I", 0, m) for m in range(CT)] + [("V", 0, m) for m in range(CT)]
    head += [("X", 0, 0), ("XT", 0, 0)] + [("D", 0, m) for m in range(CT)]
    beside = {(c, s): [] for c in range(NCH) for s in range(NS)}
    for c in range(NCH):
        if c == 0:
            beside[0, 0] += [("Z", 0, 0), ("Z", 0, 1)]
            beside[0, 1] += [("Z", 0, 2), ("Z", 0, 3)]
        else:
            for s, jobs in epilogue_slots(c - 1).items():
                beside[c, s] += jobs
        if c + 1 < NCH:
            for s, jobs in prologue_slots(c + 1).items():
                beside[c, s] += jobs
    for i, job in enumerate(attention_jobs(0)):
        beside[NCH - 1, 4 + i] += [job]
    tail = []
    for s, jobs in sorted(epilogue_slots(NCH - 1).items()):
        tail += jobs
    tail += attention_jobs(1)
    tail += [("W12", 0, 0), ("FL", 0, 0), ("H1", 0, 0), ("H2", 0, 0), ("W3", 0, 0), ("FB", 0, 0), ("FB", 1, 0)]
    return head, beside, tail


BATCH_STEPS = [f"{x}{i}" for i in range(GB // 2) for x in ("turn_x", "turn_x_out")]
BATCH_STEPS += ["a", "a_out", "g", "g_out", "m", "m_out", "r", "r_out", "s0", "s0_out", "s1", "s1_out"]
BATCH_STEPS += [f"{x}{i}" for i in range(GB // 2) for x in ("v", "v_out")]
TILE_STEPS = ["mask"] + [f"{x}{h}" for h in range(NH) for x in ("row", "add", "max", "neg", "exp", "recip", "norm", "turn", "turn_out", "pv")]
TILE_STEPS += ["o_out", "turn_o", "turn_o_out", "wo", "wo_out", "w12", "w1_out", "w2_out", "silu", "gated", "h1", "h1_out", "gelu1",
               "h2", "h2_out", "gelu2", "w3", "w3_out", "turn_f", "sum"]

HEAD, BESIDE, TAIL = all_slots()
ORDER = HEAD + [job for c in range(NCH) for s in range(NS) for job in BESIDE[c, s]] + TAIL
INDEX = {job: q for q, job in enumerate(ORDER)}


def build(nc, x, w_in, w_out, w_x, w_dt, wq, wqT, wk, wvT, wtT, woT, f1, f2, fh1, fh2, f3, mask, vecs, consts, out):
    ctx = ExitStack()
    with ctx:
        def sb(name, shape, dt=F32):
            return ctx.enter_context(nc.sbuf_tensor(name, shape, dt))

        def sem(name):
            return ctx.enter_context(nc.semaphore(name))

        xt = sb("xt", [P, NG, DM])
        x1T = sb("x1T", [P, KD, S])
        wi = sb("wi", [P, KD * 2 * DI])
        wo = sb("wo", [P, CT, DM])
        wx = sb("wx", [P, CT, DR + 2 * NS])
        wdt = sb("wdt", [DR, DI])
        aw = sb("aw", [P, 5, KD, DM])
        vec = sb("vec", [P, NVEC])
        con = sb("con", [P, P + 2 * NH])
        diag = sb("diag", [P, CT * KC * P])
        diagD = sb("diagD", [P, CT, P])
        xr = sb("xr", [P, CT * (T + KC - 1)])
        par = [sb(f"par{i}", [P, 4, CT * T]) for i in range(2)]
        scanmem = sb("scanmem", [P, BSLOTS * BROWS * T + 3 * CT * T])
        hc = sb("hc", [P, 2, T])
        small = sb("small", [P, 2, DI])
        yTd = sb("yTd", [P, 2, 2, DI])
        dbc = sb("dbc", [DR + 2 * NS, T])
        CTs = sb("CTs", [P, 2, NT, NS])
        carry = sb("carry", [P, NS, CT])
        Aneg = sb("Aneg", [P, CT * NS])
        ss = sb("ss", [P, NG])
        cnt = sb("cnt", [P, NG])
        keep = sb("keep", [P, NG])
        keep1 = sb("keep1", [P, NG])
        scl = sb("scl", [P, NG])
        lnv = sb("lnv", [P, NG])
        fr = sb("fr", [P, 4, B])
        eps = sb("eps", [P, 1])
        zero = sb("zero", [P, CT, KC - 1])
        tpD = sb("tpD", [P, KD, B, NH])
        u = sb("u", [P, KD, B * NH])
        a_sb = sb("a_sb", [P, GB, NH])
        g_sb = sb("g_sb", [P, KD, NH])
        qD = sb("qD", [P, KD, NH])
        r_sb = sb("r_sb", [P, KD, NH])
        pT = sb("pT", [P, GB, NH])
        yv = sb("yv", [P, KD, NH])
        ov = sb("ov", [P, KD])
        ovj = sb("ovj", [P, KD, NH])
        z_sb = sb("z_sb", [P, KD, B])
        sm = sb("sm", [NH, S])
        st = sb("st", [NH, 4])
        negm = sb("negm", [NH, S])
        ff = sb("ff", [P, 4, KH, B])
        fo = sb("fo", [P, KD, B])
        flag = sb("flag", [P, 2])
        flag_i = sb("flag_i", [1, 1], I32)
        gst = sb("gst", [P, 4])

        ident = con[:, 0:P]
        bm = con[:, P:P + 2 * NH].rearrange("p (k h) -> p k h", k=KD)

        def v(name):
            lo, hi = VEC[name]
            return vec[:, lo:hi]

        def xi(n):
            return par[n % 2][:, 0, :].rearrange("p (m t) -> p m t", m=CT)

        def delta(n):
            return par[n % 2][:, 1, :].rearrange("p (m t) -> p m t", m=CT)

        def dx(n):
            return par[n % 2][:, 2, :].rearrange("p (m t) -> p m t", m=CT)

        def gate(n):
            return par[n % 2][:, 3, :].rearrange("p (m t) -> p m t", m=CT)

        def xs(n):
            return par[n % 2][:, 1, 0:NT * DM].rearrange("p (i d) -> p i d", i=NT)

        def xnT(n):
            return par[n % 2 if n else 1][:, 1, NT * DM:NT * DM + KD * T].rearrange("p (k t) -> p k t", k=KD)

        win = wi[:, :].rearrange("p (k o) -> p k o", k=KD)
        Bb = scanmem[:, 0:BSLOTS * BROWS * T].rearrange("p (r t) -> p r t", t=T)
        hb = scanmem[:, BSLOTS * BROWS * T:].rearrange("p (r m t) -> p r m t", r=3, m=CT)
        xr3 = xr[:, :].rearrange("p (m t) -> p m t", m=CT)
        dg = diag[:, :].rearrange("p (m k q) -> p m k q", m=CT, k=KC)
        magrow = x1T[:, 0, :]
        junk = par[1][:, 0, :]
        mrow = x1T[0:NH, 1, 0:S // 4].bitcast(U8)
        wt = hc[:, 0, :].rearrange("p (k o) -> p k o", k=KD)
        mask_w = par[1][:, 1, :].bitcast(I32)
        mask_0 = hc[:, 0, 0:S // 4].bitcast(I32)
        outs = par[1][:, 0:3:2, :].rearrange("p a (g d) -> p a g d", d=DM)
        gv = par[1][:, 0, :].rearrange("p (i o) -> p i o", i=GB)
        gadd, gsc = par[1][:, 1, 0:S], par[1][:, 1, S:2 * S]
        gpT = par[1][:, 2, 0:S].rearrange("p (i t) -> p i t", i=GB)
        gmask = par[1][:, 2, S:S + S // 4].bitcast(U8)
        gout = par[1][:, 2, S + S // 2:S + S // 2 + DM]
        gf1 = par[1][:, 3, 0:HID].rearrange("p (m t) -> p m t", m=KH)
        gf2 = par[1][:, 3, HID:2 * HID].rearrange("p (m t) -> p m t", m=KH)
        go = small[:, 0, 0:DM]
        goT = small[:, 0, DM:2 * DM].rearrange("p (k t) -> p k t", k=KD)
        gz = small[:, 1, 0:DM].rearrange("p (k t) -> p k t", k=KD)
        gf3 = small[:, 1, DM:2 * DM].rearrange("p (k t) -> p k t", k=KD)
        W1 = wi[:, :].rearrange("p (k o) -> p k o", k=KD)
        W2 = xr[:, 0:KD * HID].rearrange("p (k o) -> p k o", k=KD)
        W3 = diag[:, :].rearrange("p (k o) -> p k o", k=KH)
        H1 = par[0][:, :, :].rearrange("p a (b o) -> p (a b) o", b=2)
        H2 = scanmem[:, 0:KH * HID].rearrange("p (k o) -> p k o", k=KH)

        dA = ctx.enter_context(nc.psum_tensor("dA", [P, 2, T], F32))
        hT = ctx.enter_context(nc.psum_tensor("hT", [P, 2, DI], F32))
        yacc = ctx.enter_context(nc.psum_tensor("yacc", [P, 2, DI], F32))
        pp = ctx.enter_context(nc.psum_tensor("pp", [P, 2, 512], F32))
        brow = nc.dram_tensor("brow", [NCH, NS, T], F32, kind="Internal").ap()

        s_vec, s_x, s_w, s_aw, s_mrow = sem("vec_in"), [sem(f"x_in{i}") for i in range(NCH)], sem("w_in"), sem("aw_in"), sem("mrow_in")
        s_ff1, s_ff2, s_ff3, s_ffh1, s_ffh2 = (sem(f"ff_in{i}") for i in range(5))
        bb_in = [sem(f"bb_in{i}") for i in range(BSLOTS)]
        brow_out = sem("brow_out")
        out_done = sem("out_done")
        job_full = sem("job_full")
        job_free = [sem("job_free0"), sem("job_free1")]
        da_ready, scan_done, bx_ready = sem("da_ready"), sem("scan_done"), sem("bx_ready")
        hT_ready, mul_done, mac_done, red_done = sem("hT_ready"), sem("mul_done"), sem("mac_done"), sem("red_done")
        carry_done, gated = sem("carry_done"), sem("gated")
        xs_ready, halo_ready, xi_ready, gate_ready = sem("xs_ready"), sem("halo_ready"), sem("xi_ready"), sem("gate_ready")
        sp_ready, delta_ready, dx_ready = sem("sp_ready"), sem("delta_ready"), sem("dx_ready")
        ss_dve, ss_act, mag_pe, mag_act = sem("ss_dve"), sem("ss_act"), sem("mag_pe"), sem("mag_act")
        dve_own, act_own, pool_own = sem("dve_own"), sem("act_own"), sem("pool_own")
        diag_ready, A_ready, rstd_ready, fe_ready = sem("diag_ready"), sem("A_ready"), sem("rstd_ready"), sem("fe_ready")
        aexp_ready, init_done = sem("aexp_ready"), sem("init_done")
        mx_ready, p_ready, pn_ready = sem("mx_ready"), sem("p_ready"), sem("pn_ready")
        f_scaled, f_silu, f_h = sem("f_scaled"), sem("f_silu"), sem("f_h")
        out_ready = sem("out_ready")
        mask_in, flag_row, flag_ready = sem("mask_in"), sem("flag_row"), sem("flag_ready")
        chain = sem("general_chain")
        gmask_in, gout_done = sem("general_mask_in"), sem("general_out_done")

        block = ctx.enter_context(nc.Block())

        def wait_full(eng, job):
            eng.wait_ge(job_full, INDEX[job] + 1)

        def wait_read(eng, job):
            q = INDEX[job]
            eng.wait_ge(job_free[q % 2], q // 2 + 1)

        def bank(job):
            return pp[:, INDEX[job] % 2, :]

        def freed(job):
            return job_free[INDEX[job] % 2]

        def batch_base(b):
            return b * (len(BATCH_STEPS) + GB * len(TILE_STEPS))

        def step(eng, b, name, i=None):
            if i is None:
                at = batch_base(b) + BATCH_STEPS.index(name)
                if at:
                    eng.wait_ge(chain, at)
            else:
                eng.wait_ge(chain, i * len(TILE_STEPS) + (batch_base(b) + len(BATCH_STEPS) + TILE_STEPS.index(name)))

        class Own:

            def __init__(self, eng, s):
                self.eng, self.s, self.n = eng, s, 0

            def mark(self, ins):
                ins.then_inc(self.s, 1)
                self.n += 1
                return self.n

            def after(self, n=None):
                self.eng.wait_ge(self.s, self.n if n is None else n)

        @block.sync
        def _(sp):
            def load_x(c):
                g = c * NT
                sp.dma_start(xt[:, g:g + NT, :], x[g * P:(g + NT) * P, :].rearrange("(g p) d -> p g d", p=P)).then_inc(s_x[c], 16)

            load_x(0)
            load_x(1)
            sp.dma_start(vec[:, :], vecs).then_inc(s_vec, 16)
            sp.dma_start(con[:, :], consts).then_inc(s_vec, 16)
            sp.dma_start(win, w_in.rearrange("(k p) o -> p k o", p=P)).then_inc(s_w, 16)
            sp.dma_start(wx[:, :, :], w_x.rearrange("(m p) o -> p m o", p=P)).then_inc(s_w, 16)
            sp.dma_start(wdt[:, :], w_dt).then_inc(s_w, 16)
            load_x(2)
            load_x(3)
            for i, w in enumerate((wq, wqT, wk, wvT, woT)):
                sp.dma_start(aw[:, i, :, :], w.rearrange("(k p) o -> p k o", p=P)).then_inc(s_aw, 16)
            sp.dma_start(wt, wtT.rearrange("(k p) o -> p k o", p=P)).then_inc(s_aw, 16)
            sp.dma_start(wo[:, :, :], w_out.rearrange("(m p) o -> p m o", p=P)).then_inc(s_aw, 16)
            sp.dma_start(mrow, mask[0:1, :].to_broadcast([NH, S])).then_inc(s_mrow, 16)
            for n in range(NCH):
                wait_read(sp, ("X", n, 0))
                sp.dma_start(brow[n], dbc[DR:DR + NS, :]).then_inc(brow_out, 16)
                sp.wait_ge(brow_out, 16 * (n + 1))
                for j in range(PIECES):
                    piece = PIECES * n + j
                    if piece >= BSLOTS:
                        sp.wait_ge(bx_ready, 2 * BROWS * (piece - BSLOTS + 1))
                    slot = piece % BSLOTS
                    src = brow[n:n + 1, j * BROWS:(j + 1) * BROWS, :].to_broadcast([P, BROWS, T])
                    sp.dma_start(Bb[:, slot * BROWS:(slot + 1) * BROWS, :], src).then_inc(bb_in[slot], 16)
            wait_full(sp, ("Z", NCH - 1, 3))
            sp.dma_start(W1, f1.rearrange("(k p) o -> p k o", p=P)).then_inc(s_ff1, 16)
            sp.dma_start(W2, f2.rearrange("(k p) o -> p k o", p=P)).then_inc(s_ff2, 16)
            sp.dma_start(W3, f3.rearrange("(k p) o -> p k o", p=P)).then_inc(s_ff3, 16)
            wait_full(sp, ("O", NCH - 2, 1))
            sp.dma_start(H1, fh1.rearrange("(k p) o -> p k o", p=P)).then_inc(s_ffh1, 16)
            sp.wait_ge(hT_ready, NCH * NS * NT)
            sp.dma_start(H2, fh2.rearrange("(k p) o -> p k o", p=P)).then_inc(s_ffh2, 16)
            sp.dma_start(mask_w, mask.bitcast(I32).rearrange("(g p) w -> p g w", p=P)).then_inc(mask_in, 16)
            sp.wait_ge(red_done, 2 * NCH * NS)
            sp.dma_start(mask_0, mask[0:1, :].bitcast(I32).to_broadcast([P, S // 4])).then_inc(mask_in, 16)
            for i in range(2 * B):
                sp.wait_ge(out_ready, i + 1)
                g = i * NT
                sp.dma_start(out[g * P:(g + NT) * P, :].rearrange("(g p) d -> p g d", p=P), outs[:, i // 2, i % 2 * NT:i % 2 * NT + NT, :]).then_inc(out_done, 16)
            sp.wait_ge(out_done, 16 * 2 * B)
            sp.wait_ge(flag_ready, 1)
            with sp.If(sp.value_load(flag_i[0:1, 0:1], min_val=0, max_val=1)):
                for b in range(B):
                    base = batch_base(b) + len(BATCH_STEPS)
                    for i in range(GB):
                        step(sp, b, "mask", i)
                        sp.dma_start(gmask, mask[i * P:(i + 1) * P, :]).then_inc(gmask_in, 16)
                        sp.wait_ge(chain, (i + 1) * len(TILE_STEPS) + base)
                        g = b * GB + i
                        sp.dma_start(out[g * P:(g + 1) * P, :], gout).then_inc(gout_done, 16)
                        sp.wait_ge(gout_done, 16 * (g + 1))

        @block.tensor
        def _(pe):
            mm = nc.tensor.matmul

            def job_F(job, o):
                pe.wait_ge(s_vec, 32)
                for b in range(B):
                    for k in range(KD):
                        c0 = VEC["cond"][0] + k * B + b
                        last = mm(o[:, b:b + 1], vec[:, c0:c0 + 1].to_broadcast([P, P]), v("score_w")[:, k:k + 1], start=k == 0, stop=k == KD - 1)
                return last

            def job_TP(job, o):
                pe.wait_ge(s_aw, 16 * 7)
                cond = v("cond").rearrange("p (k b) -> p k b", k=KD)
                for m in range(KD):
                    for k in range(KD):
                        last = mm(o[:, m * B:(m + 1) * B], wt[:, k, m * P:(m + 1) * P], cond[:, k, :], start=k == 0, stop=k == KD - 1)
                return last

            def job_U(job, o):
                wait_read(pe, ("TP", 0, 0))
                for k in range(KD):
                    for m in range(KD):
                        last = mm(o[:, k * B * NH:(k + 1) * B * NH], aw[:, 0, m, k * P:(k + 1) * P], tpD[:, m, :, :], start=m == 0, stop=m == KD - 1)
                return last

            def job_T(job, o):
                _, n, k = job
                pe.wait_ge(xs_ready, n + 1)
                for i in range(NT):
                    last = nc.tensor.transpose(o[:, i * P:(i + 1) * P], xs(n)[:, i, k * P:(k + 1) * P], ident)
                return last

            def in_proj(n, o, col):
                wait_read(pe, ("T", n, 1))
                for k in range(KD):
                    last = mm(o, win[:, k, col:col + P], xnT(n)[:, k, :], start=k == 0, stop=k == KD - 1)
                return last

            def job_I(job, o):
                _, n, m = job
                if n == 0 and m == 0:
                    wait_read(pe, ("T", n, 0))
                    pe.wait_ge(s_w, 48)
                return in_proj(n, o, m * P)

            def job_Z(job, o):
                _, n, m = job
                return in_proj(n, o, DI + m * P)

            def job_V(job, o):
                _, n, m = job
                wait_read(pe, ("I", n, m))
                pe.wait_ge(halo_ready, n + 1)
                if n == 0 and m == 0:
                    pe.wait_ge(diag_ready, CT * KC + CT)
                for k in range(KC):
                    last = mm(o, dg[:, m, k, :], xr3[:, m, k:k + T], start=k == 0, stop=k == KC - 1)
                return last

            def job_X(job, o):
                _, n, _ = job
                pe.wait_ge(xi_ready, n + 1)
                for m in range(CT):
                    last = mm(o[0:DR + 2 * NS, :], wx[:, m, :], xi(n)[:, m, :], start=m == 0, stop=m == CT - 1)
                return last

            def job_XT(job, o):
                _, n, _ = job
                wait_read(pe, ("X", n, 0))
                w = DR + 2 * NS
                for i in range(NT):
                    last = nc.tensor.transpose(o[:, i * w:(i + 1) * w], dbc[:, i * P:(i + 1) * P], ident[0:w, 0:w])
                return last

            def job_D(job, o):
                _, n, m = job
                wait_read(pe, ("X", n, 0))
                return mm(o, wdt[:, m * P:(m + 1) * P], dbc[0:DR, :], start=True, stop=True)

            def skip(o, e, i, m, first):
                mm(o[:, m * P:(m + 1) * P], diagD[:, m, :], xi(e)[:, m, i * P:(i + 1) * P], start=first, stop=False, skip_group_check=True)

            def add_turned(o, m, src, last):
                return mm(o[:, m * P:(m + 1) * P], src, ident, start=False, stop=last, is_transpose=True, skip_group_check=True)

            def job_Y(job, o):
                _, e, i = job
                pe.wait_ge(mac_done, 2 * (NS * (e + 1) - 1) + i // 2 + 1)
                for m in range(CT):
                    skip(o, e, i, m, m == 0)
                for m in range(CT):
                    last = add_turned(o, m, yTd[:, e % 2, i // 2, m * P:(m + 1) * P], True)
                return last

            def job_O(job, o):
                _, e, j = job
                for i in (1, 3):
                    wait_read(pe, ("Y", e, i))
                pe.wait_ge(gated, 2 * (e + 1))
                for i in range(2):
                    t0 = (2 * j + i) * P
                    for m in range(CT):
                        last = mm(o[:, i * DM:(i + 1) * DM], dx(e)[:, m, t0:t0 + P], wo[:, m, :], start=m == 0, stop=m == CT - 1)
                return last

            def job_R(job, o):
                _, e, j = job
                wait_read(pe, ("O", e, j))
                for k in range(KD):
                    for i in range(2):
                        g = e * NT + 2 * j + i
                        last = nc.tensor.transpose(o[:, (2 * k + i) * P:(2 * k + i + 1) * P], xt[:, g, k * P:(k + 1) * P], ident)
                return last

            def job_A(job, o):
                _, b, _ = job
                for h in range(HALVES):
                    for j in range(2):
                        wait_read(pe, ("R", b * HALVES + h, j))
                if b == 0:
                    wait_read(pe, ("U", 0, 0))
                for i in range(GB):
                    for k in range(KD):
                        last = mm(o[:, i * NH:(i + 1) * NH], x1T[:, k, i * P:(i + 1) * P], u[:, k, b * NH:(b + 1) * NH], start=k == 0, stop=k == KD - 1)
                return last

            def rows_by_heads(b, o, w):
                for k in range(KD):
                    for i in range(GB):
                        last = mm(o[:, k * NH:(k + 1) * NH], xt[:, b * GB + i, k * P:(k + 1) * P], w[:, i, :], start=i == 0, stop=i == GB - 1)
                return last

            def weight_by_heads(o, w, src):
                for m in range(KD):
                    for k in range(KD):
                        last = mm(o[:, m * NH:(m + 1) * NH], aw[:, w, k, m * P:(m + 1) * P], src[:, k, :], start=k == 0, stop=k == KD - 1)
                return last

            def job_G(job, o):
                wait_read(pe, ("A", job[1], 0))
                return rows_by_heads(job[1], o, a_sb)

            def job_M(job, o):
                wait_read(pe, ("G", job[1], 0))
                return weight_by_heads(o, 1, g_sb)

            def job_RR(job, o):
                wait_read(pe, ("M", job[1], 0))
                return weight_by_heads(o, 2, qD)

            def scores(job, o, j):
                wait_read(pe, ("RR", job[1], 0))
                for k in range(KD):
                    last = mm(o[0:NH, :], r_sb[:, k, :], x1T[:, k, j * 512:(j + 1) * 512], start=k == 0, stop=k == KD - 1)
                return last

            def job_S0(job, o):
                return scores(job, o, 0)

            def job_S1(job, o):
                return scores(job, o, 1)

            def job_PT(job, o):
                pe.wait_ge(pn_ready, job[1] + 1)
                for i in range(GB):
                    last = nc.tensor.transpose(o[:, i * NH:(i + 1) * NH], sm[:, i * P:(i + 1) * P], ident[0:NH, 0:NH])
                return last

            def job_YV(job, o):
                wait_read(pe, ("PT", job[1], 0))
                return rows_by_heads(job[1], o, pT)

            def job_VV(job, o):
                wait_read(pe, ("YV", job[1], 0))
                return weight_by_heads(o, 3, yv)

            def job_WO(job, o):
                wait_read(pe, ("VV", job[1], 0))
                for m in range(KD):
                    for k in range(KD):
                        last = mm(o[:, m:m + 1], aw[:, 4, k, m * P:(m + 1) * P], ov[:, k:k + 1], start=k == 0, stop=k == KD - 1)
                return last

            def ffn(o, w, src, outs, ins):
                for m in range(outs):
                    for k in range(ins):
                        last = mm(o[:, m * B:(m + 1) * B], w[:, k, m * P:(m + 1) * P], src[:, k, :], start=k == 0, stop=k == ins - 1)
                return last

            def job_W12(job, o):
                wait_read(pe, ("WO", 0, 0))
                wait_read(pe, ("WO", 1, 0))
                pe.wait_ge(s_ff1, 16)
                ffn(o[:, 0:KH * B], W1, z_sb, KH, KD)
                pe.wait_ge(s_ff2, 16)
                return ffn(o[:, KH * B:2 * KH * B], W2, z_sb, KH, KD)

            def job_FL(job, o):
                pe.wait_ge(flag_row, 1)
                return nc.tensor.transpose(o[0:1, 0:P], flag[:, 0:1], ident)

            def job_H1(job, o):
                pe.wait_ge(f_h, 1)
                pe.wait_ge(s_ffh1, 16)
                return ffn(o, H1, ff[:, 0, :, :], KH, KH)

            def job_H2(job, o):
                pe.wait_ge(f_h, 2)
                pe.wait_ge(s_ffh2, 16)
                return ffn(o, H2, ff[:, 1, :, :], KH, KH)

            def job_W3(job, o):
                pe.wait_ge(f_h, 3)
                pe.wait_ge(s_ff3, 16)
                return ffn(o, W3, ff[:, 0, :, :], KD, KH)

            def job_FB(job, o):
                wait_read(pe, ("W3", 0, 0))
                for k in range(KD):
                    last = nc.tensor.transpose(o[:, k * P:(k + 1) * P], fo[:, k, job[1]:job[1] + 1].to_broadcast([P, P]), ident)
                return last

            jobs = dict(F=job_F, TP=job_TP, U=job_U, T=job_T, I=job_I, Z=job_Z, V=job_V, X=job_X, XT=job_XT, D=job_D, Y=job_Y,
                        O=job_O, R=job_R, A=job_A, G=job_G, M=job_M, RR=job_RR, S0=job_S0, S1=job_S1, PT=job_PT, YV=job_YV,
                        VV=job_VV, WO=job_WO, W12=job_W12, FL=job_FL, H1=job_H1, H2=job_H2, W3=job_W3, FB=job_FB)

            def run(job):
                q = INDEX[job]
                if q >= 2:
                    pe.wait_ge(job_free[q % 2], q // 2)
                jobs[job[0]](job, bank(job)).then_inc(job_full, 1)

            def transposes(n, i):
                if i == 0:
                    pe.wait_ge(scan_done, CT * (n + 1))
                e = 2 * n + i // 2
                if e >= 1:
                    pe.wait_ge(mac_done if i % 2 else mul_done, e)
                for m in range(CT):
                    last = nc.tensor.transpose(hT[:, i % 2, m * P:(m + 1) * P], hb[:, n % 3, m, i * P:(i + 1) * P], ident)
                last.then_inc(hT_ready, 1)

            def reduce(n, i):
                e = 2 * n + i // 2
                s = n % NS
                pe.wait_ge(mul_done, e + 1)
                o = yacc[:, i // 2, :]
                if s == 0:
                    c = n // NS
                    if c:
                        pe.wait_ge(gated, 2 * (c - 1) + i // 2 + 1)
                    for m in range(CT):
                        skip(o, c, i, m, m == 0)
                for m in range(CT):
                    last = add_turned(o, m, hc[:, e % 2, m * P:(m + 1) * P], s == NS - 1)
                last.then_inc(red_done, 1)

            run(("F", 0, 0))
            for b in range(B):
                pe.wait_ge(ss_act, 4 if b == 0 else 12)
                if b == 0:
                    pe.wait_ge(ss_dve, 4)
                dst = yacc if b == 0 else hT
                for i in range(GB):
                    last = nc.tensor.transpose(dst[:, i // 4, (i % 4) * P:(i % 4 + 1) * P], ss[:, b * GB + i:b * GB + i + 1].to_broadcast([P, P]), ident)
                last.then_inc(mag_pe, 1)
            for job in HEAD[1:]:
                run(job)
            pe.wait_ge(mag_act, 2)
            for c in range(NCH):
                for s in range(NS):
                    n = c * NS + s
                    jobs_now = list(BESIDE[c, s])
                    if n:
                        transposes(n - 1, 0)
                        transposes(n - 1, 1)
                    for job in jobs_now[:1]:
                        if not (job[0] == "Y" and s == 0):
                            run(job)
                            jobs_now.remove(job)
                    if n:
                        transposes(n - 1, 2)
                        transposes(n - 1, 3)
                        reduce(n - 1, 0)
                        reduce(n - 1, 2)
                    for job in jobs_now:
                        run(job)
            n = NCH * NS
            for i in range(NT):
                transposes(n - 1, i)
            reduce(n - 1, 0)
            reduce(n - 1, 2)
            for job in TAIL:
                run(job)

            def general_batch(b):
                def did(ins):
                    ins.then_inc(chain, 1)

                for j in range(GB // 2):
                    step(pe, b, f"turn_x{j}")
                    for k in range(KD):
                        for i in range(2):
                            last = nc.tensor.transpose(pp[:, 0, (2 * k + i) * P:(2 * k + i + 1) * P], xt[:, b * GB + 2 * j + i, k * P:(k + 1) * P], ident)
                    did(last)
                step(pe, b, "a")
                for i in range(GB):
                    for k in range(KD):
                        last = mm(pp[:, 0, i * NH:(i + 1) * NH], x1T[:, k, i * P:(i + 1) * P], u[:, k, b * NH:(b + 1) * NH], start=k == 0, stop=k == KD - 1)
                did(last)
                step(pe, b, "g")
                did(rows_by_heads(b, pp[:, 0, :], a_sb))
                step(pe, b, "m")
                did(weight_by_heads(pp[:, 0, :], 1, g_sb))
                step(pe, b, "r")
                did(weight_by_heads(pp[:, 0, :], 2, qD))
                for j in range(2):
                    step(pe, b, f"s{j}")
                    for k in range(KD):
                        last = mm(pp[0:NH, 0, :], r_sb[:, k, :], x1T[:, k, j * 512:(j + 1) * 512], start=k == 0, stop=k == KD - 1)
                    did(last)
                for j in range(GB // 2):
                    step(pe, b, f"v{j}")
                    for i in range(2):
                        for k in range(KD):
                            t0 = (2 * j + i) * P
                            last = mm(pp[:, 0, i * DM:(i + 1) * DM], x1T[:, k, t0:t0 + P], aw[:, 3, k, :], start=k == 0, stop=k == KD - 1)
                    did(last)
                with pe.Fori(0, GB) as t:
                    for h in range(NH):
                        step(pe, b, f"row{h}", t)
                        for j in range(2):
                            last = mm(hT[:, j, :], ident[0:NH, h:h + 1].to_broadcast([NH, P]), sm[:, j * 512:(j + 1) * 512], start=True, stop=True)
                        did(last)
                        step(pe, b, f"turn{h}", t)
                        for i in range(GB):
                            last = nc.tensor.transpose(yacc[:, i // 4, (i % 4) * P:(i % 4 + 1) * P], gsc[:, i * P:(i + 1) * P], ident)
                        did(last)
                        step(pe, b, f"pv{h}", t)
                        for i in range(GB):
                            last = mm(dA[:, 0, h * HE:(h + 1) * HE], gpT[:, i, :], gv[:, i, h * HE:(h + 1) * HE], start=i == 0, stop=i == GB - 1)
                        did(last)
                    step(pe, b, "turn_o", t)
                    for k in range(KD):
                        last = nc.tensor.transpose(pp[:, 0, k * P:(k + 1) * P], go[:, k * P:(k + 1) * P], ident)
                    did(last)

                    def layer(dst, w, src, outs_, ins_):
                        for m in range(outs_):
                            for k in range(ins_):
                                last = mm(dst(m), w[:, k, m * P:(m + 1) * P], src[:, k, :], start=k == 0, stop=k == ins_ - 1)
                        return last

                    def in_hT(m):
                        return hT[:, m // 4, (m % 4) * P:(m % 4 + 1) * P]

                    def in_yacc(m):
                        return yacc[:, m // 4, (m % 4) * P:(m % 4 + 1) * P]

                    def in_pp(m):
                        return pp[:, 0, m * P:(m + 1) * P]

                    step(pe, b, "wo", t)
                    did(layer(in_pp, aw[:, 4, :, :], goT, KD, KD))
                    step(pe, b, "w12", t)
                    layer(in_hT, W1, gz, KH, KD)
                    did(layer(in_yacc, W2, gz, KH, KD))
                    step(pe, b, "h1", t)
                    did(layer(in_hT, H1, gf1, KH, KH))
                    step(pe, b, "h2", t)
                    did(layer(in_hT, H2, gf2, KH, KH))
                    step(pe, b, "w3", t)
                    did(layer(in_pp, W3, gf1, KD, KH))
                    step(pe, b, "turn_f", t)
                    for k in range(KD):
                        last = nc.tensor.transpose(pp[:, 1, k * P:(k + 1) * P], gf3[:, k, :], ident)
                    did(last)

            pe.wait_ge(flag_ready, 1)
            with pe.If(pe.value_load(flag_i[0:1, 0:1], min_val=0, max_val=1)):
                pe.wait_ge(out_done, 16 * 2 * B)
                for b in range(B):
                    general_batch(b)

        @block.scalar
        def _(act):
            A = nc.scalar.activation
            own = Own(act, act_own)

            def ev_U(job, o):
                return A(u[:, :, :], o[:, 0:KD * B * NH].rearrange("p (k j) -> p k j", k=KD), ACT.Copy)

            def ev_T(job, o):
                _, n, k = job
                if n == 1:
                    wait_full(act, ("Z", 0, 3))
                return A(xnT(n)[:, k, :], o, ACT.Copy, scale=v("rms_w")[:, k:k + 1])

            def ev_I(job, o):
                _, n, m = job
                if m == 0:
                    if n % HALVES == 0:
                        if n == 0:
                            act.wait_ge(init_done, 1)
                        else:
                            wait_full(act, ("V", n - 1, 3))
                        A(xr3[:, :, 0:KC - 1], zero[:, :, :], ACT.Copy).then_inc(halo_ready, 1)
                    else:
                        wait_full(act, ("V", n - 1, 3))
                        wait_read(act, ("I", n - 1, 3))
                        wait_read(act, ("I", n - 1, 2))
                        A(xr3[:, :, 0:KC - 1], xr3[:, :, T:T + KC - 1], ACT.Copy).then_inc(halo_ready, 1)
                    act.wait_ge(halo_ready, n + 1)
                return A(xr3[:, m, KC - 1:], o, ACT.Copy)

            def ev_V(job, o):
                _, n, m = job
                if n >= 2:
                    wait_full(act, ("Y", n - 2, 3))
                    act.wait_ge(red_done, 2 * NS * (n - 1))
                return A(xi(n)[:, m, :], o, ACT.Identity, bias=v("conv_b")[:, m:m + 1])

            def silu(n, both):
                for m in range(CT):
                    wait_read(act, ("V", n, m))
                A(xi(n), xi(n), ACT.Silu).then_inc(xi_ready, 1)
                if both:
                    silu_gate(n - 1)

            def silu_gate(n):
                for m in range(CT):
                    wait_read(act, ("Z", n, m))
                A(gate(n), gate(n), ACT.Silu).then_inc(gate_ready, 1)

            def ev_X(job, o):
                _, n, _ = job
                if n:
                    wait_full(act, ("D", n - 1, 3))
                    act.wait_ge(brow_out, 16 * n)
                return A(dbc[:, :], o[0:DR + 2 * NS, :], ACT.Copy)

            def ev_XT(job, o):
                _, n, _ = job
                if n >= 2:
                    act.wait_ge(mac_done, 2 * NS * (n - 1))
                w = DR + 2 * NS
                return A(CTs[:, n % 2, :, :], o[:, 0:NT * w].rearrange("p (i w) -> p i w", i=NT)[:, :, DR + NS:w], ACT.Copy)

            def ev_Z(job, o):
                _, n, m = job
                if n >= 2:
                    wait_read(act, ("Y", n - 2, 3))
                    wait_read(act, ("Y", n - 2, 1))
                    act.wait_ge(gated, 2 * (n - 1))
                return A(gate(n)[:, m, :], o, ACT.Copy)

            def ev_D(job, o):
                _, n, m = job
                if m == 0:
                    if n:
                        wait_full(act, ("Z", n, 3))
                    if n >= 2:
                        wait_full(act, ("O", n - 2, 1))
                A(delta(n)[:, m, :], o, ACT.Abs, bias=v("dt_b")[:, m:m + 1])
                return A(dx(n)[:, m, :], o, ACT.Relu, bias=v("dt_b")[:, m:m + 1])

            def softplus(n):
                for m in range(CT):
                    wait_read(act, ("D", n, m))
                own.mark(A(delta(n), delta(n), ACT.Exp, scale=-1.0))
                own.after()
                A(delta(n), delta(n), ACT.Ln, bias=1.0).then_inc(sp_ready, 1)

            def ev_R(job, o):
                _, e, j = job
                if e == HALVES:
                    wait_full(act, ("S1", 0, 0))
                if e == 0 and j == 0:
                    act.wait_ge(ss_dve, 4 + GB + 1)
                t0 = (e % HALVES) * T + 2 * j * P
                return A(x1T[:, :, t0:t0 + 2 * P], o.rearrange("p (k t) -> p k t", k=KD), ACT.Copy)

            def ev_A(job, o):
                return A(a_sb[:, :, :], o[:, 0:GB * NH].rearrange("p (i h) -> p i h", i=GB), ACT.Copy)

            def ev_G(job, o):
                return A(g_sb[:, :, :], o[:, 0:KD * NH].rearrange("p (k h) -> p k h", k=KD), ACT.Copy)

            def ev_RR(job, o):
                return A(r_sb[:, :, :], o[:, 0:KD * NH].rearrange("p (k h) -> p k h", k=KD), ACT.Copy, scale=HE ** -0.5)

            def softmax(b):
                act.wait_ge(mx_ready, b + 1)
                A(sm[:, :], sm[:, :], ACT.Exp, bias=st[:, 1:2], accum_out=st[:, 2:3]).then_inc(p_ready, 1)

            def ev_PT(job, o):
                return A(pT[:, :, :], o[:, 0:GB * NH].rearrange("p (i h) -> p i h", i=GB), ACT.Copy)

            def ev_YV(job, o):
                return A(yv[:, :, :], o[:, 0:KD * NH].rearrange("p (k h) -> p k h", k=KD), ACT.Copy)

            def ev_WO(job, o):
                return A(z_sb[:, :, job[1]], o[:, 0:KD], ACT.Copy)

            evs = dict(U=ev_U, T=ev_T, I=ev_I, V=ev_V, X=ev_X, XT=ev_XT, Z=ev_Z, D=ev_D, R=ev_R, A=ev_A, G=ev_G, RR=ev_RR,
                       PT=ev_PT, YV=ev_YV, WO=ev_WO)

            def after_job(job):
                name, n, i = job
                if name == "V" and i == CT - 1:
                    silu(n, n > 0)
                if name == "D" and i == CT - 1:
                    softplus(n)
                if name == "S1":
                    softmax(n)

            def read(job):
                if job[0] in evs:
                    wait_full(act, job)
                    evs[job[0]](job, bank(job)).then_inc(freed(job), 1)
                after_job(job)

            def square(g):
                if g % NT == 0 or (g < GB and g % NT == 1):
                    act.wait_ge(s_x[g // NT], 16)
                A(hb[:, 0, g % CT, 0:DM], xt[:, g, :], ACT.Square, accum_out=ss[:, g:g + 1]).then_inc(ss_act, 1)
            for i, g in enumerate(range(1, GB, 2)):
                if i:
                    act.wait_ge(ss_act, i)
                square(g)
            wait_read(act, ("F", 0, 0))
            A(fr[:, 1, :], fr[:, 0, :], ACT.Exp, scale=-1.0).then_inc(fe_ready, 1)
            def rstd(b):
                act.wait_ge(ss_act, 4 if b == 0 else 12)
                if b == 0:
                    act.wait_ge(ss_dve, 4)
                    act.wait_ge(init_done, 1)
                gs = slice(b * GB, (b + 1) * GB)
                own.mark(A(lnv[:, gs], ss[:, gs], ACT.Ln, bias=eps[:, :], scale=1.0 / DM))
                own.after()
                A(lnv[:, gs], lnv[:, gs], ACT.Exp, scale=-0.5).then_inc(rstd_ready, 1)
            rstd(0)
            act.wait_ge(s_vec, 32)
            A(Aneg[:, :], v("A_log"), ACT.Exp).then_inc(aexp_ready, 1)
            for g in range(GB, 2 * GB):
                act.wait_ge(ss_act, 4 + g - GB)
                square(g)
            rstd(1)
            act.wait_ge(mag_pe, 2)
            for i in range(2):
                A(magrow[:, i * 512:(i + 1) * 512], hT[:, i, :], ACT.Copy).then_inc(mag_act, 1)
            for job in HEAD:
                read(job)

            def exp_step(n, m):
                c, s = n // NS, n % NS
                i = n * CT + m
                if s == 0 and m == 0:
                    act.wait_ge(delta_ready, c + 1)
                if n == 0 and m == 0:
                    act.wait_ge(A_ready, 1)
                if i >= 2:
                    act.wait_ge(scan_done, i - 1)
                A(dA[:, m % 2, :], delta(c)[:, m, :], ACT.Exp, scale=Aneg[:, m * NS + s:m * NS + s + 1]).then_inc(da_ready, 1)

            def mul_step(n, i):
                c, s = n // NS, n % NS
                e = 2 * n + i // 2
                act.wait_ge(hT_ready, NT * n + i + 1)
                if e >= 2:
                    act.wait_ge(red_done, e - 1)
                A(hc[:, e % 2, :], hT[:, 0, :], ACT.Copy, scale=CTs[:, c % 2, i, s:s + 1]).then_inc(mul_done, 1)

            def carry_step(n):
                c, s = n // NS, n % NS
                if c % HALVES == 0:
                    act.wait_ge(scan_done, CT * (n + 1))
                    A(carry[:, s, :], hb[:, n % 3, :, T - 1], ACT.Copy).then_inc(carry_done, 1)

            for c in range(NCH):
                for s in range(NS):
                    n = c * NS + s
                    exp_step(n, 0)
                    exp_step(n, 1)
                    if n:
                        mul_step(n - 1, 0)
                    exp_step(n, 2)
                    exp_step(n, 3)
                    if n:
                        mul_step(n - 1, 2)
                        carry_step(n - 1)
                    for job in BESIDE[c, s]:
                        read(job)
                    if c == NCH - 1 and s == 8:
                        silu_gate(NCH - 1)
            n = NCH * NS
            mul_step(n - 1, 0)
            mul_step(n - 1, 2)
            for job in TAIL:
                read(job)
                if job[0] == "W12":
                    act.wait_ge(f_scaled, 1)
                    A(ff[:, 2, :, :], ff[:, 2, :, :], ACT.Silu).then_inc(f_silu, 1)
                if job[0] in ("H1", "H2"):
                    i = 1 if job[0] == "H1" else 2
                    wait_read(act, job)
                    A(ff[:, i % 2, :, :], ff[:, 2, :, :], ACT.Gelu).then_inc(f_h, 1)

            def general_batch(b):
                def did(ins):
                    ins.then_inc(chain, 1)

                for j in range(GB // 2):
                    step(act, b, f"turn_x_out{j}")
                    did(A(x1T[:, :, 2 * j * P:2 * (j + 1) * P], pp[:, 0, :].rearrange("p (k t) -> p k t", k=KD), ACT.Copy))
                step(act, b, "a_out")
                did(ev_A(None, pp[:, 0, :]))
                step(act, b, "g_out")
                did(ev_G(None, pp[:, 0, :]))
                step(act, b, "r_out")
                did(ev_RR(None, pp[:, 0, :]))
                for j in range(2):
                    step(act, b, f"s{j}_out")
                    did(A(sm[:, j * 512:(j + 1) * 512], pp[0:NH, 0, :], ACT.Copy))
                for j in range(GB // 2):
                    step(act, b, f"v_out{j}")
                    did(A(gv[:, 2 * j:2 * j + 2, :], pp[:, 0, :].rearrange("p (i o) -> p i o", i=2), ACT.Copy))
                with act.Fori(0, GB) as t:
                    for h in range(NH):
                        step(act, b, f"exp{h}", t)
                        did(A(gsc, gsc, ACT.Exp, bias=gst[:, 1:2], accum_out=gst[:, 2:3]))
                        step(act, b, f"turn_out{h}", t)
                        did(A(gpT, yacc[:, :, :].rearrange("p a (i t) -> p (a i) t", i=4), ACT.Copy))
                    step(act, b, "turn_o_out", t)
                    did(A(goT, pp[:, 0, 0:DM].rearrange("p (k t) -> p k t", k=KD), ACT.Copy))
                    step(act, b, "wo_out", t)
                    did(A(gz, pp[:, 0, 0:DM].rearrange("p (k t) -> p k t", k=KD), ACT.Copy))
                    step(act, b, "silu", t)
                    did(A(gf1, gf1, ACT.Silu))
                    step(act, b, "gelu1", t)
                    did(A(gf2, gf2, ACT.Gelu))
                    step(act, b, "gelu2", t)
                    did(A(gf1, gf1, ACT.Gelu))

            act.wait_ge(flag_ready, 1)
            with act.If(act.value_load(flag_i[0:1, 0:1], min_val=0, max_val=1)):
                for b in range(B):
                    general_batch(b)

        @block.gpsimd
        def _(pool):
            nc.gpsimd.memset(eps[:, :], EPS)
            nc.gpsimd.memset(zero[:, :, :], 0.0).then_inc(init_done, 1)
            pool.wait_ge(s_vec, 32)
            for m in range(CT):
                for k in range(KC):
                    nc.gpsimd.tensor_scalar(dg[:, m, k, :], ident, v("conv_w")[:, m * KC + k:m * KC + k + 1], 1.0, ALU.mult, ALU.mult).then_inc(diag_ready, 1)
            for m in range(CT):
                nc.gpsimd.tensor_scalar(diagD[:, m, :], ident, v("D")[:, m:m + 1], 1.0, ALU.mult, ALU.mult).then_inc(diag_ready, 1)

            def input_step(n, pair):
                c, s = n // NS, n % NS
                piece = n // BROWS
                row = (piece % BSLOTS) * BROWS + s % BROWS
                if s % BROWS == 0 and pair == 0:
                    pool.wait_ge(bb_in[piece % BSLOTS], 16 * (piece // BSLOTS + 1))
                if s == 0 and pair == 0:
                    pool.wait_ge(dx_ready, c + 1)
                if n >= 3:
                    pool.wait_ge(hT_ready, NT * (n - 2))
                    if (n - 3) // NS % HALVES == 0:
                        done = (n - 3) // NS // HALVES * NS + (n - 3) % NS + 1
                        pool.wait_ge(carry_done, done)
                ms = slice(2 * pair, 2 * pair + 2)
                nc.gpsimd.tensor_tensor(hb[:, n % 3, ms, :], dx(c)[:, ms, :], Bb[:, row:row + 1, :].to_broadcast([P, 2, T]), ALU.mult).then_inc(bx_ready, 1)

            def dx_step(c):
                pool.wait_ge(delta_ready, c + 1)
                pool.wait_ge(xi_ready, c + 1)
                nc.gpsimd.tensor_tensor(dx(c), delta(c), xi(c), ALU.mult).then_inc(dx_ready, 1)

            dx_step(0)
            for c in range(NCH):
                for s in range(NS):
                    n = c * NS + s
                    input_step(n, 0)
                    input_step(n, 1)
                    if s == 13 and c + 1 < NCH:
                        dx_step(c + 1)

        @block.vector
        def _(dve):
            V = nc.vector
            own = Own(dve, dve_own)

            def rows(c):
                if c >= 2:
                    dve.wait_ge(scan_done, NS * CT * (c - 1))
                for i in range(NT):
                    g = c * NT + i
                    last = V.tensor_scalar(xs(c)[:, i, :], xt[:, g, :], scl[:, g:g + 1], None, ALU.mult)
                last.then_inc(xs_ready, 1)

            def ev_F(job, o):
                return V.tensor_scalar(fr[:, 0, :], o[:, 0:B], v("score_b"), None, ALU.add)

            def ev_TP(job, o):
                tp = o[:, 0:KD * B].rearrange("p (m b) -> p m b", m=KD)
                return V.tensor_tensor(tpD[:, :, :, :], bm[:, :, None, :].to_broadcast([P, KD, B, NH]), tp[:, :, :, None].to_broadcast([P, KD, B, NH]), ALU.mult)

            def gate_tile(e, i, o):
                dve.wait_ge(gate_ready, e + 1)
                t0 = slice(i * P, (i + 1) * P)
                return V.tensor_tensor(dx(e)[:, :, t0], o.rearrange("p (m t) -> p m t", m=CT), gate(e)[:, :, t0], ALU.mult)

            def gate_even(e):
                for i in (0, 2):
                    dve.wait_ge(red_done, 2 * (NS * (e + 1) - 1) + i // 2 + 1)
                    gate_tile(e, i, yacc[:, i // 2, :]).then_inc(gated, 1)

            def ev_Y(job, o):
                return gate_tile(job[1], job[2], o)

            def ev_O(job, o):
                _, e, j = job
                for i in range(2):
                    g = e * NT + 2 * j + i
                    last = V.scalar_tensor_tensor(xt[:, g, :], xt[:, g, :], keep1[:, g:g + 1], o[:, i * DM:(i + 1) * DM], ALU.mult, ALU.add)
                return last

            def ev_M(job, o):
                return V.tensor_tensor(qD[:, :, :], o[:, 0:KD * NH].rearrange("p (m h) -> p m h", m=KD), bm, ALU.mult)

            def ev_S0(job, o):
                if job[1]:
                    wait_full(dve, ("PT", 0, 0))
                return V.tensor_tensor(sm[:, 0:512], o[0:NH, :], negm[:, 0:512], ALU.add)

            def ev_S1(job, o):
                return V.tensor_tensor(sm[:, 512:1024], o[0:NH, :], negm[:, 512:1024], ALU.add)

            def softmax(b):
                wait_read(dve, ("S0", b, 0))
                wait_read(dve, ("S1", b, 0))
                own.mark(V.reduce_max(st[:, 0:1], sm[:, :], AX.X))
                own.after()
                V.tensor_scalar(st[:, 1:2], st[:, 0:1], -1.0, None, ALU.mult).then_inc(mx_ready, 1)
                dve.wait_ge(p_ready, b + 1)
                own.mark(V.reciprocal(st[:, 3:4], st[:, 2:3]))
                own.after()
                V.tensor_scalar(sm[:, :], sm[:, :], st[:, 3:4], None, ALU.mult).then_inc(pn_ready, 1)

            def ev_VV(job, o):
                own.mark(V.tensor_tensor(ovj[:, :, :], o[:, 0:KD * NH].rearrange("p (m h) -> p m h", m=KD), bm, ALU.mult))
                own.after()
                return V.reduce_sum(ov[:, :], ovj[:, :, :], AX.X)

            def scaled(dst, o, name, n):
                return V.tensor_tensor(dst, o.rearrange("p (m b) -> p m b", b=B), v(name)[:, :, None].to_broadcast([P, n, B]), ALU.mult)

            def ev_W12(job, o):
                w = KH * B
                scaled(ff[:, 2, :, :], o[:, 0:w], "w1_s", KH).then_inc(f_scaled, 1)
                scaled(ff[:, 3, :, :], o[:, w:2 * w], "w2_s", KH).then_inc(freed(job), 1)
                dve.wait_ge(f_silu, 1)
                wait_read(dve, job)
                V.tensor_tensor(ff[:, 0, :, :], ff[:, 2, :, :], ff[:, 3, :, :], ALU.mult).then_inc(f_h, 1)
                return None

            def ev_H(job, o):
                i = 1 if job[0] == "H1" else 2
                dve.wait_ge(f_h, i)
                return scaled(ff[:, 2, :, :], o[:, 0:KH * B], "h1_s" if i == 1 else "h2_s", KH)

            def ev_W3(job, o):
                return scaled(fo[:, :, :], o[:, 0:KD * B], "w3_s", KD)

            def ev_FB(job, o):
                b = job[1]
                for j in range(2):
                    g = b * GB + j * NT
                    V.tensor_tensor(outs[:, b, j * NT:(j + 1) * NT, :], xt[:, g:g + NT, :], o[:, None, 0:DM].to_broadcast([P, NT, DM]), ALU.add).then_inc(out_ready, 1)
                return None

            def compare_rows():
                dve.wait_ge(mask_in, 32)
                m3 = mask_w.rearrange("p (g w) -> p g w", g=GB)
                own.mark(V.tensor_tensor(m3, m3, mask_0[:, None, :].to_broadcast([P, GB, S // 4]), ALU.bitwise_xor))
                own.after()
                V.reduce_max(flag[:, 0:1], mask_w, AX.X).then_inc(flag_row, 1)

            def ev_FL(job, o):
                own.mark(V.reduce_max(flag[0:1, 1:2], o[0:1, 0:P], AX.X))
                own.after()
                own.mark(V.tensor_scalar(flag[0:1, 1:2], flag[0:1, 1:2], 1.0, None, ALU.min))
                own.after()
                return V.tensor_copy(flag_i[:, :], flag[0:1, 1:2])

            evs = dict(F=ev_F, TP=ev_TP, Y=ev_Y, O=ev_O, M=ev_M, S0=ev_S0, S1=ev_S1, VV=ev_VV, W12=ev_W12, H1=ev_H, H2=ev_H, W3=ev_W3, FB=ev_FB, FL=ev_FL)

            def read(job):
                if job[0] in evs:
                    wait_full(dve, job)
                    last = evs[job[0]](job, bank(job))
                    if last is not None:
                        last.then_inc(freed(job), 1)
                if job[0] == "S1":
                    softmax(job[1])
                if job == ("VV", 1, 0):
                    compare_rows()

            for i, g in enumerate(range(0, GB, 2)):
                if g % NT == 0:
                    dve.wait_ge(s_x[g // NT], 16)
                V.tensor_tensor_reduce(out=hb[:, 1, i, 0:DM], in0=xt[:, g, :], in1=xt[:, g, :], scale=1.0, scalar=0.0, op0=ALU.mult, op1=ALU.add,
                                       accum_out=ss[:, g:g + 1]).then_inc(ss_dve, 1)
            read(("F", 0, 0))
            dve.wait_ge(fe_ready, 1)
            own.mark(V.tensor_scalar(fr[:, 2, :], fr[:, 1, :], 1.0, None, ALU.add))
            own.after()
            own.mark(V.reciprocal(fr[:, 1, :], fr[:, 2, :]))
            own.after()
            frac = own.mark(V.tensor_scalar(fr[:, 2, :], fr[:, 1, :], float(S), 1.0, ALU.mult, ALU.max))

            def count(g, rows_, scratch):
                return V.tensor_scalar(scratch, rows_, ss[:, g:g + 1], None, ALU.is_gt, ALU.add, accum_out=cnt[:, g:g + 1])

            def kept(gs, b):
                own.mark(V.tensor_scalar(keep[:, gs], cnt[:, gs], 1.0, fr[:, 2, b:b + 1], ALU.add, ALU.is_le))
                own.after()
                V.tensor_scalar(keep1[:, gs], keep[:, gs], 1.0, None, ALU.add)
                own.mark(V.tensor_tensor(scl[:, gs], keep[:, gs], lnv[:, gs], ALU.mult))
                own.after()

            dve.wait_ge(mag_pe, 1)
            dve.wait_ge(ss_act, 4)
            rows0 = yacc[:, :, :].rearrange("p a b -> p (a b)")
            for g in range(NT):
                if g:
                    own.after()
                own.mark(count(g, rows0, junk[:, 0:S]))
            dve.wait_ge(rstd_ready, 1)
            own.after()
            kept(slice(0, NT), 0)
            rows(0)
            for g in range(NT, GB):
                own.after()
                own.mark(count(g, rows0, junk[:, 0:S]))
            own.after()
            kept(slice(NT, GB), 0)
            dve.wait_ge(aexp_ready, 1)
            V.tensor_scalar(Aneg[:, :], Aneg[:, :], -1.0, None, ALU.mult).then_inc(A_ready, 1)
            read(("TP", 0, 0))
            dve.wait_ge(s_mrow, 16)
            V.tensor_scalar(negm[:, :], mrow, -1.0, FLT_MAX, ALU.add, ALU.mult)
            dve.wait_ge(ss_act, 12)
            dve.wait_ge(mag_act, 2)
            for g in range(GB, 2 * GB):
                own.after()
                own.mark(count(g, magrow, junk[:, 0:S]))
            dve.wait_ge(rstd_ready, 2)
            own.after()
            kept(slice(GB, 2 * GB), 1)
            V.tensor_copy(fr[:, 3, :], cnt[:, 14:16]).then_inc(ss_dve, GB + 1)

            def delta_step(c):
                dve.wait_ge(sp_ready, c + 1)
                V.tensor_tensor(delta(c), delta(c), dx(c), ALU.add).then_inc(delta_ready, 1)

            def scan_step(n, m):
                c, s = n // NS, n % NS
                i = n * CT + m
                dve.wait_ge(da_ready, i + 1)
                if m % 2 == 0:
                    dve.wait_ge(bx_ready, 2 * n + m // 2 + 1)
                if c % HALVES:
                    if m == 0:
                        dve.wait_ge(carry_done, c // HALVES * NS + s + 1)
                    start = carry[:, s, m:m + 1]
                else:
                    start = 0.0
                V.tensor_tensor_scan(hb[:, n % 3, m, :], dA[:, m % 2, :], hb[:, n % 3, m, :], start, ALU.mult, ALU.add).then_inc(scan_done, 1)

            def mac_step(n, i):
                c, s = n // NS, n % NS
                e = 2 * n + i // 2
                dve.wait_ge(hT_ready, NT * n + i + 1)
                dst = yTd[:, c % 2, i // 2, :]
                src, cs = hT[:, 1, :], CTs[:, c % 2, i, s:s + 1]
                if s == 0:
                    if c >= 2 and i == 1:
                        wait_full(dve, ("Y", c - 2, 3))
                    V.tensor_scalar(dst, src, cs, None, ALU.mult).then_inc(mac_done, 1)
                else:
                    dve.wait_ge(mac_done, e - 1)
                    V.scalar_tensor_tensor(dst, src, cs, dst, ALU.mult, ALU.add).then_inc(mac_done, 1)

            delta_step(0)
            for c in range(NCH):
                for s in range(NS):
                    n = c * NS + s
                    scan_step(n, 0)
                    scan_step(n, 1)
                    if n:
                        mac_step(n - 1, 1)
                    scan_step(n, 2)
                    scan_step(n, 3)
                    if n:
                        mac_step(n - 1, 3)
                    if s == 0:
                        if c:
                            gate_even(c - 1)
                        if c + 1 < NCH:
                            rows(c + 1)
                    for job in BESIDE[c, s]:
                        read(job)
                    if s == 12 and c + 1 < NCH:
                        delta_step(c + 1)
            n = NCH * NS
            mac_step(n - 1, 1)
            mac_step(n - 1, 3)
            gate_even(NCH - 1)
            for job in TAIL:
                read(job)

            def general_batch(b):
                def did(ins):
                    ins.then_inc(chain, 1)

                step(dve, b, "m_out")
                did(ev_M(None, pp[:, 0, :]))
                with dve.Fori(0, GB) as t:
                    step(dve, b, "mask", t)
                    dve.wait_ge(gmask_in, (t + (b * GB + 1)) * 16)
                    did(V.tensor_scalar(gadd, gmask, -1.0, FLT_MAX, ALU.add, ALU.mult))
                    for h in range(NH):
                        step(dve, b, f"add{h}", t)
                        did(V.tensor_tensor(gsc, hT[:, :, :].rearrange("p a s -> p (a s)"), gadd, ALU.add))
                        step(dve, b, f"max{h}", t)
                        did(V.reduce_max(gst[:, 0:1], gsc, AX.X))
                        step(dve, b, f"neg{h}", t)
                        did(V.tensor_scalar(gst[:, 1:2], gst[:, 0:1], -1.0, None, ALU.mult))
                        step(dve, b, f"recip{h}", t)
                        did(V.reciprocal(gst[:, 3:4], gst[:, 2:3]))
                        step(dve, b, f"norm{h}", t)
                        did(V.tensor_scalar(gsc, gsc, gst[:, 3:4], None, ALU.mult))
                    step(dve, b, "o_out", t)
                    did(V.tensor_copy(go, dA[:, 0, 0:DM]))

                    def by_row(dst, src, name, n):
                        return V.tensor_tensor(dst, src, v(name)[:, :, None].to_broadcast([P, n, P]), ALU.mult)

                    hT3 = hT[:, :, :].rearrange("p a (m t) -> p (a m) t", m=4)
                    yacc3 = yacc[:, :, :].rearrange("p a (m t) -> p (a m) t", m=4)
                    step(dve, b, "w1_out", t)
                    did(by_row(gf1, hT3, "w1_s", KH))
                    step(dve, b, "w2_out", t)
                    did(by_row(gf2, yacc3, "w2_s", KH))
                    step(dve, b, "gated", t)
                    did(V.tensor_tensor(gf1, gf1, gf2, ALU.mult))
                    step(dve, b, "h1_out", t)
                    did(by_row(gf2, hT3, "h1_s", KH))
                    step(dve, b, "h2_out", t)
                    did(by_row(gf1, hT3, "h2_s", KH))
                    step(dve, b, "w3_out", t)
                    did(by_row(gf3, pp[:, 0, 0:DM].rearrange("p (k t) -> p k t", k=KD), "w3_s", KD))
                    step(dve, b, "sum", t)
                    x1 = xt[:, bass.ds(t + b * GB, 1), :].rearrange("p a d -> p (a d)")
                    did(V.tensor_tensor(gout, x1, pp[:, 1, 0:DM], ALU.add))

            wait_read(dve, ("FL", 0, 0))
            V.tensor_copy(flag[0:1, 0:1], flag_i[:, :]).then_inc(flag_ready, 1)
            with dve.If(dve.value_load(flag_i[0:1, 0:1], min_val=0, max_val=1)):
                for b in range(B):
                    general_batch(b)


_OUT = [B, S, DM]


def layout(i):
    def parts(name, a):
        a = np.asarray(a)
        n = a.shape[0] // P
        return a.reshape((n, P) + a.shape[1:]).swapaxes(0, 1).reshape(P, -1)

    cols = {
        "rms_w": i["L0_attn_rms_w"], "conv_w": i["L0_attn_conv_w"], "conv_b": i["L0_attn_conv_b"], "dt_b": i["L0_attn_dt_b"],
        "A_log": i["L0_attn_A_log"], "D": i["L0_attn_D"], "score_w": i["L0_cond_score_w"],
        "cond": np.asarray(i["cond_1024"]).T, "w1_s": i["L0_ffn_w1_s"], "w2_s": i["L0_ffn_w2_s"],
        "h1_s": i["L0_ffn_h1_s"], "h2_s": i["L0_ffn_h2_s"], "w3_s": i["L0_ffn_w3_s"],
    }
    packed = [np.broadcast_to(np.asarray(i["L0_cond_score_b"]).reshape(1, 1), (P, 1)) if n == "score_b" else parts(n, cols[n]) for n in VEC]
    eye = np.eye(P, dtype=np.float32)
    heads = (np.arange(DM)[:, None] // HE == np.arange(NH)[None, :]).astype(np.float32)
    return [
        np.asarray(i["x"]).reshape(B * S, DM), np.asarray(i["L0_attn_in_proj"]), np.asarray(i["L0_attn_out_proj"]),
        np.asarray(i["L0_attn_x_proj"]), np.asarray(i["L0_attn_dt_w"]), np.asarray(i["L0_cond2_Wq"]),
        np.asarray(i["L0_cond2_Wq"]).T, np.asarray(i["L0_cond2_Wk"]), np.asarray(i["L0_cond2_Wv"]).T,
        np.asarray(i["L0_cond2_Wt"]).T, np.asarray(i["L0_cond2_Wo"]).T, np.asarray(i["L0_ffn_w1_w"]).T,
        np.asarray(i["L0_ffn_w2_w"]).T, np.asarray(i["L0_ffn_h1_w"]).T, np.asarray(i["L0_ffn_h2_w"]).T,
        np.asarray(i["L0_ffn_w3_w"]).T, np.asarray(i["mask_SxS_bk0"]), np.concatenate(packed, axis=1),
        np.concatenate([eye, parts("heads", heads)], axis=1),
    ]


def kernel(**inputs):
    import concourse.bacc as bacc
    from concourse.bass_utils import run_bass_kernel_spmd

    nc = bacc.Bacc("TRN2", target_bir_lowering=False, num_devices=1)
    arrays, args = {}, []
    for n, a in enumerate(layout(inputs)):
        a = np.ascontiguousarray(a)
        arrays[f"in_{n}"] = a
        args.append(nc.dram_tensor(f"in_{n}", a.shape, mybir.dt.from_np(a.dtype), kind="ExternalInput").ap())
    out = nc.dram_tensor("out_0", [B * S, DM], F32, kind="ExternalOutput").ap()
    build(nc, *args, out)
    r = run_bass_kernel_spmd(nc, [arrays], core_ids=[0])
    return r.results[0]["out_0"].reshape(B, S, DM)
```

```python
import numpy as np
import concourse.bass as bass
from concourse import mybir
from concourse.alu_op_type import AluOpType as ALU
from contextlib import ExitStack

F32 = mybir.dt.float32
BF16 = mybir.dt.bfloat16
U8 = mybir.dt.uint8
I32 = mybir.dt.int32
ACT = mybir.ActivationFunctionType
AX = mybir.AxisListType

P = 128
B, S, DM = 2, 1024, 256
DI, NS, DR, KC = 512, 16, 16, 4
NH, HE = 16, 16
HID = 1024
KD = DM // P
CT = DI // P
T = 512
NT = T // P
HALVES = S // T
NCH = B * HALVES
NG = B * S // P
GB = S // P
KH = HID // P
FLT_MAX = float(np.finfo(np.float32).max)
EPS = 1e-5

VEC = {}
_at = 0
for _name, _n in (("rms_w", KD), ("conv_w", CT * KC), ("conv_b", CT), ("dt_b", CT), ("A_log", CT * NS), ("D", CT),
                  ("score_w", KD), ("cond", KD * B), ("score_b", 1), ("w1_s", KH), ("w2_s", KH), ("h1_s", KH),
                  ("h2_s", KH), ("w3_s", KD)):
    VEC[_name] = (_at, _at + _n)
    _at += _n
NVEC = _at

BROWS = 2
BSLOTS = 5
PIECES = NS // BROWS


ATT = [6, 8, 7, 9, 11, 13, 14, 16, 17, 19, 21, 23, 25, 27]
ATT1 = [28, 30]
DXS = [13, 14]


def prologue_slots(n):
    slots = {4: [("I", n, 0)], 6: [("I", n, 1), ("I", n, 2)], 8: [("I", n, 3)], 9: [("V", n, 0)], 10: [("V", n, 1)], 12: [("V", n, 2)],
             14: [("V", n, 3)], 16: [("Z", n, 0), ("Z", n, 1)], 18: [("Z", n, 2), ("Z", n, 3)], 20: [("X", n, 0)],
             22: [("XT", n, 0), ("D", n, 0)], 24: [("D", n, 1), ("D", n, 2)], 26: [("D", n, 3)]}
    slots[2] = [("T", n, 0), ("T", n, 1)]
    return slots


def epilogue_slots(e):
    turn = (18, 20) if e == NCH - 2 else (11, 13)
    return {1: [("Y", e, 1), ("Y", e, 3)], 3: [("O", e, 0)], 5: [("O", e, 1)], turn[0]: [("R", e, 0)], turn[1]: [("R", e, 1)]}


def attention_jobs(b):
    return [("A", b, 0), ("G", b, 0), ("A", b, 1), ("G", b, 1)] + [(name, b, 0) for name in ("GT", "M", "RR", "S0", "S1", "PT", "YV", "YT", "VV", "WO")]


def all_slots():
    head = [("F", 0, 0), ("TP", 0, 0), ("U", 0, 0)]
    head += [("T", 0, k) for k in range(KD)] + [("I", 0, m) for m in range(CT)] + [("V", 0, m) for m in range(CT)]
    head += [("X", 0, 0), ("XT", 0, 0)] + [("D", 0, m) for m in range(CT)]
    beside = [[] for _ in range(2 * NCH * NS)]
    for c in range(NCH):
        at = 2 * c * NS
        if c == 0:
            for m in range(CT):
                beside[m // 2] += [("Z", 0, m)]
        else:
            for h, jobs in epilogue_slots(c - 1).items():
                beside[at + h] += jobs
        if c + 1 < NCH:
            for h, jobs in prologue_slots(c + 1).items():
                beside[at + h] += jobs
    for i, job in enumerate(attention_jobs(0)):
        beside[2 * (NCH - 1) * NS + ATT[i]] += [job]
    for i, job in enumerate(attention_jobs(1)[:2]):
        beside[2 * (NCH - 1) * NS + ATT1[i]] += [job]
    tail = []
    for s, jobs in sorted(epilogue_slots(NCH - 1).items()):
        tail += jobs
    tail += attention_jobs(1)[2:]
    tail += [("W1", 0, 0), ("W1", 1, 0), ("W2", 0, 0), ("W2", 1, 0), ("WT", 0, 0)]
    tail += [("H", 1, 0), ("FL", 0, 0), ("H", 1, 1), ("HT", 1, 0), ("H", 2, 0), ("H", 2, 1), ("HT", 2, 0)]
    tail += [("W3", 0, 0), ("FB", 0, 0), ("FB", 1, 0)]
    return head, beside, tail


BATCH_STEPS = [f"{x}{i}" for i in range(GB // 2) for x in ("turn_x", "turn_x_out")]
BATCH_STEPS += ["a", "a_out", "g", "g_out", "m", "m_out", "r", "r_out", "s0", "s0_out", "s1", "s1_out"]
BATCH_STEPS += [f"{x}{i}" for i in range(GB // 2) for x in ("v", "v_out")]
TILE_STEPS = ["mask"] + [f"{x}{h}" for h in range(NH) for x in ("row", "add", "max", "neg", "exp", "recip", "norm", "turn", "turn_out", "pv")]
TILE_STEPS += ["o_out", "turn_o", "turn_o_out", "wo", "wo_out", "w12", "w1_out", "w2_out", "silu", "gated", "h1", "h1_out", "gelu1",
               "h2", "h2_out", "gelu2", "w3", "w3_out", "turn_f", "sum"]

HEAD, BESIDE, TAIL = all_slots()
ORDER = HEAD + [job for jobs in BESIDE for job in jobs] + TAIL
INDEX = {job: q for q, job in enumerate(ORDER)}


def to_read(h):
    return BESIDE[h - 1] if h else []


WARM = {("A", 1, 1): 2, ("G", 1, 1): 2, ("GT", 1, 0): 2, ("M", 1, 0): 2, ("RR", 1, 0): 2, ("S1", 1, 0): 12, ("PT", 1, 0): 2, ("YV", 1, 0): 2,
        ("YT", 1, 0): 2, ("VV", 1, 0): 2, ("WO", 1, 0): 2}
WARM_HEAD = [20, 16]


def build(nc, x, w_in, w_out, w_x, w_dt, wq, wqT, wk, wvT, wtT, woT, f1, f2, fh1, fh2, f3, mask, w3_s, vecs, consts, out):
    ctx = ExitStack()
    with ctx:
        def sb(name, shape, dt=F32):
            return ctx.enter_context(nc.sbuf_tensor(name, shape, dt))

        def sem(name):
            return ctx.enter_context(nc.semaphore(name))

        xt = sb("xt", [P, NG, DM])
        x1T = sb("x1T", [P, KD, S])
        wi = sb("wi", [P, KD * 2 * DI])
        wo = sb("wo", [P, CT, DM])
        wx = sb("wx", [P, CT, DR + 2 * NS])
        wdt = sb("wdt", [DR, DI])
        aw = sb("aw", [P, 5, KD, DM])
        vec = sb("vec", [P, NVEC])
        con = sb("con", [P, P + 2 * NH])
        diag = sb("diag", [P, CT * KC * P])
        diagD = sb("diagD", [P, CT, P])
        xr = sb("xr", [P, CT * (T + KC - 1)])
        par = [sb(f"par{i}", [P, 4, CT * T]) for i in range(2)]
        scanmem = sb("scanmem", [P, BSLOTS * BROWS * T + 3 * CT * T])
        hc = sb("hc", [P, 2, T])
        small = sb("small", [P, 2, DI])
        yTd = sb("yTd", [P, 2, 2, DI])
        dbc = sb("dbc", [DR + 2 * NS, T])
        CTs = sb("CTs", [P, 2, NT, NS])
        carry = sb("carry", [P, NS, CT])
        Aneg = sb("Aneg", [P, CT * NS])
        ss = sb("ss", [P, NG])
        cnt = sb("cnt", [P, NG])
        keep = sb("keep", [P, NG])
        keep1 = sb("keep1", [P, NG])
        scl = sb("scl", [P, NG])
        lnv = sb("lnv", [P, NG])
        fr = sb("fr", [P, 4, B])
        eps = sb("eps", [P, 1])
        half_b = sb("half_b", [P, CT])
        zero = sb("zero", [P, CT, KC - 1])
        tpD = sb("tpD", [P, KD, B, NH])
        u = sb("u", [P, KD, B * NH])
        a_sb = sb("a_sb", [P, GB, NH])
        g_sb = sb("g_sb", [P, KD, NH])
        qD = sb("qD", [P, KD, NH])
        r_sb = sb("r_sb", [P, KD, NH])
        pT = sb("pT", [P, GB, NH])
        yv = sb("yv", [P, KD, NH])
        ov = sb("ov", [P, KD])
        ovj = sb("ovj", [P, KD, NH])
        z_sb = sb("z_sb", [P, KD, B])
        sm = sb("sm", [NH, S])
        st = sb("st", [NH, 5])
        negm = sb("negm", [NH, S])
        ff = sb("ff", [P, 4, KH, B])
        w3_row = sb("w3_row", [B, DM])
        flag = sb("flag", [P, 2])
        flag_i = sb("flag_i", [1, 1], I32)
        gst = sb("gst", [P, 4])

        ident = con[:, 0:P]
        bm = con[:, P:P + 2 * NH].rearrange("p (k h) -> p k h", k=KD)

        def v(name):
            lo, hi = VEC[name]
            return vec[:, lo:hi]

        def xi(n):
            return par[n % 2][:, 0, :].rearrange("p (m t) -> p m t", m=CT)

        def delta(n):
            return par[n % 2][:, 1, :].rearrange("p (m t) -> p m t", m=CT)

        def dx(n):
            return par[n % 2][:, 2, :].rearrange("p (m t) -> p m t", m=CT)

        def gate(n):
            return par[n % 2][:, 3, :].rearrange("p (m t) -> p m t", m=CT)

        def xs(n):
            return par[n % 2][:, 1, 0:NT * DM].rearrange("p (i d) -> p i d", i=NT)

        def xnT(n):
            return par[n % 2 if n else 1][:, 1, NT * DM:NT * DM + KD * T].rearrange("p (k t) -> p k t", k=KD)

        win = wi[:, :].rearrange("p (k o) -> p k o", k=KD)
        Bb = scanmem[:, 0:BSLOTS * BROWS * T].rearrange("p (r t) -> p r t", t=T)
        hb = scanmem[:, BSLOTS * BROWS * T:].rearrange("p (r m t) -> p r m t", r=3, m=CT)
        xr3 = xr[:, :].rearrange("p (m t) -> p m t", m=CT)
        dg = diag[:, :].rearrange("p (m k q) -> p m k q", m=CT, k=KC)
        magrow = x1T[:, 0, :]
        junk = par[1][:, 0, :]
        mrow = x1T[0:NH, 1, 0:S // 4].bitcast(U8)
        wt = hc[:, 0, :].rearrange("p (k o) -> p k o", k=KD)
        mask_w = par[1][:, 1, :].bitcast(I32)
        mask_0 = hc[:, 0, 0:S // 4].bitcast(I32)
        outs = par[1][:, 0:3:2, :].rearrange("p a (g d) -> p a g d", d=DM)
        gv = par[1][:, 0, :].rearrange("p (i o) -> p i o", i=GB)
        gadd, gsc = par[1][:, 1, 0:S], par[1][:, 1, S:2 * S]
        gpT = par[1][:, 2, 0:S].rearrange("p (i t) -> p i t", i=GB)
        gmask = par[1][:, 2, S:S + S // 4].bitcast(U8)
        gout = par[1][:, 2, S + S // 2:S + S // 2 + DM]
        gf1 = par[1][:, 3, 0:HID].rearrange("p (m t) -> p m t", m=KH)
        gf2 = par[1][:, 3, HID:2 * HID].rearrange("p (m t) -> p m t", m=KH)
        go = small[:, 0, 0:DM]
        goT = small[:, 0, DM:2 * DM].rearrange("p (k t) -> p k t", k=KD)
        gz = small[:, 1, 0:DM].rearrange("p (k t) -> p k t", k=KD)
        gf3 = small[:, 1, DM:2 * DM].rearrange("p (k t) -> p k t", k=KD)
        g_row, y_row = sm[:, 0:DM], sm[:, DM:2 * DM]
        row1, row2, row3 = sm[0:B, :], negm[0:B, :], negm[0:B, 0:DM]
        W1 = wi[:, :].rearrange("p (k o) -> p k o", k=KD)
        W2 = xr[:, 0:KD * HID].rearrange("p (k o) -> p k o", k=KD)
        W3 = diag[:, :].rearrange("p (k o) -> p k o", k=KH)
        H1 = par[0][:, :, :].rearrange("p a (b o) -> p (a b) o", b=2)
        H2 = scanmem[:, 0:KH * HID].rearrange("p (k o) -> p k o", k=KH)

        dA = ctx.enter_context(nc.psum_tensor("dA", [P, 2, T], F32))
        hT = ctx.enter_context(nc.psum_tensor("hT", [P, 2, DI], F32))
        yacc = ctx.enter_context(nc.psum_tensor("yacc", [P, 2, DI], F32))
        pp = ctx.enter_context(nc.psum_tensor("pp", [P, 2, 512], F32))
        brow = nc.dram_tensor("brow", [NCH, NS, T], F32, kind="Internal").ap()

        s_vec, s_x, s_w, s_aw, s_mrow = sem("vec_in"), [sem(f"x_in{i}") for i in range(NCH)], sem("w_in"), sem("aw_in"), sem("mrow_in")
        s_ff1, s_ff2, s_ff3, s_ffh1, s_ffh2 = (sem(f"ff_in{i}") for i in range(5))
        bb_in = [sem(f"bb_in{i}") for i in range(BSLOTS)]
        brow_out = sem("brow_out")
        out_done = sem("out_done")
        job_full = sem("job_full")
        job_free = [sem("job_free0"), sem("job_free1")]
        da_ready, scan_done, bx_ready = sem("da_ready"), sem("scan_done"), sem("bx_ready")
        hT_ready, mul_done, mac_done, red_done = sem("hT_ready"), sem("mul_done"), sem("mac_done"), sem("red_done")
        carry_done, gated = sem("carry_done"), sem("gated")
        xs_ready, halo_ready, xi_ready = sem("xs_ready"), sem("halo_ready"), sem("xi_ready")
        half_ready, tanh_ready = sem("half_ready"), sem("tanh_ready")
        sp_ready, delta_ready, dx_ready = sem("sp_ready"), sem("delta_ready"), sem("dx_ready")
        ss_dve, ss_act, mag_pe, mag_act = sem("ss_dve"), sem("ss_act"), sem("mag_pe"), sem("mag_act")
        dve_own, act_own, pool_own = sem("dve_own"), sem("act_own"), sem("pool_own")
        diag_ready, A_ready, rstd_ready, fe_ready = sem("diag_ready"), sem("A_ready"), sem("rstd_ready"), sem("fe_ready")
        aexp_ready, init_done = sem("aexp_ready"), sem("init_done")
        mx_ready, p_ready, recip_ready = sem("mx_ready"), sem("p_ready"), sem("recip_ready")
        f_scaled, f_silu, f_h = sem("f_scaled"), sem("f_silu"), sem("f_h")
        out_ready = sem("out_ready")
        mask_in, flag_row, flag_ready = sem("mask_in"), sem("flag_row"), sem("flag_ready")
        chain = sem("general_chain")
        gmask_in, gout_done = sem("general_mask_in"), sem("general_out_done")

        block = ctx.enter_context(nc.Block())

        def wait_full(eng, job):
            eng.wait_ge(job_full, INDEX[job] + 1)

        def wait_read(eng, job):
            q = INDEX[job]
            eng.wait_ge(job_free[q % 2], q // 2 + 1)

        def bank(job):
            return pp[:, INDEX[job] % 2, :]

        def freed(job):
            return job_free[INDEX[job] % 2]

        def batch_base(b):
            return b * (len(BATCH_STEPS) + GB * len(TILE_STEPS))

        def step(eng, b, name, i=None):
            if i is None:
                at = batch_base(b) + BATCH_STEPS.index(name)
                if at:
                    eng.wait_ge(chain, at)
            else:
                eng.wait_ge(chain, i * len(TILE_STEPS) + (batch_base(b) + len(BATCH_STEPS) + TILE_STEPS.index(name)))

        class Own:

            def __init__(self, eng, s):
                self.eng, self.s, self.n = eng, s, 0

            def mark(self, ins):
                ins.then_inc(self.s, 1)
                self.n += 1
                return self.n

            def after(self, n=None):
                self.eng.wait_ge(self.s, self.n if n is None else n)

        @block.sync
        def _(sp):
            def load_x(c):
                g = c * NT
                sp.dma_start(xt[:, g:g + NT, :], x[g * P:(g + NT) * P, :].rearrange("(g p) d -> p g d", p=P)).then_inc(s_x[c], 16)

            load_x(0)
            load_x(1)
            sp.dma_start(vec[:, :], vecs).then_inc(s_vec, 16)
            sp.dma_start(con[:, :], consts).then_inc(s_vec, 16)
            sp.dma_start(win, w_in.rearrange("(k p) o -> p k o", p=P)).then_inc(s_w, 16)
            sp.dma_start(wx[:, :, :], w_x.rearrange("(m p) o -> p m o", p=P)).then_inc(s_w, 16)
            sp.dma_start(wdt[:, :], w_dt).then_inc(s_w, 16)
            load_x(2)
            load_x(3)
            for i, w in enumerate((wq, wqT, wk, wvT, woT)):
                sp.dma_start(aw[:, i, :, :], w.rearrange("(k p) o -> p k o", p=P)).then_inc(s_aw, 16)
            sp.dma_start(wt, wtT.rearrange("(k p) o -> p k o", p=P)).then_inc(s_aw, 16)
            sp.dma_start(wo[:, :, :], w_out.rearrange("(m p) o -> p m o", p=P)).then_inc(s_aw, 16)
            sp.dma_start(w3_row[:, :], w3_s.to_broadcast([B, DM])).then_inc(s_ff3, 16)
            sp.dma_start(mrow, mask[0:1, :].to_broadcast([NH, S])).then_inc(s_mrow, 16)
            for n in range(NCH):
                wait_read(sp, ("X", n, 0))
                sp.dma_start(brow[n], dbc[DR:DR + NS, :]).then_inc(brow_out, 16)
                sp.wait_ge(brow_out, 16 * (n + 1))
                for j in range(PIECES):
                    piece = PIECES * n + j
                    if piece >= BSLOTS:
                        sp.wait_ge(bx_ready, 2 * BROWS * (piece - BSLOTS + 1))
                    slot = piece % BSLOTS
                    src = brow[n:n + 1, j * BROWS:(j + 1) * BROWS, :].to_broadcast([P, BROWS, T])
                    sp.dma_start(Bb[:, slot * BROWS:(slot + 1) * BROWS, :], src).then_inc(bb_in[slot], 16)
            wait_full(sp, ("Z", NCH - 1, 3))
            sp.dma_start(W1, f1.rearrange("(k p) o -> p k o", p=P)).then_inc(s_ff1, 16)
            sp.dma_start(W2, f2.rearrange("(k p) o -> p k o", p=P)).then_inc(s_ff2, 16)
            sp.dma_start(W3, f3.rearrange("(k p) o -> p k o", p=P)).then_inc(s_ff3, 16)
            wait_full(sp, ("O", NCH - 2, 1))
            sp.dma_start(H1, fh1.rearrange("(k p) o -> p k o", p=P)).then_inc(s_ffh1, 16)
            sp.wait_ge(hT_ready, NCH * NS * NT)
            sp.dma_start(H2, fh2.rearrange("(k p) o -> p k o", p=P)).then_inc(s_ffh2, 16)
            sp.dma_start(mask_w, mask.bitcast(I32).rearrange("(g p) w -> p g w", p=P)).then_inc(mask_in, 16)
            sp.wait_ge(red_done, 2 * NCH * NS)
            sp.dma_start(mask_0, mask[0:1, :].bitcast(I32).to_broadcast([P, S // 4])).then_inc(mask_in, 16)
            for i in range(2 * B):
                sp.wait_ge(out_ready, i + 1)
                g = i * NT
                sp.dma_start(out[g * P:(g + NT) * P, :].rearrange("(g p) d -> p g d", p=P), outs[:, i // 2, i % 2 * NT:i % 2 * NT + NT, :]).then_inc(out_done, 16)
            sp.wait_ge(out_done, 16 * 2 * B)
            sp.wait_ge(flag_ready, 1)
            with sp.If(sp.value_load(flag_i[0:1, 0:1], min_val=0, max_val=1)):
                for b in range(B):
                    base = batch_base(b) + len(BATCH_STEPS)
                    for i in range(GB):
                        step(sp, b, "mask", i)
                        sp.dma_start(gmask, mask[i * P:(i + 1) * P, :]).then_inc(gmask_in, 16)
                        sp.wait_ge(chain, (i + 1) * len(TILE_STEPS) + base)
                        g = b * GB + i
                        sp.dma_start(out[g * P:(g + 1) * P, :], gout).then_inc(gout_done, 16)
                        sp.wait_ge(gout_done, 16 * (g + 1))

        @block.tensor
        def _(pe):
            mm = nc.tensor.matmul

            def job_F(job, o):
                pe.wait_ge(s_vec, 32)
                for b in range(B):
                    for k in range(KD):
                        c0 = VEC["cond"][0] + k * B + b
                        last = mm(o[:, b:b + 1], vec[:, c0:c0 + 1].to_broadcast([P, P]), v("score_w")[:, k:k + 1], start=k == 0, stop=k == KD - 1)
                return last

            def job_TP(job, o):
                pe.wait_ge(s_aw, 16 * 7)
                cond = v("cond").rearrange("p (k b) -> p k b", k=KD)
                for m in range(KD):
                    for k in range(KD):
                        last = mm(o[:, m * B:(m + 1) * B], wt[:, k, m * P:(m + 1) * P], cond[:, k, :], start=k == 0, stop=k == KD - 1)
                return last

            def job_U(job, o):
                wait_read(pe, ("TP", 0, 0))
                for k in range(KD):
                    for m in range(KD):
                        last = mm(o[:, k * B * NH:(k + 1) * B * NH], aw[:, 0, m, k * P:(k + 1) * P], tpD[:, m, :, :], start=m == 0, stop=m == KD - 1)
                return last

            def job_T(job, o):
                _, n, k = job
                pe.wait_ge(xs_ready, n + 1)
                for i in range(NT):
                    last = nc.tensor.transpose(o[:, i * P:(i + 1) * P], xs(n)[:, i, k * P:(k + 1) * P], ident)
                return last

            def in_proj(n, o, col):
                wait_read(pe, ("T", n, 1))
                for k in range(KD):
                    last = mm(o, win[:, k, col:col + P], xnT(n)[:, k, :], start=k == 0, stop=k == KD - 1)
                return last

            def job_I(job, o):
                _, n, m = job
                if n == 0 and m == 0:
                    wait_read(pe, ("T", n, 0))
                    pe.wait_ge(s_w, 48)
                return in_proj(n, o, m * P)

            def job_Z(job, o):
                _, n, m = job
                return in_proj(n, o, DI + m * P)

            def job_V(job, o):
                _, n, m = job
                wait_read(pe, ("I", n, m))
                pe.wait_ge(halo_ready, n + 1)
                if n == 0 and m == 0:
                    pe.wait_ge(diag_ready, CT * KC + CT)
                for k in range(KC):
                    last = mm(o, dg[:, m, k, :], xr3[:, m, k:k + T], start=k == 0, stop=k == KC - 1)
                return last

            def job_X(job, o):
                _, n, _ = job
                for m in range(CT):
                    pe.wait_ge(xi_ready, n * CT + m + 1)
                    last = mm(o[0:DR + 2 * NS, :], wx[:, m, :], xi(n)[:, m, :], start=m == 0, stop=m == CT - 1)
                return last

            def job_XT(job, o):
                _, n, _ = job
                wait_read(pe, ("X", n, 0))
                w = DR + 2 * NS
                for i in range(NT):
                    last = nc.tensor.transpose(o[:, i * w:(i + 1) * w], dbc[:, i * P:(i + 1) * P], ident[0:w, 0:w])
                return last

            def job_D(job, o):
                _, n, m = job
                wait_read(pe, ("X", n, 0))
                return mm(o, wdt[:, m * P:(m + 1) * P], dbc[0:DR, :], start=True, stop=True)

            def skip(o, e, i, m, first):
                mm(o[:, m * P:(m + 1) * P], diagD[:, m, :], xi(e)[:, m, i * P:(i + 1) * P], start=first, stop=False, skip_group_check=True)

            def add_turned(o, m, src, last):
                return mm(o[:, m * P:(m + 1) * P], src, ident, start=False, stop=last, is_transpose=True, skip_group_check=True)

            def job_Y(job, o):
                _, e, i = job
                pe.wait_ge(mac_done, 2 * (NS * (e + 1) - 1) + i // 2 + 1)
                for m in range(CT):
                    skip(o, e, i, m, m == 0)
                for m in range(CT):
                    last = add_turned(o, m, yTd[:, e % 2, i // 2, m * P:(m + 1) * P], True)
                return last

            def job_O(job, o):
                _, e, j = job
                for i in (1, 3):
                    wait_read(pe, ("Y", e, i))
                pe.wait_ge(gated, 2 * (e + 1))
                if e == 0 and j == 0:
                    pe.wait_ge(half_ready, 2)
                for i in range(2):
                    t0 = (2 * j + i) * P
                    for m in range(CT):
                        last = mm(o[:, i * DM:(i + 1) * DM], dx(e)[:, m, t0:t0 + P], wo[:, m, :], start=m == 0, stop=m == CT - 1)
                return last

            def job_R(job, o):
                _, e, j = job
                wait_read(pe, ("O", e, j))
                for k in range(KD):
                    for i in range(2):
                        g = e * NT + 2 * j + i
                        last = nc.tensor.transpose(o[:, (2 * k + i) * P:(2 * k + i + 1) * P], xt[:, g, k * P:(k + 1) * P], ident)
                return last

            def job_A(job, o):
                _, b, h = job
                for j in range(2):
                    wait_read(pe, ("R", b * HALVES + h, j))
                if b == 0:
                    wait_read(pe, ("U", 0, 0))
                for i in range(NT):
                    for k in range(KD):
                        t0 = h * T + i * P
                        last = mm(o[:, i * NH:(i + 1) * NH], x1T[:, k, t0:t0 + P], u[:, k, b * NH:(b + 1) * NH], start=k == 0, stop=k == KD - 1)
                return last

            def heads_by_rows(o, w, first, tiles):
                for i in range(tiles):
                    last = mm(o[0:NH, 0:DM], w[:, i, :], xt[:, first + i, :], start=i == 0, stop=i == tiles - 1)
                return last

            def features_up(o, src):
                for k in range(KD):
                    last = nc.tensor.transpose(o[:, k * NH:(k + 1) * NH], src[:, k * P:(k + 1) * P], ident[0:NH, 0:NH])
                return last

            def rows_by_heads(b, o, w):
                for k in range(KD):
                    for i in range(GB):
                        last = mm(o[:, k * NH:(k + 1) * NH], xt[:, b * GB + i, k * P:(k + 1) * P], w[:, i, :], start=i == 0, stop=i == GB - 1)
                return last

            def weight_by_heads(o, w, src):
                for m in range(KD):
                    for k in range(KD):
                        last = mm(o[:, m * NH:(m + 1) * NH], aw[:, w, k, m * P:(m + 1) * P], src[:, k, :], start=k == 0, stop=k == KD - 1)
                return last

            def job_G(job, o):
                _, b, h = job
                wait_read(pe, ("A", b, h))
                return heads_by_rows(o, a_sb[:, h * NT:(h + 1) * NT, :], b * GB + h * NT, NT)

            def job_GT(job, o):
                wait_read(pe, ("G", job[1], 1))
                return features_up(o, g_row)

            def job_M(job, o):
                wait_read(pe, ("GT", job[1], 0))
                return weight_by_heads(o, 1, g_sb)

            def job_RR(job, o):
                wait_read(pe, ("M", job[1], 0))
                return weight_by_heads(o, 2, qD)

            def scores(job, o, j):
                wait_read(pe, ("RR", job[1], 0))
                for k in range(KD):
                    last = mm(o[0:NH, :], r_sb[:, k, :], x1T[:, k, j * 512:(j + 1) * 512], start=k == 0, stop=k == KD - 1)
                return last

            def job_S0(job, o):
                return scores(job, o, 0)

            def job_S1(job, o):
                return scores(job, o, 1)

            def job_PT(job, o):
                pe.wait_ge(p_ready, job[1] + 1)
                for i in range(GB):
                    last = nc.tensor.transpose(o[:, i * NH:(i + 1) * NH], sm[:, i * P:(i + 1) * P], ident[0:NH, 0:NH])
                return last

            def job_YV(job, o):
                wait_read(pe, ("PT", job[1], 0))
                return heads_by_rows(o, pT, job[1] * GB, GB)

            def job_YT(job, o):
                wait_read(pe, ("YV", job[1], 0))
                return features_up(o, y_row)

            def job_VV(job, o):
                wait_read(pe, ("YT", job[1], 0))
                return weight_by_heads(o, 3, yv)

            def job_WO(job, o):
                wait_read(pe, ("VV", job[1], 0))
                for m in range(KD):
                    for k in range(KD):
                        last = mm(o[:, m:m + 1], aw[:, 4, k, m * P:(m + 1) * P], ov[:, k:k + 1], start=k == 0, stop=k == KD - 1)
                return last

            def ffn(o, w, src, at, ins):
                for k in range(ins):
                    last = mm(o[0:B, 0:w.shape[2] if at is None else 512], src[:, k, :], w[:, k, :] if at is None else w[:, k, at * 512:(at + 1) * 512],
                              start=k == 0, stop=k == ins - 1)
                return last

            def turned_back(o, row, at):
                for m in range(KH):
                    last = nc.tensor.transpose(o[:, at + m * B:at + (m + 1) * B], row[:, m * P:(m + 1) * P], ident[0:B, 0:B])
                return last

            def job_W1(job, o):
                if job[1] == 0:
                    wait_read(pe, ("WO", 0, 0))
                    wait_read(pe, ("WO", 1, 0))
                    pe.wait_ge(s_ff1, 16)
                return ffn(o, W1, z_sb, job[1], KD)

            def job_W2(job, o):
                if job[1] == 0:
                    pe.wait_ge(s_ff2, 16)
                return ffn(o, W2, z_sb, job[1], KD)

            def job_WT(job, o):
                for name in ("W1", "W2"):
                    for half in range(2):
                        wait_read(pe, (name, half, 0))
                turned_back(o, row1, 0)
                return turned_back(o, row2, KH * B)

            def job_FL(job, o):
                pe.wait_ge(flag_row, 1)
                return nc.tensor.transpose(o[0:1, 0:P], flag[:, 0:1], ident)

            def job_H(job, o):
                _, layer, half = job
                pe.wait_ge(f_h, layer)
                pe.wait_ge(s_ffh1 if layer == 1 else s_ffh2, 16)
                return ffn(o, H1 if layer == 1 else H2, ff[:, layer - 1, :, :], half, KH)

            def job_HT(job, o):
                for half in range(2):
                    wait_read(pe, ("H", job[1], half))
                return turned_back(o, row1, 0)

            def job_W3(job, o):
                pe.wait_ge(f_h, 3)
                pe.wait_ge(s_ff3, 32)
                return ffn(o, W3, ff[:, 0, :, :], None, KH)

            def job_FB(job, o):
                wait_read(pe, ("W3", 0, 0))
                return mm(o[:, 0:DM], ident[0:B, job[1]:job[1] + 1].to_broadcast([B, P]), row3, start=True, stop=True)

            jobs = dict(F=job_F, TP=job_TP, U=job_U, T=job_T, I=job_I, Z=job_Z, V=job_V, X=job_X, XT=job_XT, D=job_D, Y=job_Y,
                        O=job_O, R=job_R, A=job_A, G=job_G, GT=job_GT, M=job_M, RR=job_RR, S0=job_S0, S1=job_S1, PT=job_PT, YV=job_YV, YT=job_YT,
                        VV=job_VV, WO=job_WO, W1=job_W1, W2=job_W2, WT=job_WT, FL=job_FL, H=job_H, HT=job_HT, W3=job_W3, FB=job_FB)

            def keep_warm(products):
                for _ in range(products):
                    mm(dA[:, 0, 0:P], ident, ident, start=True, stop=True)

            def run(job):
                q = INDEX[job]
                if q >= 2:
                    pe.wait_ge(job_free[q % 2], q // 2)
                jobs[job[0]](job, bank(job)).then_inc(job_full, 1)

            def transposes(n, i):
                if i == 0:
                    pe.wait_ge(scan_done, CT * (n + 1))
                e = 2 * n + i // 2
                if e >= 1:
                    pe.wait_ge(mac_done if i % 2 else mul_done, e)
                for m in range(CT):
                    last = nc.tensor.transpose(hT[:, i % 2, m * P:(m + 1) * P], hb[:, n % 3, m, i * P:(i + 1) * P], ident)
                last.then_inc(hT_ready, 1)

            def reduce(n, i):
                e = 2 * n + i // 2
                s = n % NS
                pe.wait_ge(mul_done, e + 1)
                o = yacc[:, i // 2, :]
                if s == 0:
                    c = n // NS
                    if c:
                        pe.wait_ge(gated, 2 * (c - 1) + i // 2 + 1)
                    for m in range(CT):
                        skip(o, c, i, m, m == 0)
                for m in range(CT):
                    last = add_turned(o, m, hc[:, e % 2, m * P:(m + 1) * P], s == NS - 1)
                last.then_inc(red_done, 1)

            run(("F", 0, 0))
            for b in range(B):
                pe.wait_ge(ss_act, 4 if b == 0 else 12)
                if b == 0:
                    pe.wait_ge(ss_dve, 4)
                dst = yacc if b == 0 else hT
                for i in range(GB):
                    last = nc.tensor.transpose(dst[:, i // 4, (i % 4) * P:(i % 4 + 1) * P], ss[:, b * GB + i:b * GB + i + 1].to_broadcast([P, P]), ident)
                last.then_inc(mag_pe, 1)
                keep_warm(WARM_HEAD[b])
            for job in HEAD[1:]:
                run(job)
            pe.wait_ge(mag_act, 2)
            for c in range(NCH):
                for s in range(NS):
                    n = c * NS + s
                    if n:
                        transposes(n - 1, 0)
                        transposes(n - 1, 1)
                    for job in BESIDE[2 * n]:
                        run(job)
                    if n:
                        transposes(n - 1, 2)
                        transposes(n - 1, 3)
                        reduce(n - 1, 0)
                        reduce(n - 1, 2)
                    for job in BESIDE[2 * n + 1]:
                        run(job)
            n = NCH * NS
            for i in range(NT):
                transposes(n - 1, i)
            reduce(n - 1, 0)
            reduce(n - 1, 2)
            for job in TAIL:
                run(job)
                keep_warm(WARM.get(job, 0))

            def general_batch(b):
                def did(ins):
                    ins.then_inc(chain, 1)

                for j in range(GB // 2):
                    step(pe, b, f"turn_x{j}")
                    for k in range(KD):
                        for i in range(2):
                            last = nc.tensor.transpose(pp[:, 0, (2 * k + i) * P:(2 * k + i + 1) * P], xt[:, b * GB + 2 * j + i, k * P:(k + 1) * P], ident)
                    did(last)
                step(pe, b, "a")
                for i in range(GB):
                    for k in range(KD):
                        last = mm(pp[:, 0, i * NH:(i + 1) * NH], x1T[:, k, i * P:(i + 1) * P], u[:, k, b * NH:(b + 1) * NH], start=k == 0, stop=k == KD - 1)
                did(last)
                step(pe, b, "g")
                did(rows_by_heads(b, pp[:, 0, :], a_sb))
                step(pe, b, "m")
                did(weight_by_heads(pp[:, 0, :], 1, g_sb))
                step(pe, b, "r")
                did(weight_by_heads(pp[:, 0, :], 2, qD))
                for j in range(2):
                    step(pe, b, f"s{j}")
                    for k in range(KD):
                        last = mm(pp[0:NH, 0, :], r_sb[:, k, :], x1T[:, k, j * 512:(j + 1) * 512], start=k == 0, stop=k == KD - 1)
                    did(last)
                for j in range(GB // 2):
                    step(pe, b, f"v{j}")
                    for i in range(2):
                        for k in range(KD):
                            t0 = (2 * j + i) * P
                            last = mm(pp[:, 0, i * DM:(i + 1) * DM], x1T[:, k, t0:t0 + P], aw[:, 3, k, :], start=k == 0, stop=k == KD - 1)
                    did(last)
                with pe.Fori(0, GB) as t:
                    for h in range(NH):
                        step(pe, b, f"row{h}", t)
                        for j in range(2):
                            last = mm(hT[:, j, :], ident[0:NH, h:h + 1].to_broadcast([NH, P]), sm[:, j * 512:(j + 1) * 512], start=True, stop=True)
                        did(last)
                        step(pe, b, f"turn{h}", t)
                        for i in range(GB):
                            last = nc.tensor.transpose(yacc[:, i // 4, (i % 4) * P:(i % 4 + 1) * P], gsc[:, i * P:(i + 1) * P], ident)
                        did(last)
                        step(pe, b, f"pv{h}", t)
                        for i in range(GB):
                            last = mm(dA[:, 0, h * HE:(h + 1) * HE], gpT[:, i, :], gv[:, i, h * HE:(h + 1) * HE], start=i == 0, stop=i == GB - 1)
                        did(last)
                    step(pe, b, "turn_o", t)
                    for k in range(KD):
                        last = nc.tensor.transpose(pp[:, 0, k * P:(k + 1) * P], go[:, k * P:(k + 1) * P], ident)
                    did(last)

                    def layer(dst, w, src, outs_, ins_):
                        for m in range(outs_):
                            for k in range(ins_):
                                last = mm(dst(m), w[:, k, m * P:(m + 1) * P], src[:, k, :], start=k == 0, stop=k == ins_ - 1)
                        return last

                    def in_hT(m):
                        return hT[:, m // 4, (m % 4) * P:(m % 4 + 1) * P]

                    def in_yacc(m):
                        return yacc[:, m // 4, (m % 4) * P:(m % 4 + 1) * P]

                    def in_pp(m):
                        return pp[:, 0, m * P:(m + 1) * P]

                    step(pe, b, "wo", t)
                    did(layer(in_pp, aw[:, 4, :, :], goT, KD, KD))
                    step(pe, b, "w12", t)
                    layer(in_hT, W1, gz, KH, KD)
                    did(layer(in_yacc, W2, gz, KH, KD))
                    step(pe, b, "h1", t)
                    did(layer(in_hT, H1, gf1, KH, KH))
                    step(pe, b, "h2", t)
                    did(layer(in_hT, H2, gf2, KH, KH))
                    step(pe, b, "w3", t)
                    did(layer(in_pp, W3, gf1, KD, KH))
                    step(pe, b, "turn_f", t)
                    for k in range(KD):
                        last = nc.tensor.transpose(pp[:, 1, k * P:(k + 1) * P], gf3[:, k, :], ident)
                    did(last)

            pe.wait_ge(flag_ready, 1)
            with pe.If(pe.value_load(flag_i[0:1, 0:1], min_val=0, max_val=1)):
                pe.wait_ge(out_done, 16 * 2 * B)
                for b in range(B):
                    general_batch(b)

        @block.scalar
        def _(act):
            A = nc.scalar.activation
            own = Own(act, act_own)

            def exp_ln_table():
                act.preload_act_table_set("natural_log_exp_and_others")

            def ev_U(job, o):
                return A(u[:, :, :], o[:, 0:KD * B * NH].rearrange("p (k j) -> p k j", k=KD), ACT.Copy)

            def ev_T(job, o):
                _, n, k = job
                if n == 1:
                    wait_full(act, ("Z", 0, 3))
                return A(xnT(n)[:, k, :], o, ACT.Copy, scale=v("rms_w")[:, k:k + 1])

            def ev_I(job, o):
                _, n, m = job
                if m == 0:
                    if n % HALVES == 0:
                        if n == 0:
                            act.wait_ge(init_done, 1)
                        else:
                            wait_full(act, ("V", n - 1, 3))
                        A(xr3[:, :, 0:KC - 1], zero[:, :, :], ACT.Copy).then_inc(halo_ready, 1)
                    else:
                        wait_full(act, ("V", n - 1, 3))
                        wait_read(act, ("I", n - 1, 3))
                        wait_read(act, ("I", n - 1, 2))
                        A(xr3[:, :, 0:KC - 1], xr3[:, :, T:T + KC - 1], ACT.Copy).then_inc(halo_ready, 1)
                    act.wait_ge(halo_ready, n + 1)
                return A(xr3[:, m, KC - 1:], o, ACT.Copy)

            def ev_V(job, o):
                _, n, m = job
                if n >= 2:
                    wait_full(act, ("Y", n - 2, 3))
                    act.wait_ge(red_done, 2 * NS * (n - 1))
                if n == 0 and m == 0:
                    act.wait_ge(half_ready, 1)
                A(xi(n)[:, m, :], o, ACT.Identity, bias=half_b[:, m:m + 1], scale=0.5)
                return A(dx(n)[:, m, :], o, ACT.Tanh, bias=half_b[:, m:m + 1], scale=0.5)


            def ev_X(job, o):
                _, n, _ = job
                if n:
                    wait_full(act, ("D", n - 1, 3))
                    act.wait_ge(brow_out, 16 * n)
                return A(dbc[:, :], o[0:DR + 2 * NS, :], ACT.Copy)

            def ev_XT(job, o):
                _, n, _ = job
                if n >= 2:
                    act.wait_ge(mac_done, 2 * NS * (n - 1))
                w = DR + 2 * NS
                return A(CTs[:, n % 2, :, :], o[:, 0:NT * w].rearrange("p (i w) -> p i w", i=NT)[:, :, DR + NS:w], ACT.Copy)

            def ev_Z(job, o):
                _, n, m = job
                if n >= 2:
                    wait_read(act, ("Y", n - 2, 3))
                    wait_read(act, ("Y", n - 2, 1))
                    act.wait_ge(gated, 2 * (n - 1))
                A(gate(n)[:, m, :], o, ACT.Tanh, scale=0.5).then_inc(tanh_ready, 1)
                return None

            def ev_D(job, o):
                _, n, m = job
                if m == 0:
                    if n:
                        wait_full(act, ("Z", n, 3))
                    if n >= 2:
                        wait_full(act, ("O", n - 2, 1))
                A(delta(n)[:, m, :], o, ACT.Abs, bias=v("dt_b")[:, m:m + 1])
                return A(dx(n)[:, m, :], o, ACT.Relu, bias=v("dt_b")[:, m:m + 1])

            def softplus(n, m):
                wait_read(act, ("D", n, m))
                if m == 0:
                    exp_ln_table()
                own.mark(A(delta(n)[:, m, :], delta(n)[:, m, :], ACT.Exp, scale=-1.0))
                own.after()
                A(delta(n)[:, m, :], delta(n)[:, m, :], ACT.Ln, bias=1.0).then_inc(sp_ready, 1)

            def ev_R(job, o):
                _, e, j = job
                if e == HALVES:
                    wait_full(act, ("S1", 0, 0))
                if e == 0 and j == 0:
                    act.wait_ge(ss_dve, 4 + GB + 1)
                t0 = (e % HALVES) * T + 2 * j * P
                return A(x1T[:, :, t0:t0 + 2 * P], o.rearrange("p (k t) -> p k t", k=KD), ACT.Copy)

            def ev_A(job, o):
                h = job[2]
                return A(a_sb[:, h * NT:(h + 1) * NT, :], o[:, 0:NT * NH].rearrange("p (i h) -> p i h", i=NT), ACT.Copy)

            def ev_GT(job, o):
                return A(g_sb[:, :, :], o[:, 0:KD * NH].rearrange("p (k h) -> p k h", k=KD), ACT.Copy)

            def ev_RR(job, o):
                return A(r_sb[:, :, :], o[:, 0:KD * NH].rearrange("p (k h) -> p k h", k=KD), ACT.Copy, scale=HE ** -0.5)

            def softmax(b):
                act.wait_ge(mx_ready, b + 1)
                A(sm[:, :], sm[:, :], ACT.Exp, bias=st[:, 1:2], accum_out=st[:, 2:3]).then_inc(p_ready, 1)

            def ev_PT(job, o):
                return A(pT[:, :, :], o[:, 0:GB * NH].rearrange("p (i h) -> p i h", i=GB), ACT.Copy)

            def ev_YV(job, o):
                act.wait_ge(recip_ready, job[1] + 1)
                return A(y_row, o[0:NH, 0:DM], ACT.Copy, scale=st[:, 3:4])

            def ev_YT(job, o):
                return A(yv[:, :, :], o[:, 0:KD * NH].rearrange("p (k h) -> p k h", k=KD), ACT.Copy)

            def ev_WO(job, o):
                return A(z_sb[:, :, job[1]], o[:, 0:KD], ACT.Copy)

            def ev_W1(job, o):
                return A(row1[:, job[1] * 512:(job[1] + 1) * 512], o[0:B, :], ACT.Copy)

            def ev_W2(job, o):
                return A(row2[:, job[1] * 512:(job[1] + 1) * 512], o[0:B, :], ACT.Copy)

            def ev_H(job, o):
                return A(row1[:, job[2] * 512:(job[2] + 1) * 512], o[0:B, :], ACT.Copy)

            evs = dict(W1=ev_W1, W2=ev_W2, H=ev_H, U=ev_U, T=ev_T, I=ev_I, V=ev_V, X=ev_X, XT=ev_XT, Z=ev_Z, D=ev_D, R=ev_R, A=ev_A, GT=ev_GT, RR=ev_RR,
                       PT=ev_PT, YV=ev_YV, YT=ev_YT, WO=ev_WO)

            def after_job(job):
                name, n, i = job
                if name == "D":
                    softplus(n, i)
                if name == "S1":
                    softmax(n)

            def read(job):
                if job[0] in evs:
                    wait_full(act, job)
                    last = evs[job[0]](job, bank(job))
                    if last is not None:
                        last.then_inc(freed(job), 1)
                after_job(job)

            exp_ln_table()
            def square(g):
                if g % NT == 0 or (g < GB and g % NT == 1):
                    act.wait_ge(s_x[g // NT], 16)
                A(hb[:, 0, g % CT, 0:DM], xt[:, g, :], ACT.Square, accum_out=ss[:, g:g + 1]).then_inc(ss_act, 1)
            for i, g in enumerate(range(1, GB, 2)):
                if i:
                    act.wait_ge(ss_act, i)
                square(g)
            wait_read(act, ("F", 0, 0))
            A(fr[:, 1, :], fr[:, 0, :], ACT.Exp, scale=-1.0).then_inc(fe_ready, 1)
            def rstd(b):
                act.wait_ge(ss_act, 4 if b == 0 else 12)
                if b == 0:
                    act.wait_ge(ss_dve, 4)
                    act.wait_ge(init_done, 1)
                gs = slice(b * GB, (b + 1) * GB)
                own.mark(A(lnv[:, gs], ss[:, gs], ACT.Ln, bias=eps[:, :], scale=1.0 / DM))
                own.after()
                A(lnv[:, gs], lnv[:, gs], ACT.Exp, scale=-0.5).then_inc(rstd_ready, 1)
            rstd(0)
            act.wait_ge(s_vec, 32)
            A(Aneg[:, :], v("A_log"), ACT.Exp).then_inc(aexp_ready, 1)
            for g in range(GB, 2 * GB):
                act.wait_ge(ss_act, 4 + g - GB)
                square(g)
            rstd(1)
            act.wait_ge(mag_pe, 2)
            for i in range(2):
                A(magrow[:, i * 512:(i + 1) * 512], hT[:, i, :], ACT.Copy).then_inc(mag_act, 1)
            for job in HEAD:
                read(job)

            def exp_step(n, m):
                c, s = n // NS, n % NS
                i = n * CT + m
                if s == 0:
                    act.wait_ge(delta_ready, CT * c + m + 1)
                if n == 0 and m == 0:
                    act.wait_ge(A_ready, 1)
                if i >= 2:
                    act.wait_ge(scan_done, i - 1)
                A(dA[:, m % 2, :], delta(c)[:, m, :], ACT.Exp, scale=Aneg[:, m * NS + s:m * NS + s + 1]).then_inc(da_ready, 1)

            def mul_step(n, i):
                c, s = n // NS, n % NS
                e = 2 * n + i // 2
                act.wait_ge(hT_ready, NT * n + i + 1)
                if e >= 2:
                    act.wait_ge(red_done, e - 1)
                A(hc[:, e % 2, :], hT[:, 0, :], ACT.Copy, scale=CTs[:, c % 2, i, s:s + 1]).then_inc(mul_done, 1)

            def carry_step(n):
                c, s = n // NS, n % NS
                if c % HALVES == 0:
                    act.wait_ge(scan_done, CT * (n + 1))
                    A(carry[:, s, :], hb[:, n % 3, :, T - 1], ACT.Copy).then_inc(carry_done, 1)

            for c in range(NCH):
                for s in range(NS):
                    n = c * NS + s
                    exp_step(n, 0)
                    exp_step(n, 1)
                    if n:
                        mul_step(n - 1, 0)
                    for job in to_read(2 * n):
                        read(job)
                    exp_step(n, 2)
                    exp_step(n, 3)
                    if n:
                        mul_step(n - 1, 2)
                        carry_step(n - 1)
                    for job in to_read(2 * n + 1):
                        read(job)
            n = NCH * NS
            mul_step(n - 1, 0)
            mul_step(n - 1, 2)
            for job in BESIDE[-1] + TAIL:
                read(job)
                if job[0] == "WO":
                    act.preload_act_table(ACT.Silu)
                if job[0] == "WT":
                    act.wait_ge(f_scaled, 1)
                    A(ff[:, 2, :, :], ff[:, 2, :, :], ACT.Silu).then_inc(f_silu, 1)
                    act.preload_act_table(ACT.Gelu)
                if job[0] == "HT":
                    wait_read(act, job)
                    A(ff[:, job[1] % 2, :, :], ff[:, 2, :, :], ACT.Gelu).then_inc(f_h, 1)

            def general_batch(b):
                def did(ins):
                    ins.then_inc(chain, 1)

                for j in range(GB // 2):
                    step(act, b, f"turn_x_out{j}")
                    did(A(x1T[:, :, 2 * j * P:2 * (j + 1) * P], pp[:, 0, :].rearrange("p (k t) -> p k t", k=KD), ACT.Copy))
                step(act, b, "a_out")
                did(A(a_sb[:, :, :], pp[:, 0, 0:GB * NH].rearrange("p (i h) -> p i h", i=GB), ACT.Copy))
                step(act, b, "g_out")
                did(ev_GT(None, pp[:, 0, :]))
                step(act, b, "r_out")
                did(ev_RR(None, pp[:, 0, :]))
                for j in range(2):
                    step(act, b, f"s{j}_out")
                    did(A(sm[:, j * 512:(j + 1) * 512], pp[0:NH, 0, :], ACT.Copy))
                for j in range(GB // 2):
                    step(act, b, f"v_out{j}")
                    did(A(gv[:, 2 * j:2 * j + 2, :], pp[:, 0, :].rearrange("p (i o) -> p i o", i=2), ACT.Copy))
                with act.Fori(0, GB) as t:
                    for h in range(NH):
                        step(act, b, f"exp{h}", t)
                        did(A(gsc, gsc, ACT.Exp, bias=gst[:, 1:2], accum_out=gst[:, 2:3]))
                        step(act, b, f"turn_out{h}", t)
                        did(A(gpT, yacc[:, :, :].rearrange("p a (i t) -> p (a i) t", i=4), ACT.Copy))
                    step(act, b, "turn_o_out", t)
                    did(A(goT, pp[:, 0, 0:DM].rearrange("p (k t) -> p k t", k=KD), ACT.Copy))
                    step(act, b, "wo_out", t)
                    did(A(gz, pp[:, 0, 0:DM].rearrange("p (k t) -> p k t", k=KD), ACT.Copy))
                    step(act, b, "silu", t)
                    did(A(gf1, gf1, ACT.Silu))
                    step(act, b, "gelu1", t)
                    did(A(gf2, gf2, ACT.Gelu))
                    step(act, b, "gelu2", t)
                    did(A(gf1, gf1, ACT.Gelu))

            act.wait_ge(flag_ready, 1)
            with act.If(act.value_load(flag_i[0:1, 0:1], min_val=0, max_val=1)):
                for b in range(B):
                    general_batch(b)

        @block.gpsimd
        def _(pool):
            nc.gpsimd.memset(eps[:, :], EPS)
            nc.gpsimd.memset(zero[:, :, :], 0.0).then_inc(init_done, 1)
            pool.wait_ge(s_vec, 32)
            nc.gpsimd.tensor_scalar(half_b[:, :], v("conv_b"), 0.5, 1.0, ALU.mult, ALU.mult).then_inc(half_ready, 1)
            for m in range(CT):
                for k in range(KC):
                    nc.gpsimd.tensor_scalar(dg[:, m, k, :], ident, v("conv_w")[:, m * KC + k:m * KC + k + 1], 1.0, ALU.mult, ALU.mult).then_inc(diag_ready, 1)
            for m in range(CT):
                nc.gpsimd.tensor_scalar(diagD[:, m, :], ident, v("D")[:, m:m + 1], 1.0, ALU.mult, ALU.mult).then_inc(diag_ready, 1)

            pool.wait_ge(s_aw, 16 * 7)
            nc.gpsimd.tensor_scalar(wo[:, :, :], wo[:, :, :], 0.5, 1.0, ALU.mult, ALU.mult).then_inc(half_ready, 1)

            def input_step(n, pair):
                c, s = n // NS, n % NS
                piece = n // BROWS
                row = (piece % BSLOTS) * BROWS + s % BROWS
                if s % BROWS == 0 and pair == 0:
                    pool.wait_ge(bb_in[piece % BSLOTS], 16 * (piece // BSLOTS + 1))
                if s == 0:
                    pool.wait_ge(dx_ready, 2 * c + pair + 1)
                if n >= 3:
                    pool.wait_ge(hT_ready, NT * (n - 2))
                    if (n - 3) // NS % HALVES == 0:
                        done = (n - 3) // NS // HALVES * NS + (n - 3) % NS + 1
                        pool.wait_ge(carry_done, done)
                ms = slice(2 * pair, 2 * pair + 2)
                nc.gpsimd.tensor_tensor(hb[:, n % 3, ms, :], dx(c)[:, ms, :], Bb[:, row:row + 1, :].to_broadcast([P, 2, T]), ALU.mult).then_inc(bx_ready, 1)

            def dx_step(c, pair):
                pool.wait_ge(delta_ready, CT * c + 2 * pair + 2)
                pool.wait_ge(xi_ready, CT * c + 2 * pair + 2)
                ms = slice(2 * pair, 2 * pair + 2)
                nc.gpsimd.tensor_tensor(dx(c)[:, ms, :], delta(c)[:, ms, :], xi(c)[:, ms, :], ALU.mult).then_inc(dx_ready, 1)

            dx_step(0, 0)
            dx_step(0, 1)
            for c in range(NCH):
                for s in range(NS):
                    n = c * NS + s
                    input_step(n, 0)
                    input_step(n, 1)
                    if s in DXS and c + 1 < NCH:
                        dx_step(c + 1, DXS.index(s))

        @block.vector
        def _(dve):
            V = nc.vector
            own = Own(dve, dve_own)

            def rows(c):
                if c >= 2:
                    dve.wait_ge(scan_done, NS * CT * (c - 1))
                for i in range(NT):
                    g = c * NT + i
                    last = V.tensor_scalar(xs(c)[:, i, :], xt[:, g, :], scl[:, g:g + 1], None, ALU.mult)
                last.then_inc(xs_ready, 1)

            def ev_F(job, o):
                return V.tensor_scalar(fr[:, 0, :], o[:, 0:B], v("score_b"), None, ALU.add)

            def ev_TP(job, o):
                tp = o[:, 0:KD * B].rearrange("p (m b) -> p m b", m=KD)
                return V.tensor_tensor(tpD[:, :, :, :], bm[:, :, None, :].to_broadcast([P, KD, B, NH]), tp[:, :, :, None].to_broadcast([P, KD, B, NH]), ALU.mult)

            def gate_tile(e, i, o):
                for m in (CT - 2, CT - 1):
                    wait_read(dve, ("Z", e, m))
                t0 = slice(i * P, (i + 1) * P)
                return V.tensor_tensor(dx(e)[:, :, t0], o.rearrange("p (m t) -> p m t", m=CT), gate(e)[:, :, t0], ALU.mult)

            def gate_even(e):
                for i in (0, 2):
                    dve.wait_ge(red_done, 2 * (NS * (e + 1) - 1) + i // 2 + 1)
                    gate_tile(e, i, yacc[:, i // 2, :]).then_inc(gated, 1)

            def ev_V(job, o):
                _, n, m = job
                wait_read(dve, job)
                V.scalar_tensor_tensor(xi(n)[:, m, :], dx(n)[:, m, :], 1.0, xi(n)[:, m, :], ALU.add, ALU.mult).then_inc(xi_ready, 1)
                return None

            def ev_Z(job, o):
                _, n, m = job
                dve.wait_ge(tanh_ready, CT * n + m + 1)
                return V.scalar_tensor_tensor(gate(n)[:, m, :], gate(n)[:, m, :], 1.0, o, ALU.add, ALU.mult)

            def ev_D(job, o):
                _, n, m = job
                dve.wait_ge(sp_ready, CT * n + m + 1)
                V.tensor_tensor(delta(n)[:, m, :], delta(n)[:, m, :], dx(n)[:, m, :], ALU.add).then_inc(delta_ready, 1)
                return None

            def ev_Y(job, o):
                return gate_tile(job[1], job[2], o)

            def ev_O(job, o):
                _, e, j = job
                for i in range(2):
                    g = e * NT + 2 * j + i
                    last = V.scalar_tensor_tensor(xt[:, g, :], xt[:, g, :], keep1[:, g:g + 1], o[:, i * DM:(i + 1) * DM], ALU.mult, ALU.add)
                return last

            def ev_G(job, o):
                _, b, h = job
                if h == 0:
                    return V.tensor_copy(g_row, o[0:NH, 0:DM])
                wait_read(dve, ("G", b, 0))
                return V.tensor_tensor(g_row, g_row, o[0:NH, 0:DM], ALU.add)

            def ev_M(job, o):
                return V.tensor_tensor(qD[:, :, :], o[:, 0:KD * NH].rearrange("p (m h) -> p m h", m=KD), bm, ALU.mult)

            def ev_S0(job, o):
                if job[1]:
                    wait_full(dve, ("GT", 1, 0))
                return V.tensor_tensor(sm[:, 0:512], o[0:NH, :], negm[:, 0:512], ALU.add)

            def ev_S1(job, o):
                return V.tensor_tensor(sm[:, 512:1024], o[0:NH, :], negm[:, 512:1024], ALU.add)

            def softmax(b):
                wait_read(dve, ("S1", b, 0))
                own.mark(V.reduce_max(st[:, 0:1], sm[:, 512:1024], AX.X))
                own.after()
                own.mark(V.tensor_tensor(st[:, 0:1], st[:, 0:1], st[:, 4:5], ALU.max))
                own.after()
                V.tensor_scalar(st[:, 1:2], st[:, 0:1], -1.0, None, ALU.mult).then_inc(mx_ready, 1)
                dve.wait_ge(p_ready, b + 1)
                V.reciprocal(st[:, 3:4], st[:, 2:3]).then_inc(recip_ready, 1)

            def ev_VV(job, o):
                own.mark(V.tensor_tensor(ovj[:, :, :], o[:, 0:KD * NH].rearrange("p (m h) -> p m h", m=KD), bm, ALU.mult))
                own.after()
                return V.reduce_sum(ov[:, :], ovj[:, :, :], AX.X)

            def scaled(dst, o, name, n):
                return V.tensor_tensor(dst, o.rearrange("p (m b) -> p m b", b=B), v(name)[:, :, None].to_broadcast([P, n, B]), ALU.mult)

            def ev_WT(job, o):
                w = KH * B
                scaled(ff[:, 2, :, :], o[:, 0:w], "w1_s", KH).then_inc(f_scaled, 1)
                scaled(ff[:, 3, :, :], o[:, w:2 * w], "w2_s", KH).then_inc(freed(job), 1)
                dve.wait_ge(f_silu, 1)
                wait_read(dve, job)
                V.tensor_tensor(ff[:, 0, :, :], ff[:, 2, :, :], ff[:, 3, :, :], ALU.mult).then_inc(f_h, 1)
                return None

            def ev_HT(job, o):
                i = job[1]
                dve.wait_ge(f_h, i)
                return scaled(ff[:, 2, :, :], o[:, 0:KH * B], "h1_s" if i == 1 else "h2_s", KH)

            def ev_W3(job, o):
                return V.tensor_tensor(row3, o[0:B, 0:DM], w3_row[:, :], ALU.mult)

            def ev_FB(job, o):
                b = job[1]
                for j in range(2):
                    g = b * GB + j * NT
                    V.tensor_tensor(outs[:, b, j * NT:(j + 1) * NT, :], xt[:, g:g + NT, :], o[:, None, 0:DM].to_broadcast([P, NT, DM]), ALU.add).then_inc(out_ready, 1)
                return None

            def compare_rows():
                dve.wait_ge(mask_in, 32)
                m3 = mask_w.rearrange("p (g w) -> p g w", g=GB)
                own.mark(V.tensor_tensor(m3, m3, mask_0[:, None, :].to_broadcast([P, GB, S // 4]), ALU.bitwise_xor))
                own.after()
                V.reduce_max(flag[:, 0:1], mask_w, AX.X).then_inc(flag_row, 1)

            def ev_FL(job, o):
                own.mark(V.reduce_max(flag[0:1, 1:2], o[0:1, 0:P], AX.X))
                own.after()
                own.mark(V.tensor_scalar(flag[0:1, 1:2], flag[0:1, 1:2], 1.0, None, ALU.min))
                own.after()
                return V.tensor_copy(flag_i[:, :], flag[0:1, 1:2])

            evs = dict(F=ev_F, TP=ev_TP, V=ev_V, D=ev_D, G=ev_G, Z=ev_Z, Y=ev_Y, O=ev_O, M=ev_M, S0=ev_S0, S1=ev_S1, VV=ev_VV, WT=ev_WT, HT=ev_HT, W3=ev_W3, FB=ev_FB, FL=ev_FL)

            def read(job):
                if job[0] in evs:
                    wait_full(dve, job)
                    last = evs[job[0]](job, bank(job))
                    if last is not None:
                        last.then_inc(freed(job), 1)
                if job[0] == "S0":
                    wait_read(dve, job)
                    own.mark(V.reduce_max(st[:, 4:5], sm[:, 0:512], AX.X))
                if job[0] == "S1":
                    softmax(job[1])
                if job == ("VV", 1, 0):
                    compare_rows()

            for i, g in enumerate(range(0, GB, 2)):
                if g % NT == 0:
                    dve.wait_ge(s_x[g // NT], 16)
                V.tensor_tensor_reduce(out=hb[:, 1, i, 0:DM], in0=xt[:, g, :], in1=xt[:, g, :], scale=1.0, scalar=0.0, op0=ALU.mult, op1=ALU.add,
                                       accum_out=ss[:, g:g + 1]).then_inc(ss_dve, 1)
            read(("F", 0, 0))
            dve.wait_ge(fe_ready, 1)
            own.mark(V.tensor_scalar(fr[:, 2, :], fr[:, 1, :], 1.0, None, ALU.add))
            own.after()
            own.mark(V.reciprocal(fr[:, 1, :], fr[:, 2, :]))
            own.after()
            frac = own.mark(V.tensor_scalar(fr[:, 2, :], fr[:, 1, :], float(S), 1.0, ALU.mult, ALU.max))

            def count(g, rows_, scratch):
                return V.tensor_scalar(scratch, rows_, ss[:, g:g + 1], None, ALU.is_gt, ALU.add, accum_out=cnt[:, g:g + 1])

            def kept(gs, b):
                own.mark(V.tensor_scalar(keep[:, gs], cnt[:, gs], 1.0, fr[:, 2, b:b + 1], ALU.add, ALU.is_le))
                own.after()
                V.tensor_scalar(keep1[:, gs], keep[:, gs], 1.0, None, ALU.add)
                own.mark(V.tensor_tensor(scl[:, gs], keep[:, gs], lnv[:, gs], ALU.mult))
                own.after()

            dve.wait_ge(mag_pe, 1)
            dve.wait_ge(ss_act, 4)
            rows0 = yacc[:, :, :].rearrange("p a b -> p (a b)")
            for g in range(NT):
                if g:
                    own.after()
                own.mark(count(g, rows0, junk[:, 0:S]))
            dve.wait_ge(rstd_ready, 1)
            own.after()
            kept(slice(0, NT), 0)
            rows(0)
            for g in range(NT, GB):
                own.after()
                own.mark(count(g, rows0, junk[:, 0:S]))
            own.after()
            kept(slice(NT, GB), 0)
            dve.wait_ge(aexp_ready, 1)
            V.tensor_scalar(Aneg[:, :], Aneg[:, :], -1.0, None, ALU.mult).then_inc(A_ready, 1)
            read(("TP", 0, 0))
            dve.wait_ge(s_mrow, 16)
            V.tensor_scalar(negm[:, :], mrow, -1.0, FLT_MAX, ALU.add, ALU.mult)
            dve.wait_ge(ss_act, 12)
            dve.wait_ge(mag_act, 2)
            for g in range(GB, 2 * GB):
                own.after()
                own.mark(count(g, magrow, junk[:, 0:S]))
            dve.wait_ge(rstd_ready, 2)
            own.after()
            kept(slice(GB, 2 * GB), 1)
            V.tensor_copy(fr[:, 3, :], cnt[:, 14:16]).then_inc(ss_dve, GB + 1)

            def scan_step(n, m):
                c, s = n // NS, n % NS
                i = n * CT + m
                dve.wait_ge(da_ready, i + 1)
                if m % 2 == 0:
                    dve.wait_ge(bx_ready, 2 * n + m // 2 + 1)
                if c % HALVES:
                    if m == 0:
                        dve.wait_ge(carry_done, c // HALVES * NS + s + 1)
                    start = carry[:, s, m:m + 1]
                else:
                    start = 0.0
                V.tensor_tensor_scan(hb[:, n % 3, m, :], dA[:, m % 2, :], hb[:, n % 3, m, :], start, ALU.mult, ALU.add).then_inc(scan_done, 1)

            def mac_step(n, i):
                c, s = n // NS, n % NS
                e = 2 * n + i // 2
                dve.wait_ge(hT_ready, NT * n + i + 1)
                dst = yTd[:, c % 2, i // 2, :]
                src, cs = hT[:, 1, :], CTs[:, c % 2, i, s:s + 1]
                if s == 0:
                    if c >= 2 and i == 1:
                        wait_full(dve, ("Y", c - 2, 3))
                    V.tensor_scalar(dst, src, cs, None, ALU.mult).then_inc(mac_done, 1)
                else:
                    dve.wait_ge(mac_done, e - 1)
                    V.scalar_tensor_tensor(dst, src, cs, dst, ALU.mult, ALU.add).then_inc(mac_done, 1)

            for m in range(CT):
                read(("V", 0, m))
            for m in range(CT):
                read(("D", 0, m))
            for c in range(NCH):
                for s in range(NS):
                    n = c * NS + s
                    scan_step(n, 0)
                    scan_step(n, 1)
                    if n:
                        mac_step(n - 1, 1)
                    for job in to_read(2 * n):
                        read(job)
                    scan_step(n, 2)
                    scan_step(n, 3)
                    if n:
                        mac_step(n - 1, 3)
                    if s == 0:
                        if c:
                            gate_even(c - 1)
                        if c + 1 < NCH:
                            rows(c + 1)
                    for job in to_read(2 * n + 1):
                        read(job)
            n = NCH * NS
            mac_step(n - 1, 1)
            mac_step(n - 1, 3)
            gate_even(NCH - 1)
            for job in BESIDE[-1] + TAIL:
                read(job)

            def general_batch(b):
                def did(ins):
                    ins.then_inc(chain, 1)

                step(dve, b, "m_out")
                did(ev_M(None, pp[:, 0, :]))
                with dve.Fori(0, GB) as t:
                    step(dve, b, "mask", t)
                    dve.wait_ge(gmask_in, (t + (b * GB + 1)) * 16)
                    did(V.tensor_scalar(gadd, gmask, -1.0, FLT_MAX, ALU.add, ALU.mult))
                    for h in range(NH):
                        step(dve, b, f"add{h}", t)
                        did(V.tensor_tensor(gsc, hT[:, :, :].rearrange("p a s -> p (a s)"), gadd, ALU.add))
                        step(dve, b, f"max{h}", t)
                        did(V.reduce_max(gst[:, 0:1], gsc, AX.X))
                        step(dve, b, f"neg{h}", t)
                        did(V.tensor_scalar(gst[:, 1:2], gst[:, 0:1], -1.0, None, ALU.mult))
                        step(dve, b, f"recip{h}", t)
                        did(V.reciprocal(gst[:, 3:4], gst[:, 2:3]))
                        step(dve, b, f"norm{h}", t)
                        did(V.tensor_scalar(gsc, gsc, gst[:, 3:4], None, ALU.mult))
                    step(dve, b, "o_out", t)
                    did(V.tensor_copy(go, dA[:, 0, 0:DM]))

                    def by_row(dst, src, name, n):
                        return V.tensor_tensor(dst, src, v(name)[:, :, None].to_broadcast([P, n, P]), ALU.mult)

                    hT3 = hT[:, :, :].rearrange("p a (m t) -> p (a m) t", m=4)
                    yacc3 = yacc[:, :, :].rearrange("p a (m t) -> p (a m) t", m=4)
                    step(dve, b, "w1_out", t)
                    did(by_row(gf1, hT3, "w1_s", KH))
                    step(dve, b, "w2_out", t)
                    did(by_row(gf2, yacc3, "w2_s", KH))
                    step(dve, b, "gated", t)
                    did(V.tensor_tensor(gf1, gf1, gf2, ALU.mult))
                    step(dve, b, "h1_out", t)
                    did(by_row(gf2, hT3, "h1_s", KH))
                    step(dve, b, "h2_out", t)
                    did(by_row(gf1, hT3, "h2_s", KH))
                    step(dve, b, "w3_out", t)
                    did(by_row(gf3, pp[:, 0, 0:DM].rearrange("p (k t) -> p k t", k=KD), "w3_s", KD))
                    step(dve, b, "sum", t)
                    x1 = xt[:, bass.ds(t + b * GB, 1), :].rearrange("p a d -> p (a d)")
                    did(V.tensor_tensor(gout, x1, pp[:, 1, 0:DM], ALU.add))

            wait_read(dve, ("FL", 0, 0))
            V.tensor_copy(flag[0:1, 0:1], flag_i[:, :]).then_inc(flag_ready, 1)
            with dve.If(dve.value_load(flag_i[0:1, 0:1], min_val=0, max_val=1)):
                for b in range(B):
                    general_batch(b)


_OUT = [B, S, DM]


def layout(i):
    def parts(name, a):
        a = np.asarray(a)
        n = a.shape[0] // P
        return a.reshape((n, P) + a.shape[1:]).swapaxes(0, 1).reshape(P, -1)

    cols = {
        "rms_w": i["L0_attn_rms_w"], "conv_w": i["L0_attn_conv_w"], "conv_b": i["L0_attn_conv_b"], "dt_b": i["L0_attn_dt_b"],
        "A_log": i["L0_attn_A_log"], "D": i["L0_attn_D"], "score_w": i["L0_cond_score_w"],
        "cond": np.asarray(i["cond_1024"]).T, "w1_s": i["L0_ffn_w1_s"], "w2_s": i["L0_ffn_w2_s"],
        "h1_s": i["L0_ffn_h1_s"], "h2_s": i["L0_ffn_h2_s"], "w3_s": i["L0_ffn_w3_s"],
    }
    packed = [np.broadcast_to(np.asarray(i["L0_cond_score_b"]).reshape(1, 1), (P, 1)) if n == "score_b" else parts(n, cols[n]) for n in VEC]
    eye = np.eye(P, dtype=np.float32)
    heads = (np.arange(DM)[:, None] // HE == np.arange(NH)[None, :]).astype(np.float32)
    return [
        np.asarray(i["x"]).reshape(B * S, DM), np.asarray(i["L0_attn_in_proj"]), np.asarray(i["L0_attn_out_proj"]),
        np.asarray(i["L0_attn_x_proj"]), np.asarray(i["L0_attn_dt_w"]), np.asarray(i["L0_cond2_Wq"]),
        np.asarray(i["L0_cond2_Wq"]).T, np.asarray(i["L0_cond2_Wk"]), np.asarray(i["L0_cond2_Wv"]).T,
        np.asarray(i["L0_cond2_Wt"]).T, np.asarray(i["L0_cond2_Wo"]).T, np.asarray(i["L0_ffn_w1_w"]).T,
        np.asarray(i["L0_ffn_w2_w"]).T, np.asarray(i["L0_ffn_h1_w"]).T, np.asarray(i["L0_ffn_h2_w"]).T,
        np.asarray(i["L0_ffn_w3_w"]).T, np.asarray(i["mask_SxS_bk0"]), np.asarray(i["L0_ffn_w3_s"]).reshape(1, DM), np.concatenate(packed, axis=1),
        np.concatenate([eye, parts("heads", heads)], axis=1),
    ]


def kernel(**inputs):
    import concourse.bacc as bacc
    from concourse.bass_utils import run_bass_kernel_spmd

    nc = bacc.Bacc("TRN2", target_bir_lowering=False, num_devices=1)
    arrays, args = {}, []
    for n, a in enumerate(layout(inputs)):
        a = np.ascontiguousarray(a)
        arrays[f"in_{n}"] = a
        args.append(nc.dram_tensor(f"in_{n}", a.shape, mybir.dt.from_np(a.dtype), kind="ExternalInput").ap())
    out = nc.dram_tensor("out_0", [B * S, DM], F32, kind="ExternalOutput").ap()
    build(nc, *args, out)
    r = run_bass_kernel_spmd(nc, [arrays], core_ids=[0])
    return r.results[0]["out_0"].reshape(B, S, DM)
```

```python
import numpy as np
import concourse.bass as bass
from concourse import mybir
from concourse.alu_op_type import AluOpType as ALU
from contextlib import ExitStack

F32 = mybir.dt.float32
U8 = mybir.dt.uint8
I32 = mybir.dt.int32
ACT = mybir.ActivationFunctionType
AX = mybir.AxisListType

P = 128
B, S, DM = 2, 1024, 256
DI, NS, DR, KC = 512, 16, 16, 4
NH, HE = 16, 16
HID = 1024
KD = DM // P
CT = DI // P
T = 512
NT = T // P
HALVES = S // T
NCH = B * HALVES
NG = B * S // P
GB = S // P
KH = HID // P
FLT_MAX = float(np.finfo(np.float32).max)
EPS = 1e-5

VEC = {}
_at = 0
for _name, _n in (("rms_w", KD), ("conv_w", CT * KC), ("conv_b", CT), ("dt_b", CT), ("A_log", CT * NS), ("D", CT),
                  ("score_w", KD), ("cond", KD * B), ("score_b", 1), ("w1_s", KH), ("w2_s", KH), ("h1_s", KH),
                  ("h2_s", KH), ("w3_s", KD)):
    VEC[_name] = (_at, _at + _n)
    _at += _n
NVEC = _at

BROWS = 2
BSLOTS = 3
RING = 4
PIECES = NS // BROWS


PROLOGUE = {2: [("T", 0), ("T", 1)], 4: [("I", 0)], 5: [("I", 1)], 6: [("I", 2)], 7: [("I", 3)], 8: [("V", 2)],
            10: [("V", 3)], 14: [("X", 0)], 18: [("XT", 0), ("D", 0)], 20: [("D", 1), ("D", 2)], 21: [("D", 3)],
            22: [("Z", 0)], 23: [("Z", 1)], 24: [("Z", 2)], 25: [("Z", 3)]}
EPILOGUE = {1: [("Y", 1), ("Y", 3)], 11: [("O", 0)], 16: [("O", 1)], 28: [("R", 0)], 30: [("R", 1)]}
LAST_EPILOGUE = {1: [("Y", 1)], 2: [("Y", 3)], 3: [("O", 0)], 5: [("O", 1)], 17: [("R", 0)], 19: [("R", 1)]}
ATT = [6, 8, 8, 10, 12, 14, 15, 16, 17, 20, 22, 23, 24, 27]
ATT1 = [28, 29]
HEAD_CONV = 3
LOOP_CONV = 1
CONV_AT = {"taps0": 6, "taps1": 7, "tanh": 8, "finish": 9}
POOL_TILE = 1
POOL_AT = [4, 5]
POOL_CONV_AT = {"tanh": 12, "finish": 13}


def own_conv(n):
    return LOOP_CONV if n else HEAD_CONV


def convs_done(n):
    return HEAD_CONV + LOOP_CONV * n


def slots(table, n):
    return {h: [(name, n, m) for name, m in jobs] for h, jobs in table.items()}


def prologue_slots(n):
    return slots(PROLOGUE, n)


def epilogue_slots(e):
    return slots(LAST_EPILOGUE if e == NCH - 2 else EPILOGUE, e)


def attention_jobs(b):
    return [("A", b, 0), ("G", b, 0), ("A", b, 1), ("G", b, 1)] + [(name, b, 0) for name in ("GT", "M", "RR", "S0", "S1", "PT", "YV", "YT", "VV", "WO")]


def all_slots():
    head = [("F", 0, 0)]
    head += [("T", 0, k) for k in range(KD)] + [("I", 0, m) for m in range(CT)] + [("V", 0, m) for m in range(HEAD_CONV, CT)]
    head += [("X", 0, 0), ("XT", 0, 0)] + [("D", 0, m) for m in range(CT)]
    beside = [[] for _ in range(2 * NCH * NS)]
    for c in range(NCH):
        at = 2 * c * NS
        if c == 0:
            for m in range(CT):
                beside[m // 2] += [("Z", 0, m)]
            beside[3] += [("TP", 0, 0)]
            beside[5] += [("U", 0, 0)]
        else:
            for h, jobs in epilogue_slots(c - 1).items():
                beside[at + h] += jobs
        if c + 1 < NCH:
            for h, jobs in prologue_slots(c + 1).items():
                beside[at + h] += jobs
    for i, job in enumerate(attention_jobs(0)):
        beside[2 * (NCH - 1) * NS + ATT[i]] += [job]
    for i, job in enumerate(attention_jobs(1)[:2]):
        beside[2 * (NCH - 1) * NS + ATT1[i]] += [job]
    tail = []
    for s, jobs in sorted(epilogue_slots(NCH - 1).items()):
        tail += jobs
    tail += attention_jobs(1)[2:]
    tail += [("W1", 0, 0), ("W1", 1, 0), ("W2", 0, 0), ("W2", 1, 0), ("WT", 0, 0)]
    tail += [("H", 1, 0), ("FL", 0, 0), ("H", 1, 1), ("HT", 1, 0), ("H", 2, 0), ("H", 2, 1), ("HT", 2, 0)]
    tail += [("W3", 0, 0), ("FB", 0, 0), ("FB", 1, 0)]
    return head, beside, tail


BATCH_STEPS = [f"{x}{i}" for i in range(GB // 2) for x in ("turn_x", "turn_x_out")]
BATCH_STEPS += ["a", "a_out", "g", "g_out", "m", "m_out", "r", "r_out", "s0", "s0_out", "s1", "s1_out"]
BATCH_STEPS += [f"{x}{i}" for i in range(GB // 2) for x in ("v", "v_out")]
TILE_STEPS = ["mask"] + [f"{x}{h}" for h in range(NH) for x in ("row", "add", "max", "neg", "exp", "recip", "norm", "turn", "turn_out", "pv")]
TILE_STEPS += ["o_out", "turn_o", "turn_o_out", "wo", "wo_out", "w12", "w1_out", "w2_out", "silu", "gated", "h1", "h1_out", "gelu1",
               "h2", "h2_out", "gelu2", "w3", "w3_out", "turn_f", "sum"]

HEAD, BESIDE, TAIL = all_slots()
ORDER = HEAD + [job for jobs in BESIDE for job in jobs] + TAIL
INDEX = {job: q for q, job in enumerate(ORDER)}


def to_read(h):
    return BESIDE[h - 1] if h else []


WARM = {**{(name, 1, 0): 2 for name in ("GT", "M", "RR", "PT", "YV", "YT", "VV", "WO")}, ("A", 1, 1): 2, ("G", 1, 1): 2,
        ("S1", 1, 0): 12, ("WT", 0, 0): 4}
WARM_HEAD = [18, 6]


def build(nc, x, w_in, w_out, w_x, w_dt, wq, wqT, wk, wvT, wtT, woT, f1, f2, fh1, fh2, f3, mask, w1_s, w2_s, h1_s, h2_s, w3_s, vecs, consts, out):
    ctx = ExitStack()
    with ctx:
        def sb(name, shape, dt=F32):
            return ctx.enter_context(nc.sbuf_tensor(name, shape, dt))

        def sem(name):
            return ctx.enter_context(nc.semaphore(name))

        xt = sb("xt", [P, NG, DM])
        x1T = sb("x1T", [P, KD, S])
        wi = sb("wi", [P, KD * 2 * DI])
        wo = sb("wo", [P, CT, DM])
        wx = sb("wx", [P, CT, DR + 2 * NS])
        wdt = sb("wdt", [DR, DI])
        aw = sb("aw", [P, 5, KD, DM])
        vec = sb("vec", [P, NVEC])
        con = sb("con", [P, P + 2 * NH])
        diag = sb("diag", [P, CT * KC * P])
        diagD = sb("diagD", [P, CT, P])
        xr = sb("xr", [P, CT * (T + KC - 1)])
        par = [sb(f"par{i}", [P, 4, CT * T]) for i in range(2)]
        scanmem = sb("scanmem", [P, BSLOTS * BROWS * T + RING * CT * T])
        hc = sb("hc", [P, 2, T])
        xnT = sb("xnT", [P, KD, T])
        yTd = sb("yTd", [P, 2, 2, DI])
        dbc = sb("dbc", [DR + 2 * NS, T])
        CTs = sb("CTs", [P, 2, NT, NS])
        carry = sb("carry", [P, NS, CT])
        Aneg = sb("Aneg", [P, CT * NS])
        ss = sb("ss", [P, NG])
        cnt = sb("cnt", [P, NG])
        keep = sb("keep", [P, NG])
        keep1 = sb("keep1", [P, NG])
        scl = sb("scl", [P, NG])
        lnv = sb("lnv", [P, NG])
        fr = sb("fr", [P, 3, B])
        eps = sb("eps", [P, 1])
        half_b = sb("half_b", [P, CT])
        half_w = sb("half_w", [P, CT * KC])
        zero = sb("zero", [P, CT, KC - 1])
        tpD = sb("tpD", [P, KD, B, NH])
        u = sb("u", [P, KD, B * NH])
        a_sb = sb("a_sb", [P, GB, NH])
        g_sb = sb("g_sb", [P, KD, NH])
        qD = sb("qD", [P, KD, NH])
        r_sb = sb("r_sb", [P, KD, NH])
        pT = sb("pT", [P, GB, NH])
        yv = sb("yv", [P, KD, NH])
        ov = sb("ov", [P, KD])
        ovj = sb("ovj", [P, KD, NH])
        z_sb = sb("z_sb", [P, KD, B])
        sm = sb("sm", [NH, S])
        st = sb("st", [NH, 5])
        negm = sb("negm", [NH, S])
        ff = sb("ff", [P, 4, KH, B])
        w3_row = sb("w3_row", [B, DM])
        flag = sb("flag", [P, 2])
        flag_i = sb("flag_i", [1, 1], I32)
        gst = sb("gst", [P, 4])

        ident = con[:, 0:P]
        bm = con[:, P:P + 2 * NH].rearrange("p (k h) -> p k h", k=KD)

        def v(name):
            lo, hi = VEC[name]
            return vec[:, lo:hi]

        def xi(n):
            return par[n % 2][:, 0, :].rearrange("p (m t) -> p m t", m=CT)

        def delta(n):
            return par[n % 2][:, 1, :].rearrange("p (m t) -> p m t", m=CT)

        def dx(n):
            return par[n % 2][:, 2, :].rearrange("p (m t) -> p m t", m=CT)

        def gate(n):
            return par[n % 2][:, 3, :].rearrange("p (m t) -> p m t", m=CT)

        def xs(n):
            return par[n % 2][:, 1, 0:NT * DM].rearrange("p (i d) -> p i d", i=NT)

        win = wi[:, :].rearrange("p (k o) -> p k o", k=KD)
        Bb = scanmem[:, 0:BSLOTS * BROWS * T].rearrange("p (r t) -> p r t", t=T)
        hb = scanmem[:, BSLOTS * BROWS * T:].rearrange("p (r m t) -> p r m t", r=RING, m=CT)
        xr3 = xr[:, :].rearrange("p (m t) -> p m t", m=CT)
        dg = diag[:, :].rearrange("p (m k q) -> p m k q", m=CT, k=KC)
        magrow = x1T[:, 0, :]
        junk = yTd[:, 1, :, :].rearrange("p a b -> p (a b)")
        mrow = x1T[0:NH, 1, 0:S // 4].bitcast(U8)
        wt = par[1][:, 3, S:S + KD * DM].rearrange("p (k o) -> p k o", k=KD)
        mask_w = par[1][:, 1, :].bitcast(I32)
        mask_0 = hc[:, 0, 0:S // 4].bitcast(I32)
        outs = par[1][:, 0:3:2, :].rearrange("p a (g d) -> p a g d", d=DM)
        gv = par[1][:, 0, :].rearrange("p (i o) -> p i o", i=GB)
        gadd, gsc = par[1][:, 1, 0:S], par[1][:, 1, S:2 * S]
        gpT = par[1][:, 2, 0:S].rearrange("p (i t) -> p i t", i=GB)
        gmask = par[1][:, 2, S:S + S // 4].bitcast(U8)
        gout = par[1][:, 2, S + S // 2:S + S // 2 + DM]
        gf1 = par[1][:, 3, 0:HID].rearrange("p (m t) -> p m t", m=KH)
        gf2 = par[1][:, 3, HID:2 * HID].rearrange("p (m t) -> p m t", m=KH)
        small = yTd[:, 0, :, :]
        go = small[:, 0, 0:DM]
        goT = small[:, 0, DM:2 * DM].rearrange("p (k t) -> p k t", k=KD)
        gz = small[:, 1, 0:DM].rearrange("p (k t) -> p k t", k=KD)
        gf3 = small[:, 1, DM:2 * DM].rearrange("p (k t) -> p k t", k=KD)
        g_row, y_row = sm[:, 0:DM], sm[:, DM:2 * DM]
        row1, row2, row3 = sm[0:B, :], negm[0:B, :], negm[0:B, 0:DM]
        scale_rows = {"w1": yTd[0:B, 0, :, :].rearrange("p a b -> p (a b)"), "w2": yTd[0:B, 1, :, :].rearrange("p a b -> p (a b)"),
                      "h1": scanmem[0:B, KH * HID:KH * HID + HID], "h2": scanmem[0:B, KH * HID + HID:KH * HID + 2 * HID]}
        W1 = wi[:, :].rearrange("p (k o) -> p k o", k=KD)
        W2 = xr[:, 0:KD * HID].rearrange("p (k o) -> p k o", k=KD)
        W3 = diag[:, :].rearrange("p (k o) -> p k o", k=KH)
        H1 = par[0][:, :, :].rearrange("p a (b o) -> p (a b) o", b=2)
        H2 = scanmem[:, 0:KH * HID].rearrange("p (k o) -> p k o", k=KH)

        dA = ctx.enter_context(nc.psum_tensor("dA", [P, 2, T], F32))
        hT = ctx.enter_context(nc.psum_tensor("hT", [P, 2, DI], F32))
        yacc = ctx.enter_context(nc.psum_tensor("yacc", [P, 2, DI], F32))
        pp = ctx.enter_context(nc.psum_tensor("pp", [P, 2, 512], F32))
        brow = nc.dram_tensor("brow", [NCH, NS, T], F32, kind="Internal").ap()

        s_vec, s_w, s_aw, s_mrow = sem("vec_in"), sem("w_in"), sem("aw_in"), sem("mrow_in")
        s_x = [sem(f"x_in{i}") for i in range(NCH)]
        s_ff1, s_ff2, s_ff3, s_ffh1, s_ffh2 = (sem(f"ff_in{i}") for i in range(5))
        s_scales, mask_in, gmask_in = sem("scales_in"), sem("mask_in"), sem("general_mask_in")
        bb_in = [sem(f"bb_in{i}") for i in range(BSLOTS)]
        brow_out, out_done, gout_done = sem("brow_out"), sem("out_done"), sem("general_out_done")
        job_full = sem("job_full")
        job_free = [sem("job_free0"), sem("job_free1")]
        da_ready, bx_ready, scan_done = sem("da_ready"), sem("bx_ready"), sem("scan_done")
        hT_ready, mul_done, red_done, mac_done = sem("hT_ready"), sem("mul_done"), sem("red_done"), sem("mac_done")
        carry_done, gated = sem("carry_done"), sem("gated")
        xs_ready, halo_ready, xi_ready = sem("xs_ready"), sem("halo_ready"), sem("xi_ready")
        half_ready, diag_ready = sem("half_ready"), sem("diag_ready")
        conv_ready, conv_tanh_ready = sem("conv_ready"), sem("conv_tanh_ready")
        pool_conv_ready, pool_tanh_ready = sem("pool_conv_ready"), sem("pool_tanh_ready")
        tanh_ready, abs_ready, sp_ready = sem("tanh_ready"), sem("abs_ready"), sem("sp_ready")
        delta_ready, dx_ready = sem("delta_ready"), sem("dx_ready")
        ss_dve, ss_act, mag_pe, mag_act, ranked = sem("ss_dve"), sem("ss_act"), sem("mag_pe"), sem("mag_act"), sem("ranked")
        aexp_ready, A_ready, rstd_ready, fe_ready, init_done = (sem(x) for x in ("aexp_ready", "A_ready", "rstd_ready", "fe_ready", "init_done"))
        dve_own, act_own, pool_own = sem("dve_own"), sem("act_own"), sem("pool_own")
        mx_ready, p_ready, recip_ready = sem("mx_ready"), sem("p_ready"), sem("recip_ready")
        silu_ready, out_ready = sem("silu_ready"), sem("out_ready")
        flag_row, flag_ready = sem("flag_row"), sem("flag_ready")
        chain = sem("general_chain")

        block = ctx.enter_context(nc.Block())

        def wait_full(eng, job):
            eng.wait_ge(job_full, INDEX[job] + 1)

        def wait_read(eng, job):
            q = INDEX[job]
            eng.wait_ge(job_free[q % 2], q // 2 + 1)

        def bank(job):
            return pp[:, INDEX[job] % 2, :]

        def freed(job):
            return job_free[INDEX[job] % 2]

        def batch_base(b):
            return b * (len(BATCH_STEPS) + GB * len(TILE_STEPS))

        def step(eng, b, name, i=None):
            if i is None:
                at = batch_base(b) + BATCH_STEPS.index(name)
                if at:
                    eng.wait_ge(chain, at)
            else:
                eng.wait_ge(chain, i * len(TILE_STEPS) + (batch_base(b) + len(BATCH_STEPS) + TILE_STEPS.index(name)))

        class Own:

            def __init__(self, eng, s):
                self.eng, self.s, self.n = eng, s, 0

            def mark(self, ins):
                ins.then_inc(self.s, 1)
                self.n += 1
                return self.n

            def after(self, n=None):
                self.eng.wait_ge(self.s, self.n if n is None else n)

        @block.sync
        def _(sp):
            def load_x(c):
                g = c * NT
                sp.dma_start(xt[:, g:g + NT, :], x[g * P:(g + NT) * P, :].rearrange("(g p) d -> p g d", p=P)).then_inc(s_x[c], 16)

            load_x(0)
            load_x(1)
            sp.dma_start(vec[:, :], vecs).then_inc(s_vec, 16)
            sp.dma_start(con[:, :], consts).then_inc(s_vec, 16)
            sp.dma_start(win, w_in.rearrange("(k p) o -> p k o", p=P)).then_inc(s_w, 16)
            sp.dma_start(wx[:, :, :], w_x.rearrange("(m p) o -> p m o", p=P)).then_inc(s_w, 16)
            sp.dma_start(wdt[:, :], w_dt).then_inc(s_w, 16)
            load_x(2)
            load_x(3)
            for i, w in enumerate((wq, wqT, wk, wvT, woT)):
                sp.dma_start(aw[:, i, :, :], w.rearrange("(k p) o -> p k o", p=P)).then_inc(s_aw, 16)
            sp.dma_start(wt, wtT.rearrange("(k p) o -> p k o", p=P)).then_inc(s_aw, 16)
            sp.dma_start(wo[:, :, :], w_out.rearrange("(m p) o -> p m o", p=P)).then_inc(s_aw, 16)
            sp.dma_start(w3_row[:, :], w3_s.to_broadcast([B, DM])).then_inc(s_ff3, 16)
            sp.dma_start(mrow, mask[0:1, :].to_broadcast([NH, S])).then_inc(s_mrow, 16)
            for n in range(NCH):
                wait_read(sp, ("X", n, 0))
                sp.dma_start(brow[n], dbc[DR:DR + NS, :]).then_inc(brow_out, 16)
                sp.wait_ge(brow_out, 16 * (n + 1))
                for j in range(PIECES):
                    piece = PIECES * n + j
                    if piece >= BSLOTS:
                        sp.wait_ge(bx_ready, 2 * BROWS * (piece - BSLOTS + 1))
                    slot = piece % BSLOTS
                    src = brow[n:n + 1, j * BROWS:(j + 1) * BROWS, :].to_broadcast([P, BROWS, T])
                    sp.dma_start(Bb[:, slot * BROWS:(slot + 1) * BROWS, :], src).then_inc(bb_in[slot], 16)
            wait_full(sp, ("Z", NCH - 1, 3))
            sp.dma_start(W1, f1.rearrange("(k p) o -> p k o", p=P)).then_inc(s_ff1, 16)
            sp.dma_start(W2, f2.rearrange("(k p) o -> p k o", p=P)).then_inc(s_ff2, 16)
            sp.dma_start(W3, f3.rearrange("(k p) o -> p k o", p=P)).then_inc(s_ff3, 16)
            wait_full(sp, ("O", NCH - 2, 1))
            sp.dma_start(H1, fh1.rearrange("(k p) o -> p k o", p=P)).then_inc(s_ffh1, 16)
            sp.wait_ge(hT_ready, NCH * NS * NT)
            for name, w in (("h1", h1_s), ("h2", h2_s)):
                sp.dma_start(scale_rows[name], w.to_broadcast([B, HID])).then_inc(s_scales, 16)
            wait_full(sp, ("Y", NCH - 1, 3))
            for name, w in (("w1", w1_s), ("w2", w2_s)):
                sp.dma_start(scale_rows[name], w.to_broadcast([B, HID])).then_inc(s_scales, 16)
            sp.dma_start(H2, fh2.rearrange("(k p) o -> p k o", p=P)).then_inc(s_ffh2, 16)
            sp.dma_start(mask_w, mask.bitcast(I32).rearrange("(g p) w -> p g w", p=P)).then_inc(mask_in, 16)
            sp.wait_ge(red_done, 2 * NCH * NS)
            sp.dma_start(mask_0, mask[0:1, :].bitcast(I32).to_broadcast([P, S // 4])).then_inc(mask_in, 16)
            for i in range(2 * B):
                sp.wait_ge(out_ready, i + 1)
                g = i * NT
                sp.dma_start(out[g * P:(g + NT) * P, :].rearrange("(g p) d -> p g d", p=P), outs[:, i // 2, i % 2 * NT:i % 2 * NT + NT, :]).then_inc(out_done, 16)
            sp.wait_ge(out_done, 16 * 2 * B)
            sp.wait_ge(flag_ready, 1)
            with sp.If(sp.value_load(flag_i[0:1, 0:1], min_val=0, max_val=1)):
                for b in range(B):
                    base = batch_base(b) + len(BATCH_STEPS)
                    for i in range(GB):
                        step(sp, b, "mask", i)
                        sp.dma_start(gmask, mask[i * P:(i + 1) * P, :]).then_inc(gmask_in, 16)
                        sp.wait_ge(chain, (i + 1) * len(TILE_STEPS) + base)
                        g = b * GB + i
                        sp.dma_start(out[g * P:(g + 1) * P, :], gout).then_inc(gout_done, 16)
                        sp.wait_ge(gout_done, 16 * (g + 1))

        @block.tensor
        def _(pe):
            mm = nc.tensor.matmul

            def job_F(job, o):
                pe.wait_ge(s_vec, 32)
                for b in range(B):
                    for k in range(KD):
                        c0 = VEC["cond"][0] + k * B + b
                        last = mm(o[:, b:b + 1], vec[:, c0:c0 + 1].to_broadcast([P, P]), v("score_w")[:, k:k + 1], start=k == 0, stop=k == KD - 1)
                return last

            def job_TP(job, o):
                pe.wait_ge(s_aw, 16 * 7)
                cond = v("cond").rearrange("p (k b) -> p k b", k=KD)
                for m in range(KD):
                    for k in range(KD):
                        last = mm(o[:, m * B:(m + 1) * B], wt[:, k, m * P:(m + 1) * P], cond[:, k, :], start=k == 0, stop=k == KD - 1)
                return last

            def job_U(job, o):
                wait_read(pe, ("TP", 0, 0))
                for k in range(KD):
                    for m in range(KD):
                        last = mm(o[:, k * B * NH:(k + 1) * B * NH], aw[:, 0, m, k * P:(k + 1) * P], tpD[:, m, :, :], start=m == 0, stop=m == KD - 1)
                return last

            def job_T(job, o):
                _, n, k = job
                pe.wait_ge(xs_ready, n + 1)
                for i in range(NT):
                    last = nc.tensor.transpose(o[:, i * P:(i + 1) * P], xs(n)[:, i, k * P:(k + 1) * P], ident)
                return last

            def in_proj(n, o, col):
                wait_read(pe, ("T", n, 1))
                for k in range(KD):
                    last = mm(o, win[:, k, col:col + P], xnT[:, k, :], start=k == 0, stop=k == KD - 1)
                return last

            def job_I(job, o):
                _, n, m = job
                if n == 0 and m == 0:
                    wait_read(pe, ("T", n, 0))
                    pe.wait_ge(s_w, 48)
                return in_proj(n, o, m * P)

            def job_Z(job, o):
                _, n, m = job
                return in_proj(n, o, DI + m * P)

            def job_V(job, o):
                _, n, m = job
                wait_read(pe, ("I", n, m))
                pe.wait_ge(halo_ready, n + 1)
                if n == 0 and m == own_conv(0):
                    pe.wait_ge(diag_ready, CT * KC + CT)
                for k in range(KC):
                    last = mm(o, dg[:, m, k, :], xr3[:, m, k:k + T], start=k == 0, stop=k == KC - 1)
                return last

            def job_X(job, o):
                _, n, _ = job
                for m in range(CT):
                    pe.wait_ge(xi_ready, n * CT + (m + 1 if n == 0 else CT))
                    last = mm(o[0:DR + 2 * NS, :], wx[:, m, :], xi(n)[:, m, :], start=m == 0, stop=m == CT - 1)
                return last

            def job_XT(job, o):
                _, n, _ = job
                wait_read(pe, ("X", n, 0))
                w = DR + 2 * NS
                for i in range(NT):
                    last = nc.tensor.transpose(o[:, i * w:(i + 1) * w], dbc[:, i * P:(i + 1) * P], ident[0:w, 0:w])
                return last

            def job_D(job, o):
                _, n, m = job
                wait_read(pe, ("X", n, 0))
                return mm(o, wdt[:, m * P:(m + 1) * P], dbc[0:DR, :], start=True, stop=True)

            def skip(o, e, i, m, first):
                mm(o[:, m * P:(m + 1) * P], diagD[:, m, :], xi(e)[:, m, i * P:(i + 1) * P], start=first, stop=False, skip_group_check=True)

            def add_turned(o, m, src, last):
                return mm(o[:, m * P:(m + 1) * P], src, ident, start=False, stop=last, is_transpose=True, skip_group_check=True)

            def job_Y(job, o):
                _, e, i = job
                pe.wait_ge(mac_done, 2 * (NS * (e + 1) - 1) + i // 2 + 1)
                for m in range(CT):
                    skip(o, e, i, m, m == 0)
                for m in range(CT):
                    last = add_turned(o, m, yTd[:, e % 2, i // 2, m * P:(m + 1) * P], True)
                return last

            def job_O(job, o):
                _, e, j = job
                if j:
                    for i in (1, 3):
                        wait_read(pe, ("Y", e, i))
                pe.wait_ge(gated, 2 * (e + 1))
                if e == 0 and j == 0:
                    pe.wait_ge(half_ready, 3)
                for i in range(2):
                    t0 = (j + 2 * i) * P
                    for m in range(CT):
                        last = mm(o[:, i * DM:(i + 1) * DM], dx(e)[:, m, t0:t0 + P], wo[:, m, :], start=m == 0, stop=m == CT - 1)
                return last

            def job_R(job, o):
                _, e, j = job
                wait_read(pe, ("O", e, j))
                for k in range(KD):
                    for i in range(2):
                        g = e * NT + j + 2 * i
                        last = nc.tensor.transpose(o[:, (2 * k + i) * P:(2 * k + i + 1) * P], xt[:, g, k * P:(k + 1) * P], ident)
                return last

            def job_A(job, o):
                _, b, h = job
                for j in range(2):
                    wait_read(pe, ("R", b * HALVES + h, j))
                if b == 0:
                    wait_read(pe, ("U", 0, 0))
                for i in range(NT):
                    for k in range(KD):
                        t0 = h * T + i * P
                        last = mm(o[:, i * NH:(i + 1) * NH], x1T[:, k, t0:t0 + P], u[:, k, b * NH:(b + 1) * NH], start=k == 0, stop=k == KD - 1)
                return last

            def heads_by_rows(o, w, first, tiles):
                for i in range(tiles):
                    last = mm(o[0:NH, 0:DM], w[:, i, :], xt[:, first + i, :], start=i == 0, stop=i == tiles - 1)
                return last

            def features_up(o, src):
                for k in range(KD):
                    last = nc.tensor.transpose(o[:, k * NH:(k + 1) * NH], src[:, k * P:(k + 1) * P], ident[0:NH, 0:NH])
                return last

            def rows_by_heads(b, o, w):
                for k in range(KD):
                    for i in range(GB):
                        last = mm(o[:, k * NH:(k + 1) * NH], xt[:, b * GB + i, k * P:(k + 1) * P], w[:, i, :], start=i == 0, stop=i == GB - 1)
                return last

            def weight_by_heads(o, w, src):
                for m in range(KD):
                    for k in range(KD):
                        last = mm(o[:, m * NH:(m + 1) * NH], aw[:, w, k, m * P:(m + 1) * P], src[:, k, :], start=k == 0, stop=k == KD - 1)
                return last

            def job_G(job, o):
                _, b, h = job
                wait_read(pe, ("A", b, h))
                return heads_by_rows(o, a_sb[:, h * NT:(h + 1) * NT, :], b * GB + h * NT, NT)

            def job_GT(job, o):
                wait_read(pe, ("G", job[1], 1))
                return features_up(o, g_row)

            def job_M(job, o):
                wait_read(pe, ("GT", job[1], 0))
                return weight_by_heads(o, 1, g_sb)

            def job_RR(job, o):
                wait_read(pe, ("M", job[1], 0))
                return weight_by_heads(o, 2, qD)

            def scores(job, o, j):
                wait_read(pe, ("RR", job[1], 0))
                for k in range(KD):
                    last = mm(o[0:NH, :], r_sb[:, k, :], x1T[:, k, j * 512:(j + 1) * 512], start=k == 0, stop=k == KD - 1)
                return last

            def job_S0(job, o):
                return scores(job, o, 0)

            def job_S1(job, o):
                return scores(job, o, 1)

            def job_PT(job, o):
                pe.wait_ge(p_ready, job[1] + 1)
                for i in range(GB):
                    last = nc.tensor.transpose(o[:, i * NH:(i + 1) * NH], sm[:, i * P:(i + 1) * P], ident[0:NH, 0:NH])
                return last

            def job_YV(job, o):
                wait_read(pe, ("PT", job[1], 0))
                return heads_by_rows(o, pT, job[1] * GB, GB)

            def job_YT(job, o):
                wait_read(pe, ("YV", job[1], 0))
                return features_up(o, y_row)

            def job_VV(job, o):
                wait_read(pe, ("YT", job[1], 0))
                return weight_by_heads(o, 3, yv)

            def job_WO(job, o):
                wait_read(pe, ("VV", job[1], 0))
                for m in range(KD):
                    for k in range(KD):
                        last = mm(o[:, m:m + 1], aw[:, 4, k, m * P:(m + 1) * P], ov[:, k:k + 1], start=k == 0, stop=k == KD - 1)
                return last

            def ffn(o, w, src, half, ins, width=HID // 2):
                for k in range(ins):
                    last = mm(o[0:B, 0:width], src[:, k, :], w[:, k, half * width:(half + 1) * width], start=k == 0, stop=k == ins - 1)
                return last

            def turned_back(o, row, at):
                for m in range(KH):
                    last = nc.tensor.transpose(o[:, at + m * B:at + (m + 1) * B], row[:, m * P:(m + 1) * P], ident[0:B, 0:B])
                return last

            def job_W1(job, o):
                if job[1] == 0:
                    wait_read(pe, ("WO", 0, 0))
                    wait_read(pe, ("WO", 1, 0))
                    pe.wait_ge(s_ff1, 16)
                return ffn(o, W1, z_sb, job[1], KD)

            def job_W2(job, o):
                if job[1] == 0:
                    pe.wait_ge(s_ff2, 16)
                return ffn(o, W2, z_sb, job[1], KD)

            def job_WT(job, o):
                for name in ("W1", "W2"):
                    for half in range(2):
                        wait_read(pe, (name, half, 0))
                turned_back(o, row1, 0)
                return turned_back(o, row2, KH * B)

            def job_FL(job, o):
                pe.wait_ge(flag_row, 1)
                return nc.tensor.transpose(o[0:1, 0:P], flag[:, 0:1], ident)

            def job_H(job, o):
                _, layer, half = job
                wait_read(pe, ("WT", 0, 0) if layer == 1 else ("HT", 1, 0))
                pe.wait_ge(s_ffh1 if layer == 1 else s_ffh2, 16)
                return ffn(o, H1 if layer == 1 else H2, ff[:, layer - 1, :, :], half, KH)

            def job_HT(job, o):
                for half in range(2):
                    wait_read(pe, ("H", job[1], half))
                return turned_back(o, row1, 0)

            def job_W3(job, o):
                wait_read(pe, ("HT", 2, 0))
                pe.wait_ge(s_ff3, 32)
                return ffn(o, W3, ff[:, 0, :, :], 0, KH, width=DM)

            def job_FB(job, o):
                wait_read(pe, ("W3", 0, 0))
                return mm(o[:, 0:DM], ident[0:B, job[1]:job[1] + 1].to_broadcast([B, P]), row3, start=True, stop=True)

            jobs = dict(F=job_F, TP=job_TP, U=job_U, T=job_T, I=job_I, Z=job_Z, V=job_V, X=job_X, XT=job_XT, D=job_D, Y=job_Y,
                        O=job_O, R=job_R, A=job_A, G=job_G, GT=job_GT, M=job_M, RR=job_RR, S0=job_S0, S1=job_S1, PT=job_PT, YV=job_YV, YT=job_YT,
                        VV=job_VV, WO=job_WO, W1=job_W1, W2=job_W2, WT=job_WT, FL=job_FL, H=job_H, HT=job_HT, W3=job_W3, FB=job_FB)

            def keep_warm(products):
                for _ in range(products):
                    mm(dA[:, 0, 0:P], ident, ident, start=True, stop=True)

            def run(job):
                q = INDEX[job]
                if q >= 2:
                    pe.wait_ge(job_free[q % 2], q // 2)
                jobs[job[0]](job, bank(job)).then_inc(job_full, 1)

            def transposes(n, i):
                if i == 0:
                    pe.wait_ge(scan_done, CT * (n + 1))
                e = 2 * n + i // 2
                if e >= 1:
                    pe.wait_ge(mac_done if i % 2 else mul_done, e)
                for m in range(CT):
                    last = nc.tensor.transpose(hT[:, i % 2, m * P:(m + 1) * P], hb[:, n % RING, m, i * P:(i + 1) * P], ident)
                last.then_inc(hT_ready, 1)

            def reduce(n, i):
                e = 2 * n + i // 2
                s = n % NS
                pe.wait_ge(mul_done, e + 1)
                o = yacc[:, i // 2, :]
                if s == 0:
                    c = n // NS
                    if c:
                        pe.wait_ge(gated, 2 * (c - 1) + i // 2 + 1)
                    for m in range(CT):
                        skip(o, c, i, m, m == 0)
                for m in range(CT):
                    last = add_turned(o, m, hc[:, e % 2, m * P:(m + 1) * P], s == NS - 1)
                last.then_inc(red_done, 1)

            run(("F", 0, 0))
            for b in range(B):
                pe.wait_ge(ss_act, 4 if b == 0 else 12)
                if b == 0:
                    pe.wait_ge(ss_dve, 4)
                dst = yacc if b == 0 else hT
                for i in range(GB):
                    last = nc.tensor.transpose(dst[:, i // 4, (i % 4) * P:(i % 4 + 1) * P], ss[:, b * GB + i:b * GB + i + 1].to_broadcast([P, P]), ident)
                last.then_inc(mag_pe, 1)
                keep_warm(WARM_HEAD[b])
            for job in HEAD[1:]:
                run(job)
            pe.wait_ge(mag_act, 2)
            for c in range(NCH):
                for s in range(NS):
                    n = c * NS + s
                    if n:
                        transposes(n - 1, 0)
                        transposes(n - 1, 1)
                    for job in BESIDE[2 * n]:
                        run(job)
                    if n:
                        transposes(n - 1, 2)
                        transposes(n - 1, 3)
                        reduce(n - 1, 0)
                        reduce(n - 1, 2)
                    for job in BESIDE[2 * n + 1]:
                        run(job)
            n = NCH * NS
            for i in range(NT):
                transposes(n - 1, i)
            reduce(n - 1, 0)
            reduce(n - 1, 2)
            for job in TAIL:
                run(job)
                keep_warm(WARM.get(job, 0))

            def general_batch(b):
                def did(ins):
                    ins.then_inc(chain, 1)

                for j in range(GB // 2):
                    step(pe, b, f"turn_x{j}")
                    for k in range(KD):
                        for i in range(2):
                            last = nc.tensor.transpose(pp[:, 0, (2 * k + i) * P:(2 * k + i + 1) * P], xt[:, b * GB + 2 * j + i, k * P:(k + 1) * P], ident)
                    did(last)
                step(pe, b, "a")
                for i in range(GB):
                    for k in range(KD):
                        last = mm(pp[:, 0, i * NH:(i + 1) * NH], x1T[:, k, i * P:(i + 1) * P], u[:, k, b * NH:(b + 1) * NH], start=k == 0, stop=k == KD - 1)
                did(last)
                step(pe, b, "g")
                did(rows_by_heads(b, pp[:, 0, :], a_sb))
                step(pe, b, "m")
                did(weight_by_heads(pp[:, 0, :], 1, g_sb))
                step(pe, b, "r")
                did(weight_by_heads(pp[:, 0, :], 2, qD))
                for j in range(2):
                    step(pe, b, f"s{j}")
                    for k in range(KD):
                        last = mm(pp[0:NH, 0, :], r_sb[:, k, :], x1T[:, k, j * 512:(j + 1) * 512], start=k == 0, stop=k == KD - 1)
                    did(last)
                for j in range(GB // 2):
                    step(pe, b, f"v{j}")
                    for i in range(2):
                        for k in range(KD):
                            t0 = (2 * j + i) * P
                            last = mm(pp[:, 0, i * DM:(i + 1) * DM], x1T[:, k, t0:t0 + P], aw[:, 3, k, :], start=k == 0, stop=k == KD - 1)
                    did(last)
                with pe.Fori(0, GB) as t:
                    for h in range(NH):
                        step(pe, b, f"row{h}", t)
                        for j in range(2):
                            last = mm(hT[:, j, :], ident[0:NH, h:h + 1].to_broadcast([NH, P]), sm[:, j * 512:(j + 1) * 512], start=True, stop=True)
                        did(last)
                        step(pe, b, f"turn{h}", t)
                        for i in range(GB):
                            last = nc.tensor.transpose(yacc[:, i // 4, (i % 4) * P:(i % 4 + 1) * P], gsc[:, i * P:(i + 1) * P], ident)
                        did(last)
                        step(pe, b, f"pv{h}", t)
                        for i in range(GB):
                            last = mm(dA[:, 0, h * HE:(h + 1) * HE], gpT[:, i, :], gv[:, i, h * HE:(h + 1) * HE], start=i == 0, stop=i == GB - 1)
                        did(last)
                    step(pe, b, "turn_o", t)
                    for k in range(KD):
                        last = nc.tensor.transpose(pp[:, 0, k * P:(k + 1) * P], go[:, k * P:(k + 1) * P], ident)
                    did(last)

                    def layer(dst, w, src, outs_, ins_):
                        for m in range(outs_):
                            for k in range(ins_):
                                last = mm(dst(m), w[:, k, m * P:(m + 1) * P], src[:, k, :], start=k == 0, stop=k == ins_ - 1)
                        return last

                    def in_hT(m):
                        return hT[:, m // 4, (m % 4) * P:(m % 4 + 1) * P]

                    def in_yacc(m):
                        return yacc[:, m // 4, (m % 4) * P:(m % 4 + 1) * P]

                    def in_pp(m):
                        return pp[:, 0, m * P:(m + 1) * P]

                    step(pe, b, "wo", t)
                    did(layer(in_pp, aw[:, 4, :, :], goT, KD, KD))
                    step(pe, b, "w12", t)
                    layer(in_hT, W1, gz, KH, KD)
                    did(layer(in_yacc, W2, gz, KH, KD))
                    step(pe, b, "h1", t)
                    did(layer(in_hT, H1, gf1, KH, KH))
                    step(pe, b, "h2", t)
                    did(layer(in_hT, H2, gf2, KH, KH))
                    step(pe, b, "w3", t)
                    did(layer(in_pp, W3, gf1, KD, KH))
                    step(pe, b, "turn_f", t)
                    for k in range(KD):
                        last = nc.tensor.transpose(pp[:, 1, k * P:(k + 1) * P], gf3[:, k, :], ident)
                    did(last)

            pe.wait_ge(flag_ready, 1)
            with pe.If(pe.value_load(flag_i[0:1, 0:1], min_val=0, max_val=1)):
                pe.wait_ge(out_done, 16 * 2 * B)
                for b in range(B):
                    general_batch(b)

        @block.scalar
        def _(act):
            A = nc.scalar.activation
            own = Own(act, act_own)

            def exp_ln_table():
                act.preload_act_table_set("natural_log_exp_and_others")

            def ev_U(job, o):
                return A(u[:, :, :], o[:, 0:KD * B * NH].rearrange("p (k j) -> p k j", k=KD), ACT.Copy)

            def ev_T(job, o):
                _, n, k = job
                if n:
                    wait_full(act, ("Z", n - 1, 3))
                return A(xnT[:, k, :], o, ACT.Copy, scale=v("rms_w")[:, k:k + 1])

            def ev_I(job, o):
                _, n, m = job
                if m == 0:
                    if n:
                        act.wait_ge(conv_ready, convs_done(n - 1))
                    if n >= 2:
                        act.wait_ge(pool_conv_ready, n - 1)
                    if n % HALVES == 0:
                        if n == 0:
                            act.wait_ge(init_done, 1)
                        else:
                            wait_full(act, ("V", n - 1, 3))
                        A(xr3[:, :, 0:KC - 1], zero[:, :, :], ACT.Copy).then_inc(halo_ready, 1)
                    else:
                        wait_full(act, ("V", n - 1, 3))
                        wait_read(act, ("I", n - 1, 3))
                        wait_read(act, ("I", n - 1, 2))
                        A(xr3[:, :, 0:KC - 1], xr3[:, :, T:T + KC - 1], ACT.Copy).then_inc(halo_ready, 1)
                    act.wait_ge(halo_ready, n + 1)
                return A(xr3[:, m, KC - 1:], o, ACT.Copy)

            def ev_V(job, o):
                _, n, m = job
                if n >= 2:
                    wait_full(act, ("Y", n - 2, 3))
                    act.wait_ge(red_done, 2 * NS * (n - 1))
                if n == 0 and m == own_conv(0):
                    act.wait_ge(half_ready, 1)
                A(xi(n)[:, m, :], o, ACT.Identity, bias=half_b[:, m:m + 1], scale=0.5)
                return A(delta(n)[:, m, :], o, ACT.Tanh, bias=half_b[:, m:m + 1], scale=0.5)


            def ev_X(job, o):
                _, n, _ = job
                if n:
                    wait_full(act, ("D", n - 1, 3))
                    act.wait_ge(brow_out, 16 * n)
                return A(dbc[:, :], o[0:DR + 2 * NS, :], ACT.Copy)

            def ev_XT(job, o):
                _, n, _ = job
                if n >= 2:
                    act.wait_ge(mac_done, 2 * NS * (n - 1))
                w = DR + 2 * NS
                return A(CTs[:, n % 2, :, :], o[:, 0:NT * w].rearrange("p (i w) -> p i w", i=NT)[:, :, DR + NS:w], ACT.Copy)

            def conv_tanh(n, m):
                done = convs_done(n) - own_conv(n) + m + 1
                act.wait_ge(conv_ready, done)
                A(delta(n)[:, m, :], xi(n)[:, m, :], ACT.Tanh).then_inc(conv_tanh_ready, 1)

            def pool_conv_tanh(n):
                act.wait_ge(pool_conv_ready, n)
                A(delta(n)[:, POOL_TILE, :], xi(n)[:, POOL_TILE, :], ACT.Tanh).then_inc(pool_tanh_ready, 1)

            def ev_Z(job, o):
                _, n, m = job
                if n >= 2:
                    wait_read(act, ("Y", n - 2, 3))
                    wait_read(act, ("Y", n - 2, 1))
                    act.wait_ge(gated, 2 * (n - 1))
                A(gate(n)[:, m, :], o, ACT.Tanh, scale=0.5).then_inc(tanh_ready, 1)
                return None

            def ev_D(job, o):
                _, n, m = job
                if m == 0:
                    if n >= 2:
                        wait_full(act, ("O", n - 2, 1))
                whole = A(delta(n)[:, m, :], o, ACT.Abs, bias=v("dt_b")[:, m:m + 1])
                if n == 0:
                    whole.then_inc(abs_ready, 1)
                    return None
                return A(dx(n)[:, m, :], o, ACT.Relu, bias=v("dt_b")[:, m:m + 1])

            def softplus(n, m):
                if n == 0:
                    act.wait_ge(abs_ready, m + 1)
                else:
                    wait_read(act, ("D", n, m))
                own.mark(A(delta(n)[:, m, :], delta(n)[:, m, :], ACT.Exp, scale=-1.0))
                own.after()
                A(delta(n)[:, m, :], delta(n)[:, m, :], ACT.Ln, bias=1.0).then_inc(sp_ready, 1)

            def ev_R(job, o):
                _, e, j = job
                if e == HALVES:
                    wait_full(act, ("S1", 0, 0))
                if e == 0 and j == 0:
                    act.wait_ge(ranked, 3)
                dst = x1T.rearrange("p k (e i j t) -> p k e i j t", e=HALVES, i=2, j=2)[:, :, e % HALVES, :, j, :]
                return A(dst, o.rearrange("p (k i t) -> p k i t", k=KD, i=2), ACT.Copy)

            def ev_A(job, o):
                h = job[2]
                return A(a_sb[:, h * NT:(h + 1) * NT, :], o[:, 0:NT * NH].rearrange("p (i h) -> p i h", i=NT), ACT.Copy)

            def ev_GT(job, o):
                return A(g_sb[:, :, :], o[:, 0:KD * NH].rearrange("p (k h) -> p k h", k=KD), ACT.Copy)

            def ev_RR(job, o):
                return A(r_sb[:, :, :], o[:, 0:KD * NH].rearrange("p (k h) -> p k h", k=KD), ACT.Copy, scale=HE ** -0.5)

            def softmax(b):
                act.wait_ge(mx_ready, b + 1)
                A(sm[:, :], sm[:, :], ACT.Exp, bias=st[:, 1:2], accum_out=st[:, 2:3]).then_inc(p_ready, 1)

            def ev_PT(job, o):
                return A(pT[:, :, :], o[:, 0:GB * NH].rearrange("p (i h) -> p i h", i=GB), ACT.Copy)

            def ev_YV(job, o):
                act.wait_ge(recip_ready, job[1] + 1)
                return A(y_row, o[0:NH, 0:DM], ACT.Copy, scale=st[:, 3:4])

            def ev_YT(job, o):
                return A(yv[:, :, :], o[:, 0:KD * NH].rearrange("p (k h) -> p k h", k=KD), ACT.Copy)

            def ev_WO(job, o):
                return A(z_sb[:, :, job[1]], o[:, 0:KD], ACT.Copy)

            def ev_HT(job, o):
                return A(ff[:, job[1] % 2, :, :], o[:, 0:KH * B].rearrange("p (m b) -> p m b", b=B), ACT.Gelu)

            evs = dict(HT=ev_HT, U=ev_U, T=ev_T, I=ev_I, V=ev_V, X=ev_X, XT=ev_XT, Z=ev_Z, D=ev_D, R=ev_R, A=ev_A, GT=ev_GT, RR=ev_RR,
                       PT=ev_PT, YV=ev_YV, YT=ev_YT, WO=ev_WO)

            def after_job(job):
                name, n, i = job
                if name == "D" and n and i == 0:
                    exp_ln_table()
                if name == "D":
                    softplus(n, i)
                if name == "S1":
                    softmax(n)

            def read(job):
                if job[0] in evs:
                    wait_full(act, job)
                    last = evs[job[0]](job, bank(job))
                    if last is not None:
                        last.then_inc(freed(job), 1)
                after_job(job)

            exp_ln_table()
            def square(g):
                if g % NT == 0 or (g < GB and g % NT == 1):
                    act.wait_ge(s_x[g // NT], 16)
                A(hb[:, 0, g % CT, 0:DM], xt[:, g, :], ACT.Square, accum_out=ss[:, g:g + 1]).then_inc(ss_act, 1)
            for i, g in enumerate(range(1, GB, 2)):
                if i:
                    act.wait_ge(ss_act, i)
                square(g)
            wait_read(act, ("F", 0, 0))
            A(fr[:, 1, :], fr[:, 0, :], ACT.Exp, scale=-1.0).then_inc(fe_ready, 1)
            def rstd(b):
                act.wait_ge(ss_act, 4 if b == 0 else 12)
                if b == 0:
                    act.wait_ge(ss_dve, 4)
                    act.wait_ge(init_done, 1)
                gs = slice(b * GB, (b + 1) * GB)
                own.mark(A(lnv[:, gs], ss[:, gs], ACT.Ln, bias=eps[:, :], scale=1.0 / DM))
                own.after()
                A(lnv[:, gs], lnv[:, gs], ACT.Exp, scale=-0.5).then_inc(rstd_ready, 1)
            rstd(0)
            act.wait_ge(s_vec, 32)
            A(Aneg[:, :], v("A_log"), ACT.Exp).then_inc(aexp_ready, 1)
            for g in range(GB, 2 * GB):
                act.wait_ge(ss_act, 4 + g - GB)
                square(g)
            rstd(1)
            act.wait_ge(mag_pe, 2)
            for i in range(2):
                A(magrow[:, i * 512:(i + 1) * 512], hT[:, i, :], ACT.Copy).then_inc(mag_act, 1)
            for job in HEAD:
                read(job)
                if job == ("I", 0, CT - 1):
                    for m in range(own_conv(0)):
                        conv_tanh(0, m)
                if job == ("V", 0, CT - 1):
                    exp_ln_table()

            def exp_step(n, m):
                c, s = n // NS, n % NS
                i = n * CT + m
                if s == 0:
                    act.wait_ge(delta_ready, CT * c + m + 1)
                if n == 0 and m == 0:
                    act.wait_ge(A_ready, 1)
                if i >= 2:
                    act.wait_ge(scan_done, i - 1)
                A(dA[:, m % 2, :], delta(c)[:, m, :], ACT.Exp, scale=Aneg[:, m * NS + s:m * NS + s + 1]).then_inc(da_ready, 1)

            def mul_step(n, i):
                c, s = n // NS, n % NS
                e = 2 * n + i // 2
                act.wait_ge(hT_ready, NT * n + i + 1)
                if e >= 2:
                    act.wait_ge(red_done, e - 1)
                A(hc[:, e % 2, :], hT[:, 0, :], ACT.Copy, scale=CTs[:, c % 2, i, s:s + 1]).then_inc(mul_done, 1)

            def carry_step(n):
                c, s = n // NS, n % NS
                if c % HALVES == 0:
                    act.wait_ge(scan_done, CT * (n + 1))
                    A(carry[:, s, :], hb[:, n % RING, :, T - 1], ACT.Copy).then_inc(carry_done, 1)

            for c in range(NCH):
                for s in range(NS):
                    n = c * NS + s
                    exp_step(n, 0)
                    exp_step(n, 1)
                    if n:
                        mul_step(n - 1, 0)
                    for job in to_read(2 * n):
                        read(job)
                    if c + 1 < NCH and 2 * s == POOL_CONV_AT["tanh"]:
                        pool_conv_tanh(c + 1)
                    if c + 1 < NCH and 2 * s == CONV_AT["tanh"]:
                        for m in range(LOOP_CONV):
                            conv_tanh(c + 1, m)
                    exp_step(n, 2)
                    exp_step(n, 3)
                    if n:
                        mul_step(n - 1, 2)
                        carry_step(n - 1)
                    for job in to_read(2 * n + 1):
                        read(job)
                    if c + 1 < NCH and 2 * s + 1 == POOL_CONV_AT["tanh"]:
                        pool_conv_tanh(c + 1)
                    if c + 1 < NCH and 2 * s + 1 == CONV_AT["tanh"]:
                        for m in range(LOOP_CONV):
                            conv_tanh(c + 1, m)
            n = NCH * NS
            mul_step(n - 1, 0)
            mul_step(n - 1, 2)
            for job in BESIDE[-1] + TAIL:
                read(job)
                if job[0] == "WO":
                    act.preload_act_table(ACT.Silu)
                if job[0] == "WT":
                    wait_full(act, job)
                    A(ff[:, 2, :, :], bank(job)[:, 0:KH * B].rearrange("p (m b) -> p m b", b=B), ACT.Silu).then_inc(silu_ready, 1)
                    act.preload_act_table(ACT.Gelu)

            def general_batch(b):
                def did(ins):
                    ins.then_inc(chain, 1)

                for j in range(GB // 2):
                    step(act, b, f"turn_x_out{j}")
                    did(A(x1T[:, :, 2 * j * P:2 * (j + 1) * P], pp[:, 0, :].rearrange("p (k t) -> p k t", k=KD), ACT.Copy))
                step(act, b, "a_out")
                did(A(a_sb[:, :, :], pp[:, 0, 0:GB * NH].rearrange("p (i h) -> p i h", i=GB), ACT.Copy))
                step(act, b, "g_out")
                did(ev_GT(None, pp[:, 0, :]))
                step(act, b, "r_out")
                did(ev_RR(None, pp[:, 0, :]))
                for j in range(2):
                    step(act, b, f"s{j}_out")
                    did(A(sm[:, j * 512:(j + 1) * 512], pp[0:NH, 0, :], ACT.Copy))
                for j in range(GB // 2):
                    step(act, b, f"v_out{j}")
                    did(A(gv[:, 2 * j:2 * j + 2, :], pp[:, 0, :].rearrange("p (i o) -> p i o", i=2), ACT.Copy))
                with act.Fori(0, GB) as t:
                    for h in range(NH):
                        step(act, b, f"exp{h}", t)
                        did(A(gsc, gsc, ACT.Exp, bias=gst[:, 1:2], accum_out=gst[:, 2:3]))
                        step(act, b, f"turn_out{h}", t)
                        did(A(gpT, yacc[:, :, :].rearrange("p a (i t) -> p (a i) t", i=4), ACT.Copy))
                    step(act, b, "turn_o_out", t)
                    did(A(goT, pp[:, 0, 0:DM].rearrange("p (k t) -> p k t", k=KD), ACT.Copy))
                    step(act, b, "wo_out", t)
                    did(A(gz, pp[:, 0, 0:DM].rearrange("p (k t) -> p k t", k=KD), ACT.Copy))
                    step(act, b, "silu", t)
                    did(A(gf1, gf1, ACT.Silu))
                    step(act, b, "gelu1", t)
                    did(A(gf2, gf2, ACT.Gelu))
                    step(act, b, "gelu2", t)
                    did(A(gf1, gf1, ACT.Gelu))

            act.wait_ge(flag_ready, 1)
            with act.If(act.value_load(flag_i[0:1, 0:1], min_val=0, max_val=1)):
                for b in range(B):
                    general_batch(b)

        @block.gpsimd
        def _(pool):
            nc.gpsimd.memset(eps[:, :], EPS)
            nc.gpsimd.memset(zero[:, :, :], 0.0).then_inc(init_done, 1)
            pool.wait_ge(s_vec, 32)
            nc.gpsimd.tensor_scalar(half_b[:, :], v("conv_b"), 0.5, 1.0, ALU.mult, ALU.mult).then_inc(half_ready, 1)
            nc.gpsimd.tensor_scalar(half_w[:, :], v("conv_w"), 0.5, 1.0, ALU.mult, ALU.mult).then_inc(half_ready, 1)
            for m in range(CT):
                for k in range(KC):
                    nc.gpsimd.tensor_scalar(dg[:, m, k, :], ident, v("conv_w")[:, m * KC + k:m * KC + k + 1], 1.0, ALU.mult, ALU.mult).then_inc(diag_ready, 1)
            for m in range(CT):
                nc.gpsimd.tensor_scalar(diagD[:, m, :], ident, v("D")[:, m:m + 1], 1.0, ALU.mult, ALU.mult).then_inc(diag_ready, 1)

            pool.wait_ge(s_aw, 16 * 7)
            nc.gpsimd.tensor_scalar(wo[:, :, :], wo[:, :, :], 0.5, 1.0, ALU.mult, ALU.mult).then_inc(half_ready, 1)

            def input_step(n, pair):
                c, s = n // NS, n % NS
                piece = n // BROWS
                row = (piece % BSLOTS) * BROWS + s % BROWS
                if s % BROWS == 0 and pair == 0:
                    pool.wait_ge(bb_in[piece % BSLOTS], 16 * (piece // BSLOTS + 1))
                if s == 0:
                    pool.wait_ge(dx_ready, CT * c + 2 * (pair + 1))
                if n >= RING:
                    pool.wait_ge(hT_ready, NT * (n - RING + 1))
                    if (n - RING) // NS % HALVES == 0:
                        done = (n - RING) // NS // HALVES * NS + (n - RING) % NS + 1
                        pool.wait_ge(carry_done, done)
                ms = slice(2 * pair, 2 * pair + 2)
                nc.gpsimd.tensor_tensor(hb[:, n % RING, ms, :], dx(c)[:, ms, :], Bb[:, row:row + 1, :].to_broadcast([P, 2, T]), ALU.mult).then_inc(bx_ready, 1)

            own = Own(pool, pool_own)

            def conv_taps(n, taps):
                m = POOL_TILE
                acc = xi(n)[:, m, :]
                for k in taps:
                    if k == 0:
                        wait_read(pool, ("I", n, m))
                        pool.wait_ge(halo_ready, n + 1)
                        if n >= 2:
                            wait_full(pool, ("Y", n - 2, 3))
                            pool.wait_ge(red_done, 2 * NS * (n - 1))
                        tap = nc.gpsimd.tensor_scalar(acc, xr3[:, m, 0:T], half_w[:, m * KC:m * KC + 1], half_b[:, m:m + 1], ALU.mult, ALU.add)
                    else:
                        own.after()
                        own.mark(nc.gpsimd.tensor_scalar(delta(n)[:, m, :], xr3[:, m, k:k + T], half_w[:, m * KC + k:m * KC + k + 1], 1.0, ALU.mult, ALU.mult))
                        own.after()
                        tap = nc.gpsimd.tensor_tensor(acc, acc, delta(n)[:, m, :], ALU.add)
                    if k < KC - 1:
                        own.mark(tap)
                    else:
                        tap.then_inc(pool_conv_ready, 1)

            for c in range(NCH):
                for s in range(NS):
                    n = c * NS + s
                    input_step(n, 0)
                    input_step(n, 1)
                    if c + 1 < NCH and s in POOL_AT:
                        conv_taps(c + 1, range(0, 2) if s == POOL_AT[0] else range(2, KC))

        @block.vector
        def _(dve):
            V = nc.vector
            own = Own(dve, dve_own)

            def conv_taps(n, m, taps):
                acc = xi(n)[:, m, :]
                for k in taps:
                    if k == 0:
                        wait_read(dve, ("I", n, m))
                        dve.wait_ge(halo_ready, n + 1)
                        if n >= 2:
                            wait_full(dve, ("Y", n - 2, 3))
                            dve.wait_ge(red_done, 2 * NS * (n - 1))
                        tap = V.tensor_scalar(acc, xr3[:, m, 0:T], half_w[:, m * KC:m * KC + 1], half_b[:, m:m + 1], ALU.mult, ALU.add)
                    else:
                        own.after()
                        tap = V.scalar_tensor_tensor(acc, xr3[:, m, k:k + T], half_w[:, m * KC + k:m * KC + k + 1], acc, ALU.mult, ALU.add)
                    if k < KC - 1:
                        own.mark(tap)
                    else:
                        tap.then_inc(conv_ready, 1)

            def conv_finish(n, m):
                dve.wait_ge(conv_tanh_ready, convs_done(n) - own_conv(n) + m + 1)
                V.scalar_tensor_tensor(xi(n)[:, m, :], delta(n)[:, m, :], 1.0, xi(n)[:, m, :], ALU.add, ALU.mult).then_inc(xi_ready, 1)

            def rows(c):
                if c >= 2:
                    dve.wait_ge(scan_done, NS * CT * (c - 1))
                for i in range(NT):
                    g = c * NT + i
                    last = V.tensor_scalar(xs(c)[:, i, :], xt[:, g, :], scl[:, g:g + 1], None, ALU.mult)
                last.then_inc(xs_ready, 1)

            def ev_F(job, o):
                return V.tensor_scalar(fr[:, 0, :], o[:, 0:B], v("score_b"), None, ALU.add)

            def ev_TP(job, o):
                tp = o[:, 0:KD * B].rearrange("p (m b) -> p m b", m=KD)
                return V.tensor_tensor(tpD[:, :, :, :], bm[:, :, None, :].to_broadcast([P, KD, B, NH]), tp[:, :, :, None].to_broadcast([P, KD, B, NH]), ALU.mult)

            def gate_tile(e, i, o):
                for m in (CT - 2, CT - 1):
                    wait_read(dve, ("Z", e, m))
                t0 = slice(i * P, (i + 1) * P)
                return V.tensor_tensor(dx(e)[:, :, t0], o.rearrange("p (m t) -> p m t", m=CT), gate(e)[:, :, t0], ALU.mult)

            def gate_even(e):
                for i in (0, 2):
                    dve.wait_ge(red_done, 2 * (NS * (e + 1) - 1) + i // 2 + 1)
                    gate_tile(e, i, yacc[:, i // 2, :]).then_inc(gated, 1)

            def ev_V(job, o):
                _, n, m = job
                wait_read(dve, job)
                V.scalar_tensor_tensor(xi(n)[:, m, :], delta(n)[:, m, :], 1.0, xi(n)[:, m, :], ALU.add, ALU.mult).then_inc(xi_ready, 1)
                return None

            def ev_Z(job, o):
                _, n, m = job
                dve.wait_ge(tanh_ready, CT * n + m + 1)
                return V.scalar_tensor_tensor(gate(n)[:, m, :], gate(n)[:, m, :], 1.0, o, ALU.add, ALU.mult)

            def ev_D(job, o):
                _, n, m = job
                if n == 0:
                    dve.wait_ge(abs_ready, m + 1)
                    V.tensor_scalar(dx(0)[:, m, :], o, v("dt_b")[:, m:m + 1], 0.0, ALU.add, ALU.max).then_inc(freed(job), 1)
                    wait_read(dve, job)
                dve.wait_ge(sp_ready, CT * n + m + 1)
                V.tensor_tensor(delta(n)[:, m, :], delta(n)[:, m, :], dx(n)[:, m, :], ALU.add).then_inc(delta_ready, 1)
                dve.wait_ge(delta_ready, CT * n + m + 1)
                V.tensor_tensor(dx(n)[:, m, :], delta(n)[:, m, :], xi(n)[:, m, :], ALU.mult).then_inc(dx_ready, 1)
                return None

            def ev_Y(job, o):
                return gate_tile(job[1], job[2], o)

            def ev_O(job, o):
                _, e, j = job
                for i in range(2):
                    g = e * NT + j + 2 * i
                    last = V.scalar_tensor_tensor(xt[:, g, :], xt[:, g, :], keep1[:, g:g + 1], o[:, i * DM:(i + 1) * DM], ALU.mult, ALU.add)
                return last

            def ev_G(job, o):
                _, b, h = job
                if h == 0:
                    return V.tensor_copy(g_row, o[0:NH, 0:DM])
                wait_read(dve, ("G", b, 0))
                return V.tensor_tensor(g_row, g_row, o[0:NH, 0:DM], ALU.add)

            def ev_M(job, o):
                return V.tensor_tensor(qD[:, :, :], o[:, 0:KD * NH].rearrange("p (m h) -> p m h", m=KD), bm, ALU.mult)

            def ev_S0(job, o):
                if job[1]:
                    wait_full(dve, ("GT", 1, 0))
                return V.tensor_tensor(sm[:, 0:512], o[0:NH, :], negm[:, 0:512], ALU.add)

            def ev_S1(job, o):
                return V.tensor_tensor(sm[:, 512:1024], o[0:NH, :], negm[:, 512:1024], ALU.add)

            def softmax(b):
                wait_read(dve, ("S1", b, 0))
                own.mark(V.reduce_max(st[:, 0:1], sm[:, 512:1024], AX.X))
                own.after()
                own.mark(V.tensor_tensor(st[:, 0:1], st[:, 0:1], st[:, 4:5], ALU.max))
                own.after()
                V.tensor_scalar(st[:, 1:2], st[:, 0:1], -1.0, None, ALU.mult).then_inc(mx_ready, 1)
                dve.wait_ge(p_ready, b + 1)
                V.reciprocal(st[:, 3:4], st[:, 2:3]).then_inc(recip_ready, 1)

            def ev_VV(job, o):
                own.mark(V.tensor_tensor(ovj[:, :, :], o[:, 0:KD * NH].rearrange("p (m h) -> p m h", m=KD), bm, ALU.mult))
                own.after()
                return V.reduce_sum(ov[:, :], ovj[:, :, :], AX.X)

            def scaled(row, name, half, o):
                cols = slice(half * 512, (half + 1) * 512)
                return V.tensor_tensor(row[:, cols], o[0:B, :], scale_rows[name][:, cols], ALU.mult)

            def ev_W1(job, o):
                dve.wait_ge(s_scales, 64)
                return scaled(row1, "w1", job[1], o)

            def ev_W2(job, o):
                return scaled(row2, "w2", job[1], o)

            def ev_H(job, o):
                return scaled(row1, f"h{job[1]}", job[2], o)

            def ev_WT(job, o):
                dve.wait_ge(silu_ready, 1)
                w2T = o[:, KH * B:2 * KH * B].rearrange("p (m b) -> p m b", b=B)
                return V.tensor_tensor(ff[:, 0, :, :], ff[:, 2, :, :], w2T, ALU.mult)

            def ev_W3(job, o):
                return V.tensor_tensor(row3, o[0:B, 0:DM], w3_row[:, :], ALU.mult)

            def ev_FB(job, o):
                b = job[1]
                for j in range(2):
                    g = b * GB + j * NT
                    V.tensor_tensor(outs[:, b, j * NT:(j + 1) * NT, :], xt[:, g:g + NT, :], o[:, None, 0:DM].to_broadcast([P, NT, DM]), ALU.add).then_inc(out_ready, 1)
                return None

            def compare_rows():
                dve.wait_ge(mask_in, 32)
                m3 = mask_w.rearrange("p (g w) -> p g w", g=GB)
                own.mark(V.tensor_tensor(m3, m3, mask_0[:, None, :].to_broadcast([P, GB, S // 4]), ALU.bitwise_xor))
                own.after()
                V.reduce_max(flag[:, 0:1], mask_w, AX.X).then_inc(flag_row, 1)

            def ev_FL(job, o):
                own.mark(V.reduce_max(flag[0:1, 1:2], o[0:1, 0:P], AX.X))
                own.after()
                own.mark(V.tensor_scalar(flag[0:1, 1:2], flag[0:1, 1:2], 1.0, None, ALU.min))
                own.after()
                return V.tensor_copy(flag_i[:, :], flag[0:1, 1:2])

            evs = dict(F=ev_F, TP=ev_TP, V=ev_V, D=ev_D, G=ev_G, Z=ev_Z, Y=ev_Y, O=ev_O, M=ev_M, S0=ev_S0, S1=ev_S1, VV=ev_VV, W1=ev_W1, W2=ev_W2, H=ev_H, WT=ev_WT, W3=ev_W3, FB=ev_FB, FL=ev_FL)

            def read(job):
                if job[0] in evs:
                    wait_full(dve, job)
                    last = evs[job[0]](job, bank(job))
                    if last is not None:
                        last.then_inc(freed(job), 1)
                if job[0] == "S0":
                    wait_read(dve, job)
                    own.mark(V.reduce_max(st[:, 4:5], sm[:, 0:512], AX.X))
                if job[0] == "S1":
                    softmax(job[1])
                if job == ("VV", 1, 0):
                    compare_rows()

            for i, g in enumerate(range(0, GB, 2)):
                if g % NT == 0:
                    dve.wait_ge(s_x[g // NT], 16)
                V.tensor_tensor_reduce(out=hb[:, 1, i, 0:DM], in0=xt[:, g, :], in1=xt[:, g, :], scale=1.0, scalar=0.0, op0=ALU.mult, op1=ALU.add,
                                       accum_out=ss[:, g:g + 1]).then_inc(ss_dve, 1)
            read(("F", 0, 0))
            dve.wait_ge(fe_ready, 1)
            own.mark(V.tensor_scalar(fr[:, 2, :], fr[:, 1, :], 1.0, None, ALU.add))
            own.after()
            own.mark(V.reciprocal(fr[:, 1, :], fr[:, 2, :]))
            own.after()
            own.mark(V.tensor_scalar(fr[:, 2, :], fr[:, 1, :], float(S), 1.0, ALU.mult, ALU.max))

            def count(g, rows_, scratch):
                return V.tensor_scalar(scratch, rows_, ss[:, g:g + 1], None, ALU.is_gt, ALU.add, accum_out=cnt[:, g:g + 1])

            def kept(gs, b):
                own.mark(V.tensor_scalar(keep[:, gs], cnt[:, gs], 1.0, fr[:, 2, b:b + 1], ALU.add, ALU.is_le))
                own.after()
                V.tensor_scalar(keep1[:, gs], keep[:, gs], 1.0, None, ALU.add).then_inc(ranked, 1)
                own.mark(V.tensor_tensor(scl[:, gs], keep[:, gs], lnv[:, gs], ALU.mult))
                own.after()

            dve.wait_ge(mag_pe, 1)
            dve.wait_ge(ss_act, 4)
            rows0 = yacc[:, :, :].rearrange("p a b -> p (a b)")
            for g in range(NT):
                if g:
                    own.after()
                own.mark(count(g, rows0, junk))
            dve.wait_ge(rstd_ready, 1)
            own.after()
            kept(slice(0, NT), 0)
            rows(0)
            for g in range(NT, GB):
                own.after()
                own.mark(count(g, rows0, junk))
            own.after()
            kept(slice(NT, GB), 0)
            dve.wait_ge(aexp_ready, 1)
            V.tensor_scalar(Aneg[:, :], Aneg[:, :], -1.0, None, ALU.mult).then_inc(A_ready, 1)
            dve.wait_ge(half_ready, 2)
            for m in range(own_conv(0)):
                conv_taps(0, m, range(KC))
            for m in range(own_conv(0)):
                conv_finish(0, m)
            for job in HEAD:
                if job[0] in ("V", "D"):
                    read(job)

            def batch1_rows(s):
                if s == 0:
                    dve.wait_ge(s_mrow, 16)
                    V.tensor_scalar(negm[:, :], mrow, -1.0, FLT_MAX, ALU.add, ALU.mult)
                    dve.wait_ge(ss_act, 12)
                    dve.wait_ge(mag_act, 2)
                if s < GB:
                    own.after()
                    own.mark(count(GB + s, magrow, junk))
                if s == GB:
                    dve.wait_ge(rstd_ready, 2)
                    own.after()
                    kept(slice(GB, 2 * GB), 1)

            def scan_step(n, m):
                c, s = n // NS, n % NS
                i = n * CT + m
                dve.wait_ge(da_ready, i + 1)
                if m % 2 == 0:
                    dve.wait_ge(bx_ready, 2 * n + m // 2 + 1)
                if c % HALVES:
                    if m == 0:
                        dve.wait_ge(carry_done, c // HALVES * NS + s + 1)
                    start = carry[:, s, m:m + 1]
                else:
                    start = 0.0
                V.tensor_tensor_scan(hb[:, n % RING, m, :], dA[:, m % 2, :], hb[:, n % RING, m, :], start, ALU.mult, ALU.add).then_inc(scan_done, 1)

            def mac_step(n, i):
                c, s = n // NS, n % NS
                e = 2 * n + i // 2
                dve.wait_ge(hT_ready, NT * n + i + 1)
                dst = yTd[:, c % 2, i // 2, :]
                src, cs = hT[:, 1, :], CTs[:, c % 2, i, s:s + 1]
                if s == 0:
                    if c >= 2 and i == 1:
                        wait_full(dve, ("Y", c - 2, 3))
                    V.tensor_scalar(dst, src, cs, None, ALU.mult).then_inc(mac_done, 1)
                else:
                    dve.wait_ge(mac_done, e - 1)
                    V.scalar_tensor_tensor(dst, src, cs, dst, ALU.mult, ALU.add).then_inc(mac_done, 1)

            def beside_conv(c, h):
                if c + 1 < NCH and h == POOL_CONV_AT["finish"]:
                    dve.wait_ge(pool_tanh_ready, c + 1)
                    acc = xi(c + 1)[:, POOL_TILE, :]
                    V.scalar_tensor_tensor(acc, delta(c + 1)[:, POOL_TILE, :], 1.0, acc, ALU.add, ALU.mult).then_inc(xi_ready, 1)
                for m in range(LOOP_CONV):
                    if c + 1 < NCH and h == CONV_AT["taps0"]:
                        conv_taps(c + 1, m, range(0, 2))
                    if c + 1 < NCH and h == CONV_AT["taps1"]:
                        conv_taps(c + 1, m, range(2, KC))
                    if c + 1 < NCH and h == CONV_AT["finish"]:
                        conv_finish(c + 1, m)

            for c in range(NCH):
                for s in range(NS):
                    n = c * NS + s
                    scan_step(n, 0)
                    scan_step(n, 1)
                    if n:
                        mac_step(n - 1, 1)
                    for job in to_read(2 * n):
                        read(job)
                    beside_conv(c, 2 * s)
                    scan_step(n, 2)
                    scan_step(n, 3)
                    if n:
                        mac_step(n - 1, 3)
                    if s == 0:
                        if c:
                            gate_even(c - 1)
                        if c + 1 < NCH:
                            rows(c + 1)
                    for job in to_read(2 * n + 1):
                        read(job)
                    beside_conv(c, 2 * s + 1)
                    if c == 0:
                        batch1_rows(s)
            n = NCH * NS
            mac_step(n - 1, 1)
            mac_step(n - 1, 3)
            gate_even(NCH - 1)
            for job in BESIDE[-1] + TAIL:
                read(job)

            def general_batch(b):
                def did(ins):
                    ins.then_inc(chain, 1)

                step(dve, b, "m_out")
                did(ev_M(None, pp[:, 0, :]))
                with dve.Fori(0, GB) as t:
                    step(dve, b, "mask", t)
                    dve.wait_ge(gmask_in, (t + (b * GB + 1)) * 16)
                    did(V.tensor_scalar(gadd, gmask, -1.0, FLT_MAX, ALU.add, ALU.mult))
                    for h in range(NH):
                        step(dve, b, f"add{h}", t)
                        did(V.tensor_tensor(gsc, hT[:, :, :].rearrange("p a s -> p (a s)"), gadd, ALU.add))
                        step(dve, b, f"max{h}", t)
                        did(V.reduce_max(gst[:, 0:1], gsc, AX.X))
                        step(dve, b, f"neg{h}", t)
                        did(V.tensor_scalar(gst[:, 1:2], gst[:, 0:1], -1.0, None, ALU.mult))
                        step(dve, b, f"recip{h}", t)
                        did(V.reciprocal(gst[:, 3:4], gst[:, 2:3]))
                        step(dve, b, f"norm{h}", t)
                        did(V.tensor_scalar(gsc, gsc, gst[:, 3:4], None, ALU.mult))
                    step(dve, b, "o_out", t)
                    did(V.tensor_copy(go, dA[:, 0, 0:DM]))

                    def by_row(dst, src, name, n):
                        return V.tensor_tensor(dst, src, v(name)[:, :, None].to_broadcast([P, n, P]), ALU.mult)

                    hT3 = hT[:, :, :].rearrange("p a (m t) -> p (a m) t", m=4)
                    yacc3 = yacc[:, :, :].rearrange("p a (m t) -> p (a m) t", m=4)
                    step(dve, b, "w1_out", t)
                    did(by_row(gf1, hT3, "w1_s", KH))
                    step(dve, b, "w2_out", t)
                    did(by_row(gf2, yacc3, "w2_s", KH))
                    step(dve, b, "gated", t)
                    did(V.tensor_tensor(gf1, gf1, gf2, ALU.mult))
                    step(dve, b, "h1_out", t)
                    did(by_row(gf2, hT3, "h1_s", KH))
                    step(dve, b, "h2_out", t)
                    did(by_row(gf1, hT3, "h2_s", KH))
                    step(dve, b, "w3_out", t)
                    did(by_row(gf3, pp[:, 0, 0:DM].rearrange("p (k t) -> p k t", k=KD), "w3_s", KD))
                    step(dve, b, "sum", t)
                    x1 = xt[:, bass.ds(t + b * GB, 1), :].rearrange("p a d -> p (a d)")
                    did(V.tensor_tensor(gout, x1, pp[:, 1, 0:DM], ALU.add))

            wait_read(dve, ("FL", 0, 0))
            V.tensor_copy(flag[0:1, 0:1], flag_i[:, :]).then_inc(flag_ready, 1)
            with dve.If(dve.value_load(flag_i[0:1, 0:1], min_val=0, max_val=1)):
                for b in range(B):
                    general_batch(b)


def layout(i):
    def parts(name, a):
        a = np.asarray(a)
        n = a.shape[0] // P
        return a.reshape((n, P) + a.shape[1:]).swapaxes(0, 1).reshape(P, -1)

    cols = {
        "rms_w": i["L0_attn_rms_w"], "conv_w": i["L0_attn_conv_w"], "conv_b": i["L0_attn_conv_b"], "dt_b": i["L0_attn_dt_b"],
        "A_log": i["L0_attn_A_log"], "D": i["L0_attn_D"], "score_w": i["L0_cond_score_w"],
        "cond": np.asarray(i["cond_1024"]).T, "w1_s": i["L0_ffn_w1_s"], "w2_s": i["L0_ffn_w2_s"],
        "h1_s": i["L0_ffn_h1_s"], "h2_s": i["L0_ffn_h2_s"], "w3_s": i["L0_ffn_w3_s"],
    }
    packed = [np.broadcast_to(np.asarray(i["L0_cond_score_b"]).reshape(1, 1), (P, 1)) if n == "score_b" else parts(n, cols[n]) for n in VEC]
    eye = np.eye(P, dtype=np.float32)
    heads = (np.arange(DM)[:, None] // HE == np.arange(NH)[None, :]).astype(np.float32)
    return [
        np.asarray(i["x"]).reshape(B * S, DM), np.asarray(i["L0_attn_in_proj"]), np.asarray(i["L0_attn_out_proj"]),
        np.asarray(i["L0_attn_x_proj"]), np.asarray(i["L0_attn_dt_w"]), np.asarray(i["L0_cond2_Wq"]),
        np.asarray(i["L0_cond2_Wq"]).T, np.asarray(i["L0_cond2_Wk"]), np.asarray(i["L0_cond2_Wv"]).T,
        np.asarray(i["L0_cond2_Wt"]).T, np.asarray(i["L0_cond2_Wo"]).T, np.asarray(i["L0_ffn_w1_w"]).T,
        np.asarray(i["L0_ffn_w2_w"]).T, np.asarray(i["L0_ffn_h1_w"]).T, np.asarray(i["L0_ffn_h2_w"]).T,
        np.asarray(i["L0_ffn_w3_w"]).T, np.asarray(i["mask_SxS_bk0"]), *(np.asarray(i[f"L0_ffn_{n}_s"]).reshape(1, -1) for n in ("w1", "w2", "h1", "h2", "w3")), np.concatenate(packed, axis=1),
        np.concatenate([eye, parts("heads", heads)], axis=1),
    ]


def kernel(**inputs):
    import concourse.bacc as bacc
    from concourse.bass_utils import run_bass_kernel_spmd

    nc = bacc.Bacc("TRN2", target_bir_lowering=False, num_devices=1)
    arrays, args = {}, []
    for n, a in enumerate(layout(inputs)):
        a = np.ascontiguousarray(a)
        arrays[f"in_{n}"] = a
        args.append(nc.dram_tensor(f"in_{n}", a.shape, mybir.dt.from_np(a.dtype), kind="ExternalInput").ap())
    out = nc.dram_tensor("out_0", [B * S, DM], F32, kind="ExternalOutput").ap()
    build(nc, *args, out)
    r = run_bass_kernel_spmd(nc, [arrays], core_ids=[0])
    return r.results[0]["out_0"].reshape(B, S, DM)
```
